# Optimizing a Trainium2 kernel written in Bass

```python
import numpy as np
import jax
import jax.numpy as jnp

def _softmax(x, axis=-1):
    return jax.nn.softmax(x, axis=axis)

def _gelu(x):
    return jax.nn.gelu(x, approximate=True)

def _silu(x):
    return jax.nn.silu(x)

def _sigmoid(x):
    return jax.nn.sigmoid(x)

def _layernorm(x, axis=-1, eps=1e-05):
    m = jnp.mean(x, axis=axis, keepdims=True)
    v = jnp.var(x, axis=axis, keepdims=True)
    return (x - m) / jnp.sqrt(v + eps)

def _scatter_add(tgt, idx, src, axis=0):
    return tgt.at[idx].add(src)

def _segment_sum(src, seg, n):
    return jax.ops.segment_sum(src, seg, n)
kernel_name = 'mk_gnn_ffn_d2_gnn_r8_d35768'

def setup_inputs(seed: int=0):
    np.random.seed(seed)
    _w = jnp.asarray

    def _rec_inputs():
        import jax
        import jax.numpy as jnp
        _gk = jax.random.key(seed)
        x = -0.0002117 + 1 * jax.random.normal(jax.random.fold_in(_gk, 1), (6250, 256), jnp.float32)
        src = jax.random.randint(jax.random.fold_in(_gk, 2), (100000,), 0, 6250, jnp.int32)
        dst = jnp.minimum((6250 * jax.random.uniform(jax.random.fold_in(_gk, 3), (100000,)) ** 2.0).astype(jnp.int32), 49999)
        _o = jnp.argsort(dst, stable=True)
        src = src[_o]
        dst = dst[_o]
        edge_attr_2 = jax.random.uniform(jax.random.fold_in(_gk, 11), (100000, 2), jnp.float32, 0.0, 1)
        return (x, src, dst, edge_attr_2)
    x, src, dst, edge_attr_2 = _rec_inputs()

    def _L0_gnn_setup():
        import jax, jax.numpy as jnp
        import numpy as np
        N_NODES = 12500
        N_EDGES = 200000
        D_IN = 256
        HEADS = 8
        D_HEAD = 32
        NEG_SLOPE = 0.2
        BN_EPS = 1e-05
        key = jax.random.key(seed)
        ks = jax.random.split(key, 8)
        x = jax.random.normal(ks[0], (N_NODES, D_IN), dtype=jnp.float32)
        edge_index = jax.random.randint(ks[1], (2, N_EDGES), 0, N_NODES, dtype=jnp.int32)
        W = jax.random.normal(ks[2], (D_IN, HEADS * D_HEAD), dtype=jnp.float32) / np.sqrt(D_IN)
        att_src = jax.random.normal(ks[3], (HEADS, D_HEAD), dtype=jnp.float32) / np.sqrt(D_HEAD)
        att_dst = jax.random.normal(ks[4], (HEADS, D_HEAD), dtype=jnp.float32) / np.sqrt(D_HEAD)
        bias = jax.random.normal(ks[5], (HEADS * D_HEAD,), dtype=jnp.float32) * 0.01
        gamma = jnp.ones((HEADS * D_HEAD,), dtype=jnp.float32)
        beta = jnp.zeros((HEADS * D_HEAD,), dtype=jnp.float32)
        return {'x': x, 'edge_index': edge_index, 'W': W, 'att_src': att_src, 'att_dst': att_dst, 'bias': bias, 'gamma': gamma, 'beta': beta}
    _L0_gnn_all = _L0_gnn_setup()
    _L0_gnn_in = {k: v for k, v in _L0_gnn_all.items() if k in ('W', 'att_src', 'att_dst', 'bias', 'gamma', 'beta')}
    del _L0_gnn_all

    def _L0_ffn_setup():
        import jax, jax.numpy as jnp
        import numpy as np
        D_MODEL = 256
        EXPERT_DIM = 512
        NUM_EXPERTS = 8
        TOP_K = 2
        SEQ_LEN = 256
        BATCH = 2
        key = jax.random.key(seed)
        ks = jax.random.split(key, 8)
        s = 0.02
        x = jax.random.normal(ks[0], (SEQ_LEN, BATCH, D_MODEL), dtype=jnp.float32)
        Wg = jax.random.normal(ks[1], (D_MODEL, NUM_EXPERTS), dtype=jnp.float32) * s
        bg = jax.random.normal(ks[2], (NUM_EXPERTS,), dtype=jnp.float32) * s
        bias = jnp.zeros((NUM_EXPERTS,), dtype=jnp.float32)
        W1 = jax.random.normal(ks[3], (NUM_EXPERTS, D_MODEL, EXPERT_DIM), dtype=jnp.float32) * s
        b1 = jax.random.normal(ks[4], (NUM_EXPERTS, EXPERT_DIM), dtype=jnp.float32) * s
        W2 = jax.random.normal(ks[5], (NUM_EXPERTS, EXPERT_DIM, D_MODEL), dtype=jnp.float32) * s
        b2 = jax.random.normal(ks[6], (NUM_EXPERTS, D_MODEL), dtype=jnp.float32) * s
        return {'x': x, 'Wg': Wg, 'bg': bg, 'bias': bias, 'W1': W1, 'b1': b1, 'W2': W2, 'b2': b2}
    _L0_ffn_all = _L0_ffn_setup()
    _L0_ffn_in = {k: v for k, v in _L0_ffn_all.items() if k in ('Wg', 'bg', 'bias', 'W1', 'b1', 'W2', 'b2')}
    del _L0_ffn_all

    def _L1_gnn_setup():
        import jax, jax.numpy as jnp
        import numpy as np
        N_NODES = 12500
        N_EDGES = 200000
        IN_FEATS = 256
        OUT_FEATS = 64
        NUM_HEADS = 4
        key = jax.random.key(seed)
        k_h, k_adj, k_dir, k_wf, k_wr, k_af = jax.random.split(key, 6)
        h = jax.random.normal(k_h, (N_NODES, IN_FEATS), dtype=jnp.float32)
        adj = jax.random.randint(k_adj, (2, N_EDGES), 0, N_NODES, dtype=jnp.int64)
        bit = jax.random.randint(k_dir, (N_EDGES,), 0, 2).astype(jnp.float32)
        direction = jnp.stack([bit, 1.0 - bit], axis=1)
        s_w = float(np.sqrt(6.0 / (IN_FEATS + OUT_FEATS)))
        s_a = float(np.sqrt(6.0 / (NUM_HEADS + OUT_FEATS)))
        W_forward = jax.random.uniform(k_wf, (OUT_FEATS, IN_FEATS), jnp.float32, -s_w, s_w)
        W_reverse = jax.random.uniform(k_wr, (OUT_FEATS, IN_FEATS), jnp.float32, -s_w, s_w)
        attn_forward = jax.random.uniform(k_af, (1, NUM_HEADS, OUT_FEATS), jnp.float32, -s_a, s_a)
        return {'h': h, 'adj': adj, 'direction': direction, 'W_forward': W_forward, 'W_reverse': W_reverse, 'attn_forward': attn_forward}
    _L1_gnn_all = _L1_gnn_setup()
    _L1_gnn_in = {k: v for k, v in _L1_gnn_all.items() if k in ('W_forward', 'W_reverse', 'attn_forward')}
    del _L1_gnn_all

    def _L1_ffn_setup():
        import math
        import jax, jax.numpy as jnp
        import numpy as np
        CAPACITY_FACTOR = 1.25
        TOP_K = 2
        LN_EPS = 1e-05

        def _layer_norm(x, gamma, beta):
            mu = jnp.mean(x, axis=-1, keepdims=True)
            var = jnp.var(x, axis=-1, keepdims=True)
            return (x - mu) * jax.lax.rsqrt(var + LN_EPS) * gamma + beta
        key = jax.random.key(seed)
        ks = jax.random.split(key, 4)
        B, S, D, F, E = (8, 512, 256, 512, 8)
        x = jax.random.normal(ks[0], (B, S, D), dtype=jnp.float32)
        Wr = jax.random.normal(ks[1], (D, E), dtype=jnp.float32) / np.sqrt(D)
        br = jnp.zeros((E,), jnp.float32)
        W1 = jax.random.normal(ks[2], (E, D, F), dtype=jnp.float32) / np.sqrt(D)
        b1 = jnp.zeros((E, F), jnp.float32)
        W2 = jax.random.normal(ks[3], (E, F, D), dtype=jnp.float32) / np.sqrt(F)
        b2 = jnp.zeros((E, D), jnp.float32)
        gamma = jnp.ones((D,), jnp.float32)
        beta = jnp.zeros((D,), jnp.float32)
        return {'x': x, 'Wr': Wr, 'br': br, 'W1': W1, 'b1': b1, 'W2': W2, 'b2': b2, 'gamma': gamma, 'beta': beta}
    _L1_ffn_all = _L1_ffn_setup()
    _L1_ffn_in = {k: v for k, v in _L1_ffn_all.items() if k in ('Wr', 'br', 'W1', 'b1', 'W2', 'b2', 'gamma', 'beta')}
    del _L1_ffn_all
    return {'x': x, 'src': src, 'dst': dst, 'edge_attr_2': edge_attr_2, 'L0_gnn_W': _L0_gnn_in['W'], 'L0_gnn_att_src': _L0_gnn_in['att_src'], 'L0_gnn_att_dst': _L0_gnn_in['att_dst'], 'L0_gnn_bias': _L0_gnn_in['bias'], 'L0_gnn_gamma': _L0_gnn_in['gamma'], 'L0_gnn_beta': _L0_gnn_in['beta'], 'L0_ffn_Wg': _L0_ffn_in['Wg'], 'L0_ffn_bg': _L0_ffn_in['bg'], 'L0_ffn_bias': _L0_ffn_in['bias'], 'L0_ffn_W1': _L0_ffn_in['W1'], 'L0_ffn_b1': _L0_ffn_in['b1'], 'L0_ffn_W2': _L0_ffn_in['W2'], 'L0_ffn_b2': _L0_ffn_in['b2'], 'L1_gnn_W_forward': _L1_gnn_in['W_forward'], 'L1_gnn_W_reverse': _L1_gnn_in['W_reverse'], 'L1_gnn_attn_forward': _L1_gnn_in['attn_forward'], 'L1_ffn_Wr': _L1_ffn_in['Wr'], 'L1_ffn_br': _L1_ffn_in['br'], 'L1_ffn_W1': _L1_ffn_in['W1'], 'L1_ffn_b1': _L1_ffn_in['b1'], 'L1_ffn_W2': _L1_ffn_in['W2'], 'L1_ffn_b2': _L1_ffn_in['b2'], 'L1_ffn_gamma': _L1_ffn_in['gamma'], 'L1_ffn_beta': _L1_ffn_in['beta']}

def reference(x, src, dst, edge_attr_2, L0_gnn_W, L0_gnn_att_src, L0_gnn_att_dst, L0_gnn_bias, L0_gnn_gamma, L0_gnn_beta, L0_ffn_Wg, L0_ffn_bg, L0_ffn_bias, L0_ffn_W1, L0_ffn_b1, L0_ffn_W2, L0_ffn_b2, L1_gnn_W_forward, L1_gnn_W_reverse, L1_gnn_attn_forward, L1_ffn_Wr, L1_ffn_br, L1_ffn_W1, L1_ffn_b1, L1_ffn_W2, L1_ffn_b2, L1_ffn_gamma, L1_ffn_beta):
    import jax
    import jax.numpy as jnp

    def _L0_gnn_ref(x, edge_index, W, att_src, att_dst, bias, gamma, beta):
        import jax, jax.numpy as jnp
        import numpy as np
        N_NODES = 12500
        N_EDGES = 200000
        D_IN = 256
        HEADS = 8
        D_HEAD = 32
        NEG_SLOPE = 0.2
        BN_EPS = 1e-05
        N = x.shape[0]
        H, D = att_src.shape
        xh = (x @ W).reshape(N, H, D)
        a_src = jnp.einsum('nhd,hd->nh', xh, att_src)
        a_dst = jnp.einsum('nhd,hd->nh', xh, att_dst)
        loops = jnp.arange(N, dtype=edge_index.dtype)
        src = jnp.concatenate([edge_index[0], loops])
        dst = jnp.concatenate([edge_index[1], loops])
        e = jax.nn.leaky_relu(a_src[src] + a_dst[dst], NEG_SLOPE)
        m = jax.ops.segment_max(e, dst, num_segments=N)
        e = jnp.exp(e - m[dst])
        denom = jax.ops.segment_sum(e, dst, num_segments=N)
        alpha = e / denom[dst]
        msg = xh[src] * alpha[:, :, None]
        out = jax.ops.segment_sum(msg, dst, num_segments=N).reshape(N, H * D) + bias
        mean = jnp.mean(out, axis=0)
        var = jnp.var(out, axis=0)
        out = (out - mean) * jax.lax.rsqrt(var + BN_EPS) * gamma + beta
        return out + x

    def _L0_ffn_ref(x, Wg, bg, bias, W1, b1, W2, b2):
        import jax, jax.numpy as jnp
        import numpy as np
        D_MODEL = 256
        EXPERT_DIM = 512
        NUM_EXPERTS = 8
        TOP_K = 2
        SEQ_LEN = 256
        BATCH = 2
        x_flat = x.reshape(-1, D_MODEL)
        gate_logits = x_flat @ Wg + bg + bias
        topk_vals, topk_idx = jax.lax.top_k(gate_logits, TOP_K)
        topk_w = jax.nn.softmax(topk_vals, axis=-1)
        combine = (jax.nn.one_hot(topk_idx, NUM_EXPERTS, dtype=x.dtype) * topk_w[..., None]).sum(axis=1)
        h = jax.nn.relu(jnp.einsum('td,edh->teh', x_flat, W1) + b1)
        y = jnp.einsum('teh,ehd->ted', h, W2) + b2
        out = jnp.einsum('ted,te->td', y, combine)
        return out.reshape(x.shape)

    def _L1_gnn_ref(h, adj, direction, W_forward, W_reverse, attn_forward):
        import jax, jax.numpy as jnp
        import numpy as np
        N_NODES = 12500
        N_EDGES = 200000
        IN_FEATS = 256
        OUT_FEATS = 64
        NUM_HEADS = 4
        N = h.shape[0]
        H = attn_forward.shape[1]
        h_fwd = h @ W_forward.T
        h_rev = h @ W_reverse.T
        src, dst = (adj[0], adj[1])
        messages = h_fwd[src] * direction[:, 0:1] + h_rev[src] * direction[:, 1:2]
        scores = jnp.einsum('ef,hf->eh', messages, attn_forward[0])
        scores = jax.nn.leaky_relu(scores, negative_slope=0.2)
        exp_scores = jnp.exp(scores - scores.max(axis=0, keepdims=True))
        sum_exp = jax.ops.segment_sum(exp_scores, dst, num_segments=N)
        norm = exp_scores / (sum_exp[dst] + 1e-10)
        outs = [jax.ops.segment_sum(messages * norm[:, hd:hd + 1], dst, num_segments=N) for hd in range(H)]
        out = jnp.stack(outs, axis=1)
        return out.reshape(N, -1)

    def _L1_ffn_ref(x, Wr, br, W1, b1, W2, b2, gamma, beta):
        import math
        import jax, jax.numpy as jnp
        import numpy as np
        CAPACITY_FACTOR = 1.25
        TOP_K = 2
        LN_EPS = 1e-05

        def _layer_norm(x, gamma, beta):
            mu = jnp.mean(x, axis=-1, keepdims=True)
            var = jnp.var(x, axis=-1, keepdims=True)
            return (x - mu) * jax.lax.rsqrt(var + LN_EPS) * gamma + beta
        B, S, D = x.shape
        E = Wr.shape[1]
        N = B * S
        K = TOP_K
        logits = jnp.mean(x, axis=1) @ Wr + br
        routing_weights = jax.nn.softmax(logits, axis=-1)
        capacity = float(math.ceil(N * CAPACITY_FACTOR / E))
        expected_loads = routing_weights.sum(axis=0) * (N / B)
        scale = jnp.where(expected_loads > capacity, capacity / expected_loads, 1.0)
        routing_weights = jax.nn.softmax(routing_weights * scale, axis=-1)
        rw_tok = jnp.broadcast_to(routing_weights[:, None, :], (B, S, E)).reshape(N, E)
        top_w, top_i = jax.lax.top_k(rw_tok, K)
        top_w = jax.nn.softmax(top_w, axis=-1)
        xf = x.reshape(N, D)
        h = jax.nn.gelu(jnp.einsum('nd,edf->enf', xf, W1) + b1[:, None, :], approximate=False)
        y = jnp.einsum('enf,efd->end', h, W2) + b2[:, None, :]
        w_dense = jnp.zeros((N, E), x.dtype).at[jnp.arange(N)[:, None], top_i].add(top_w)
        out = jnp.einsum('ne,end->nd', w_dense, y).reshape(B, S, D)
        out = _layer_norm(out + x, gamma, beta)
        return out
    edge_index = jnp.stack([src, dst])
    x = x + _L0_gnn_ref(_layernorm(x, axis=-1), edge_index, L0_gnn_W, L0_gnn_att_src, L0_gnn_att_dst, L0_gnn_bias, L0_gnn_gamma, L0_gnn_beta)
    x = x + _L0_ffn_ref(_layernorm(x, axis=-1)[None], L0_ffn_Wg, L0_ffn_bg, L0_ffn_bias, L0_ffn_W1, L0_ffn_b1, L0_ffn_W2, L0_ffn_b2)[0]
    x = x + _L1_gnn_ref(_layernorm(x, axis=-1), edge_index, edge_attr_2, L1_gnn_W_forward, L1_gnn_W_reverse, L1_gnn_attn_forward)
    x = x + _L1_ffn_ref(_layernorm(x, axis=-1)[None], L1_ffn_Wr, L1_ffn_br, L1_ffn_W1, L1_ffn_b1, L1_ffn_W2, L1_ffn_b2, L1_ffn_gamma, L1_ffn_beta)[0]
    return x

_drawn_inputs = setup_inputs


def setup_inputs(seed=0):
    import zlib

    import numpy as np

    out = dict(_drawn_inputs(seed))
    spreads = {'L0_gnn_gamma': (1.0, 0.2),
     'L0_gnn_beta': (0.0, 0.1),
     'L0_ffn_bias': (0.0, 0.366),
     'L1_ffn_br': (0.0, 0.1),
     'L1_ffn_b1': (0.0, 0.561),
     'L1_ffn_b2': (0.0, 0.412),
     'L1_ffn_gamma': (1.0, 0.2),
     'L1_ffn_beta': (0.0, 0.275)}
    factors = {'L0_gnn_bias': 64.0, 'L0_ffn_bg': 25.917, 'L0_ffn_b1': 29.644, 'L0_ffn_b2': 8.0}
    for name, (base, spread) in spreads.items():
        noise = np.random.default_rng([zlib.crc32(name.encode()), seed]).standard_normal(out[name].shape)
        drawn = base * np.exp(spread * noise) if base else spread * noise
        out[name] = jnp.asarray(drawn.astype(out[name].dtype))
    for name, factor in factors.items():
        out[name] = (out[name] * factor).astype(out[name].dtype)
    return out
```

```python
from contextlib import ExitStack, contextmanager

import concourse.bass as bass
from concourse import mybir

F32 = mybir.dt.float32
I32 = mybir.dt.int32
BF16 = mybir.dt.bfloat16
ALU = mybir.AluOpType
ACT = mybir.ActivationFunctionType
AX = mybir.AxisListType
ENG = mybir.EngineType

P = 128
N_NODES = 6250
N_EDGES = 100000
D = 256
TILES = 50
N_PAD = TILES * P
GROUP = 512
GT = GROUP // P
ROW_EDGES = 1024
EDGE_ROWS = -(-N_EDGES // ROW_EDGES)
E_PAD = EDGE_ROWS * ROW_EDGES
GROUPS = E_PAD // GROUP
CHUNKS = ROW_EDGES // P
EDGE_TILES = E_PAD // P
BLOCKS = -(-N_NODES // P)
PAD_DST = BLOCKS * P - 1
DUMMY = BLOCKS
UNROLL = 6
STEPS = GROUPS + BLOCKS - 1
STEPS += -STEPS % UNROLL
HALVES = -(-STEPS // P)
H0, DH0 = 8, 32
W0 = H0 * (DH0 + 1)
H1, F1 = 4, 64
W1C = 2 * (F1 + H1)
A1 = H1 * (F1 + 1)
EXPERTS, DFF = 8, 512
BIG = 1e30
SAFE = 40.0
LN_EPS = 1e-5
FLOW = 5
BANKS = 4
SLOT_TILES = (2 * N_PAD + EXPERTS * (P - 1)) // P
SLOT_TILES += -SLOT_TILES % UNROLL
OWNERS = SLOT_TILES + UNROLL


class Steps:

    def __init__(self, eng, sem):
        self.eng, self.sem, self.base, self.count = eng, sem, 0, 0

    def done(self, ins):
        ins.then_inc(self.sem, 1)
        self.count += 1
        return self.base + self.count

    def until(self, value):
        self.eng.wait_ge(self.sem, value)

    def settle(self):
        self.eng.wait_ge(self.sem, self.base + self.count)

    def chained(self, ins):
        self.done(ins)
        self.settle()

    def loop(self, i, per):
        self.start, self.per = self.base + self.count, per
        self.base, self.count = self.start + i * per, 0

    def left(self, turns):
        assert self.count == self.per, (self.count, self.per)
        self.base, self.count = self.start + turns * self.per, 0


@contextmanager
def semaphores(nc):
    held = []

    def take(name):
        held.append(nc.alloc_semaphore(name=name))
        return held[-1]

    yield take
    nc.clear_and_free_semaphores(held)
    nc.all_engine_barrier()


def edge_lists(nc, K, dst_rows, src_rows, attr_rows):
    with ExitStack() as ctx:
        sb = lambda name, shape, dt=F32: ctx.enter_context(nc.sbuf_tensor(name, shape, dt))
        sem = ctx.enter_context(semaphores(nc))
        dst_i = sb("dst_i", [EDGE_ROWS, ROW_EDGES], I32)
        src_i = sb("src_i", [EDGE_ROWS, ROW_EDGES], I32)
        rows = sb("edge_row_data", [EDGE_ROWS, 3, ROW_EDGES])
        attr = sb("attr_rows", [EDGE_ROWS, ROW_EDGES, 2])
        fresh = sb("fresh_rows", [EDGE_ROWS, ROW_EDGES])
        ends_i = sb("group_ends_i", [1, 2, GROUPS], I32)
        ends_b = sb("group_ends_block", [1, 2, GROUPS], I32)
        ends = sb("group_ends", [1, 2, GROUPS])
        count = sb("steps_of_group", [1, GROUPS])
        lines = sb("step_lines", [1, 2, GROUPS])
        zeros = sb("zeros_row", [1, GROUPS])
        step_no = sb("step_no", [P, HALVES])
        group_no = sb("group_no", [P, GROUPS])
        below = sb("groups_below", [P, HALVES, GROUPS])
        step_g = sb("step_g", [P, HALVES])
        step_b = sb("step_b", [P, HALVES])
        late = sb("step_late", [P, HALVES])
        step_i = sb("step_i", [P, 2, HALVES], I32)
        ps = ctx.enter_context(nc.psum_tensor("edge_turned", [P, 2, CHUNKS, P], F32))
        ps_lines = ctx.enter_context(nc.psum_tensor("lines_everywhere", [P, 2, GROUPS], F32))
        dst_in, src_in, attr_in, ends_in = sem("dst_in"), sem("src_in"), sem("attr_in"), sem("ends_in")
        numbers, vec = sem("numbers"), sem("edge_vec")
        rows_ready, turned, kept = sem("rows_ready"), sem("turned"), sem("edge_kept")
        fresh_ready, fresh_out = sem("fresh_ready"), sem("fresh_out")
        lines_ready, lines_spread = sem("lines_ready"), sem("lines_spread")
        list_ready, list_out, list_in = sem("list_ready"), sem("list_out"), sem("list_in")
        iota_seeds = sem("iota_seeds")
        ARRAYS = 5
        block = ctx.enter_context(nc.Block())

        @block.sync
        def _(sp):
            sp.dma_start(dst_i[:, :], dst_rows).then_inc(dst_in, 16)
            with nc.allow_non_contiguous_dma(reason="392 numbers"):
                flat = dst_rows.rearrange("r (h c) -> (r h) c", c=GROUP)
                sp.dma_start(ends_i[:, 0, :], flat[:, 0:1].rearrange("g c -> c g")).then_inc(ends_in, 16)
                sp.dma_start(ends_i[:, 1, :], flat[:, GROUP - 1:GROUP].rearrange("g c -> c g")).then_inc(ends_in, 16)
            sp.dma_start(src_i[:, :], src_rows).then_inc(src_in, 16)
            sp.dma_start(attr[:, :, :], attr_rows).then_inc(attr_in, 16)
            sp.wait_ge(fresh_ready, 3)
            for h in range(H0):
                sp.dma_start(K.fresh_dram.rearrange("(r c) h e -> r c h e", c=CHUNKS)[:, :, h, :],
                             fresh[:, :].rearrange("r (c e) -> r c e", e=P)).then_inc(fresh_out, 16)
            sp.wait_ge(list_ready, 2)
            with nc.allow_non_contiguous_dma(reason="a list of 512 numbers"):
                sp.dma_start(K.list_dram.rearrange("k (h p) -> p k h", p=P), step_i[:, :, :]).then_inc(list_out, 16)
            sp.wait_ge(list_out, 16)
            sp.dma_start(K.step_list[0:1, :, UNROLL:UNROLL + HALVES * P],
                         K.list_dram.rearrange("(a k) s -> a k s", a=1)).then_inc(list_in, 16)
            sp.wait_ge(list_in, 16)
            sp.wait_ge(fresh_out, 16 * H0)

        @block.gpsimd
        def _(pool):
            pool.iota(K.iota_i[:, :], [[1, 2 * P]], channel_multiplier=0).then_inc(numbers, 1)
            pool.iota(K.step_seed[:, :], [[P, HALVES]], channel_multiplier=1).then_inc(numbers, 1)
            pool.memset(K.identity[:, :], 0.0).then_inc(iota_seeds, 1)
            pool.memset(K.ones[:, :], 1.0).then_inc(numbers, 1)
            pool.memset(K.step_list[:, :, :], 0).then_inc(numbers, 1)
            pool.wait_ge(iota_seeds, 1)
            pool.affine_select(out=K.identity[:, :], in_=K.identity[:, :], compare_op=ALU.not_equal, fill=1.0,
                               base=0, pattern=[[-1, P]], channel_multiplier=1).then_inc(numbers, 1)

        @block.vector
        def _(dve):
            own = Steps(dve, vec)
            dve.wait_ge(numbers, 5)
            own.done(dve.tensor_copy(K.iota[:, :], K.iota_i[:, :]))
            own.done(dve.tensor_copy(step_no[:, :], K.step_seed[:, :]))
            own.done(dve.tensor_scalar(K.minus_first[:, :], K.iota_i[:, 0:TILES], float(-P), None, ALU.mult))
            own.done(dve.tensor_copy(K.identity_b[:, :], K.identity[:, :]))
            own.done(dve.memset(K.ones_b[:, :], 1.0))
            own.done(dve.memset(zeros[:, :], 0.0))
            dve.wait_ge(ends_in, 32)
            own.chained(dve.tensor_single_scalar(ends_b[:, :, :], ends_i[:, :, :], 7, ALU.arith_shift_right))
            own.chained(dve.tensor_copy(ends[:, :, :], ends_b[:, :, :]))
            own.chained(dve.tensor_tensor(count[:, :], ends[:, 1, :], ends[:, 0, :], ALU.subtract))
            own.chained(dve.tensor_scalar(count[:, :], count[:, :], 1.0, None, ALU.add))
            own.chained(dve.tensor_tensor_scan(lines[:, 0, :], zeros[:, :], count[:, :], 0.0, ALU.add, ALU.add))
            own.chained(dve.tensor_tensor(lines[:, 1, :], count[:, :], lines[:, 0, :], ALU.subtract))
            dve.tensor_tensor(lines[:, 1, :], lines[:, 1, :], ends[:, 0, :], ALU.add).then_inc(lines_ready, 1)
            dve.wait_ge(dst_in, 16)
            dve.tensor_copy(rows[:, 0, :], dst_i[:, :]).then_inc(rows_ready, 1)
            dve.wait_ge(rows_ready, 1)
            own.chained(dve.tensor_tensor(rows[:, 1, 0:ROW_EDGES - 1], rows[:, 0, 0:ROW_EDGES - 1],
                                          rows[:, 0, 1:ROW_EDGES], ALU.not_equal))
            dve.tensor_scalar(fresh[:, 1:ROW_EDGES], rows[:, 1, 0:ROW_EDGES - 1], -BIG, None, ALU.mult) \
               .then_inc(fresh_ready, 1)
            dve.wait_ge(fresh_ready, 1)
            dve.memset(fresh[:, :].rearrange("r (c e) -> r c e", e=P)[:, :, 0:1], 0.0).then_inc(fresh_ready, 2)
            dve.memset(rows[:, 1, :].rearrange("r (c e) -> r c e", e=P)[:, :, P - 1:P], 1.0).then_inc(rows_ready, 1)
            dve.wait_ge(src_in, 16)
            dve.tensor_copy(rows[:, 2, :], src_i[:, :]).then_inc(rows_ready, 1)
            for a in range(ARRAYS):
                dve.wait_ge(turned, CHUNKS * (a + 1))
                if a < 3:
                    out = K.edges[:, :, a * GT:(a + 1) * GT]
                else:
                    out = K.edges[:, :, 3 * GT:5 * GT].rearrange("p g (t j) -> p g t j", j=2)[:, :, :, a - 3]
                if a == 2:
                    out = out.bitcast(I32)
                dve.tensor_copy(out.rearrange("p (r h) t -> p r h t", h=CHUNKS // GT),
                                ps[:, a % 2, :, 0:EDGE_ROWS].rearrange("p (h t) r -> p r h t", t=GT)) \
                   .then_inc(kept, 1)
            dve.wait_ge(lines_spread, 1)
            own.done(dve.tensor_copy(group_no[:, :], K.iota[:, 0:GROUPS]))
            own.settle()
            for h in range(HALVES):
                own.chained(dve.tensor_scalar(below[:, h, :], ps_lines[:, 0, :], step_no[:, h:h + 1], None, ALU.is_le))
            own.chained(dve.tensor_reduce(step_g[:, :], below[:, :, :], AX.X, ALU.add))
            for h in range(HALVES):
                own.chained(dve.tensor_scalar(below[:, h, :], group_no[:, :], step_g[:, h:h + 1], None, ALU.is_equal))
                own.chained(dve.tensor_tensor(below[:, h, :], below[:, h, :], ps_lines[:, 1, :], ALU.mult))
            own.chained(dve.tensor_reduce(step_b[:, :], below[:, :, :], AX.X, ALU.add))
            own.chained(dve.tensor_tensor(step_b[:, :], step_b[:, :], step_no[:, :], ALU.add))
            own.chained(dve.tensor_scalar(late[:, :], step_g[:, :], float(GROUPS), float(STEPS), ALU.is_ge, ALU.mult))
            own.chained(dve.tensor_tensor(step_b[:, :], step_b[:, :], late[:, :], ALU.add))
            own.chained(dve.tensor_scalar(step_g[:, :], step_g[:, :], float(GROUPS - 1), None, ALU.min))
            dve.tensor_copy(step_i[:, 0, :], step_g[:, :]).then_inc(list_ready, 1)
            own.chained(dve.tensor_scalar(step_b[:, :], step_b[:, :], float(DUMMY), None, ALU.min))
            dve.tensor_copy(step_i[:, 1, :], step_b[:, :]).then_inc(list_ready, 1)

        @block.tensor
        def _(pe):
            pe.wait_ge(numbers, 5)
            for a in range(ARRAYS):
                if a < 3:
                    pe.wait_ge(rows_ready, a + 1)
                else:
                    pe.wait_ge(attr_in, 16)
                if a >= 2:
                    pe.wait_ge(kept, a - 1)
                for c in range(CHUNKS):
                    part = rows[:, a, c * P:(c + 1) * P] if a < 3 else attr[:, c * P:(c + 1) * P, a - 3]
                    pe.transpose(ps[:, a % 2, c, 0:EDGE_ROWS], part, K.identity[0:EDGE_ROWS, 0:EDGE_ROWS]) \
                      .then_inc(turned, 1)
                if a == 0:
                    pe.wait_ge(lines_ready, 1)
                    pe.matmul(ps_lines[:, :, :], K.ones[0:1, :], lines[:, :, :], start=True, stop=True) \
                      .then_inc(lines_spread, 1)


def first_tables(nc, K, x_tiles, w, att_src, att_dst):
    WIDE = W0 + H0
    CH = 10
    with ExitStack() as ctx:
        sb = lambda name, shape, dt=F32: ctx.enter_context(nc.sbuf_tensor(name, shape, dt))
        sem = ctx.enter_context(semaphores(nc))
        pb = lambda name, shape: ctx.enter_context(nc.psum_tensor(name, shape, F32))
        stats = sb("x_stats", [P, TILES, 6])
        mv = sb("x_mean_var", [P, TILES, 2])
        w_raw = sb("w_raw", [P, 2, D])
        w_sb = sb("w_sb", [P, 2, WIDE])
        wT = sb("wT", [P, 2, D])
        att = sb("att", [P, 2, 2 * H0])
        y = sb("y_tile", [P, FLOW, D])
        yT = sb("yT", [P, FLOW, 2, P])
        low = sb("low_score", [P, H0])
        lowT = sb("low_scoreT", [H0, 1])
        low_diag = sb("low_diag", [H0, H0])
        psT = [pb(f"yT_ps{k}", [P, 2, 2, P]) for k in range(BANKS)]
        psX = [pb(f"xh_ps{k}", [P, 512]) for k in range(BANKS)]
        x_in = [sem(f"x_in{c}") for c in range(TILES // CH)]
        w_in, att_in, att_zero = sem("w_in"), sem("att_in"), sem("att_zero")
        vec, stats_ready, wT_ps, wT_ready, fold_ps, w_ready = (sem(n) for n in (
            "tab_vec", "stats_ready", "wT_ps_ready", "wT_ready", "fold_ps", "w_ready"))
        y_ready, yT_turned, yT_ready, xh_ready, xh_kept, dst_kept, rows_out = (sem(n) for n in (
            "y_ready", "yT_turned", "yT_ready", "xh_ready", "xh_kept", "dst_kept", "rows_out"))
        own_ready, own_weight = sem("own_ready"), sem("own_weight")
        root_ready, low_ready, low_turned, low_spread = sem("root_ready"), sem("low_ready"), sem("low_turned"), sem("low_spread")
        block = ctx.enter_context(nc.Block())
        table_v = K.table0.rearrange("(t p) w -> p t w", p=P)
        heads = lambda ap: ap.rearrange("p (h c) -> p h c", c=DH0 + 1)

        @block.sync
        def _(sp):
            for k in range(2):
                sp.dma_start(w_raw[:, k, :], w[k * P:(k + 1) * P, :]).then_inc(w_in, 16)
                sp.dma_start(heads(w_sb[:, k, 0:W0])[:, :, 0:DH0],
                             w[k * P:(k + 1) * P, :].rearrange("p (h c) -> p h c", c=DH0)).then_inc(w_in, 16)
            sp.wait_ge(att_zero, 1)
            with nc.allow_non_contiguous_dma(reason="512 numbers, once"):
                for h in range(H0):
                    k, p0 = h * DH0 // P, h * DH0 % P
                    for j, src in enumerate((att_src, att_dst)):
                        sp.dma_start(att[p0:p0 + DH0, k, j * H0 + h:j * H0 + h + 1],
                                     src[h:h + 1, :].rearrange("h d -> d h")).then_inc(att_in, 16)
            for c in range(TILES // CH):
                sp.dma_start(K.R[:, c * CH:(c + 1) * CH, :],
                             x_tiles[:, c * CH:(c + 1) * CH, :]).then_inc(x_in[c], 16)
            with sp.Fori(0, TILES // FLOW) as i:
                for k in range(FLOW):
                    sp.wait_ge(xh_kept, i * FLOW + (k + 1))
                    sp.dma_start(table_v[:, bass.ds(i * FLOW + k, 1), :],
                                 K.acc[:, bass.ds(i * FLOW + k, 1), :]).then_inc(rows_out, 16)
            sp.wait_ge(rows_out, 16 * TILES)

        @block.vector
        def _(dve):
            own = Steps(dve, vec)
            dve.memset(att[:, :, :], 0.0).then_inc(att_zero, 1)
            for c in range(TILES // CH):
                dve.wait_ge(x_in[c], 16)
                for t in range(c * CH, (c + 1) * CH):
                    own.done(dve.bn_stats(stats[:, t, :], K.R[:, t, :]))
            own.settle()
            for t in range(TILES):
                own.done(dve.bn_aggr(mv[:, t, :], stats[:, t, :]))
            own.settle()
            dve.tensor_scalar(mv[:, :, 1], mv[:, :, 1], LN_EPS, None, ALU.add).then_inc(stats_ready, 1)
            dve.wait_ge(root_ready, 1)
            own.chained(dve.reciprocal(mv[:, :, 1], mv[:, :, 1]))
            with dve.Fori(0, TILES // FLOW) as i:
                own.loop(i, FLOW)
                dve.wait_ge(yT_turned, i * FLOW)
                dve.wait_ge(vec, own.base)
                for k in range(FLOW):
                    t = i * FLOW + k
                    dve.tensor_scalar(y[:, k, :], K.R[:, bass.ds(t, 1), :].rearrange("p t d -> p (t d)"),
                                      mv[:, bass.ds(t, 1), 0], mv[:, bass.ds(t, 1), 1],
                                      ALU.subtract, ALU.mult).then_inc(y_ready, 1)
                for k in range(FLOW):
                    t = i * FLOW + k
                    dve.wait_ge(y_ready, t + 1)
                    r = K.R[:, bass.ds(t, 1), :].rearrange("p t d -> p (t d)")
                    own.done(dve.tensor_tensor(r, r, y[:, k, :], ALU.add))
            own.left(TILES // FLOW)
            score = K.acc[:, :, :].rearrange("p t (h c) -> p t h c", c=DH0 + 1)[:, :, :, DH0]
            dve.wait_ge(xh_kept, TILES)
            dve.tensor_reduce(low[:, :], score.rearrange("p t h -> p h t"), AX.X, ALU.min).then_inc(low_ready, 1)
            dve.wait_ge(low_turned, 1)
            dve.tensor_reduce(lowT[:, :], psX[0][0:H0, 0:P], AX.X, ALU.min).then_inc(low_ready, 1)
            dve.wait_ge(low_ready, 2)
            dve.tensor_scalar(low_diag[:, :], K.identity[0:H0, 0:H0], lowT[:, 0:1], None, ALU.mult) \
               .then_inc(low_ready, 1)
            dve.wait_ge(low_spread, 1)
            own.done(dve.tensor_scalar(K.low_row[:, :, :], psX[1][:, 0:H0].rearrange("p (a h) -> p a h", a=1)
                                       .to_broadcast([P, GT, H0]), -1.0, None, ALU.mult))
            own.settle()
            minus_low = K.low_row[:, 0:1, :].to_broadcast([P, TILES, H0])
            own.done(dve.tensor_tensor(K.top_src[:, :, :], score, minus_low, ALU.add))
            dve.wait_ge(dst_kept, TILES)
            own.done(dve.tensor_tensor(K.low_dst[:, :, :], K.sc_dst[:, :, :], minus_low, ALU.subtract))
            for j in range(3):
                part = K.dst_parts[:, :, j * H0:(j + 1) * H0]
                own.chained(dve.tensor_copy(part, K.sc_dst[:, :, :]))
                if j < 2:
                    own.chained(dve.tensor_tensor(K.sc_dst[:, :, :], K.sc_dst[:, :, :], part, ALU.subtract))
            dve.wait_ge(rows_out, 16 * TILES)
            own.chained(dve.tensor_tensor(K.sc_dst[:, :, :], K.top_src[:, :, :], K.low_dst[:, :, :], ALU.add))
            own.chained(dve.scalar_tensor_tensor(K.sc_dst[:, :, :], K.sc_dst[:, :, :], 0.2, K.sc_dst[:, :, :],
                                                 ALU.mult, ALU.max))
            own.chained(dve.tensor_copy(K.shift[:, :, :], K.sc_dst[:, :, :]))
            own.chained(dve.tensor_tensor(score, K.sc_dst[:, :, :], K.shift[:, :, :], ALU.subtract))
            dve.sem_inc(own_ready, 1)
            dve.wait_ge(own_weight, 1)
            all_heads = K.acc[:, :, :].rearrange("p t (h c) -> p (t h) c", c=DH0 + 1)
            own.chained(dve.tensor_tensor(all_heads[:, :, 0:DH0], all_heads[:, :, 0:DH0],
                                          all_heads[:, :, DH0:DH0 + 1].to_broadcast([P, TILES * H0, DH0]), ALU.mult))

        @block.tensor
        def _(pe):
            pe.wait_ge(w_in, 64)
            for k in range(2):
                for j in range(2):
                    pe.transpose(psT[k][:, 0, j, :], w_raw[:, k, j * P:(j + 1) * P], K.identity[:, :]).then_inc(wT_ps, 1)
            pe.wait_ge(wT_ready, 2)
            pe.wait_ge(att_in, 16 * 2 * H0)
            for k in range(2):
                for j in range(2):
                    mm = pe.matmul(psX[k][:, 0:2 * H0], wT[:, j, k * P:(k + 1) * P], att[:, j, :],
                                   start=(j == 0), stop=(j == 1))
                mm.then_inc(fold_ps, 1)
            pe.wait_ge(w_ready, 4)
            with pe.Fori(0, TILES // FLOW) as i:
                for k in range(FLOW):
                    pe.wait_ge(y_ready, i * FLOW + (k + 1))
                    pe.wait_ge(yT_ready, i * FLOW + max(0, k + 1 - BANKS))
                    for j in range(2):
                        tr = pe.transpose(psT[k % BANKS][:, 0, j, :], y[:, k, j * P:(j + 1) * P], K.identity[:, :])
                    tr.then_inc(yT_turned, 1)
                for k in range(FLOW):
                    pe.wait_ge(yT_ready, i * FLOW + (k + 1))
                    pe.wait_ge(xh_kept, i * FLOW + max(0, k + 1 - BANKS))
                    pe.wait_ge(dst_kept, i * FLOW + max(0, k + 1 - BANKS))
                    for j in range(2):
                        mm = pe.matmul(psX[k % BANKS][:, 0:WIDE], yT[:, k, j, :], w_sb[:, j, :],
                                       start=(j == 0), stop=(j == 1))
                    mm.then_inc(xh_ready, 1)
            pe.wait_ge(low_ready, 1)
            pe.wait_ge(dst_kept, TILES)
            pe.transpose(psX[0][0:H0, 0:P], low[:, :], K.identity[:, :]).then_inc(low_turned, 1)
            pe.wait_ge(low_ready, 3)
            pe.matmul(psX[1][:, 0:H0], K.ones[0:H0, :], low_diag[:, :], start=True, stop=True) \
              .then_inc(low_spread, 1)

        @block.scalar
        def _(act):
            act.wait_ge(wT_ps, 4)
            for k in range(2):
                act.activation(wT[:, :, k * P:(k + 1) * P], psT[k][:, 0, :, :], ACT.Copy).then_inc(wT_ready, 1)
            act.wait_ge(fold_ps, 2)
            act.wait_ge(w_in, 64)
            for k in range(2):
                act.activation(heads(w_sb[:, k, 0:W0])[:, :, DH0:DH0 + 1],
                               psX[k][:, 0:H0].rearrange("p (h a) -> p h a", a=1), ACT.Copy).then_inc(w_ready, 1)
                act.activation(w_sb[:, k, W0:WIDE], psX[k][:, H0:2 * H0], ACT.Copy).then_inc(w_ready, 1)
            act.wait_ge(stats_ready, 1)
            act.activation(mv[:, :, 1], mv[:, :, 1], ACT.Sqrt).then_inc(root_ready, 1)
            with act.Fori(0, TILES // FLOW) as i:
                for k in range(FLOW):
                    act.wait_ge(yT_turned, i * FLOW + (k + 1))
                    act.wait_ge(xh_ready, i * FLOW)
                    act.activation(yT[:, k, :, :], psT[k % BANKS][:, 0, :, :], ACT.Copy).then_inc(yT_ready, 1)
                for k in range(FLOW):
                    t = i * FLOW + k
                    act.wait_ge(xh_ready, t + 1)
                    act.activation(K.acc[:, bass.ds(t, 1), :].rearrange("p t w -> p (t w)"), psX[k % BANKS][:, 0:W0],
                                   ACT.Copy).then_inc(xh_kept, 1)
                    act.activation(K.sc_dst[:, bass.ds(t, 1), :].rearrange("p t h -> p (t h)"),
                                   psX[k % BANKS][:, W0:WIDE], ACT.Copy).then_inc(dst_kept, 1)
            score = K.acc[:, :, :].rearrange("p t (h c) -> p t h c", c=DH0 + 1)[:, :, :, DH0]
            act.wait_ge(own_ready, 1)
            act.activation(score, score, ACT.Exp).then_inc(own_weight, 1)


def at_block(ap, b):
    return ap[:, bass.ds(b, 1), :].rearrange("p t c -> p (t c)")


def seen(eng, sem, s):
    if not isinstance(s, int) or s >= 0:
        eng.wait_ge(sem, s + 1)


def exists(s, steps=STEPS):
    return not isinstance(s, int) or 0 <= s < steps


def slots(eng, slot, lag=0, after_loop=None, steps=STEPS):
    for k in range(UNROLL):
        slot(k, k, 0)
    with eng.Fori(1, steps // UNROLL) as i:
        for k in range(UNROLL):
            slot(i * UNROLL + k, k, i)
    if after_loop:
        after_loop()
    for k in range(lag):
        slot(steps + k, k, steps // UNROLL)


def load_list(nc, K, which, first, n, top, engine):
    _, values = nc.values_load_multi_w_load_instructions(
        K.step_list[0:1, which, bass.ds(first, n)], engines=(engine,), min_val=0, max_val=top)
    return list(values)


class Listed:

    def __init__(self, K, eng, line, top):
        self.eng, self.line, self.top = eng, line, top
        if eng.engine not in K.registers:
            K.registers[eng.engine] = [[eng.alloc_register(f"listed_{n}{k}") for k in range(UNROLL)]
                                       for n in ("now", "past")]
        self.now, self.past = K.registers[eng.engine]
        eng.load(self.now, line[:, 0:UNROLL])
        for r in self.past:
            eng.reg_mov(r, 0)

    def read(self):
        self.values = [self.eng.snap(r, min_val=0, max_val=self.top) for r in self.past + self.now]

    def of(self, k, lag):
        return self.values[UNROLL + k - lag]

    def fetch(self, i):
        for p, r in zip(self.past, self.now):
            self.eng.reg_mov(p, r)
        self.eng.load(self.now, self.line[:, bass.ds((i + 1) * UNROLL, UNROLL)])


def first_edges(nc, K):
    with ExitStack() as ctx:
        sb = lambda name, shape, dt=F32: ctx.enter_context(nc.sbuf_tensor(name, shape, dt))
        sem = ctx.enter_context(semaphores(nc))
        pb = lambda name: ctx.enter_context(nc.psum_tensor(name, [P, 512], F32))
        step_data = [sb(f"step_data{k}", [P, 3 * GT]) for k in range(UNROLL)]
        fresh = [sb(f"fresh{k}", [GT * H0, P]) for k in range(UNROLL)]
        dst_here = [sb(f"dst_here{k}", [P, GT]) for k in range(2)]
        rows = [sb(f"gathered{k}", [P, GT, W0]) for k in range(UNROLL)]
        sel = [sb(f"sel{k}", [P, GT, P], BF16) for k in range(UNROLL)]
        sel_f = [sb(f"sel_f{k}", [P, GT, P]) for k in range(UNROLL)]
        selT = [sb(f"selT{k}", [P, GT, P], BF16) for k in range(2)]
        running = [sb(f"running{k}", [GT * H0, P], BF16) for k in range(2)]
        run_top = [sb(f"run_top{k}", [P, GT, H0], BF16) for k in range(2)]
        node_top = sb("node_top", [P, H0])
        score = sb("node_score", [P, H0])
        node = [sb(f"node{k}", [P, 4 * H0], BF16) for k in range(2)]
        drop = [sb(f"drop{k}", [P, H0]) for k in range(2)]
        scale = [sb(f"scale{k}", [P, H0]) for k in range(UNROLL)]
        z = sb("z", [P, GT, H0])
        z_low = [sb(f"z_low{k}", [P, GT, H0]) for k in range(2)]
        msg = [sb(f"msg{k}", [P, GT, W0]) for k in range(2)]
        low_line = sb("low_line", [1, GT * H0], BF16)
        ps_scoreT, ps_run, ps_top, ps_edge = (pb(n) for n in ("ps_scoreT", "ps_run", "ps_top", "ps_edge"))
        ps_selT = ctx.enter_context(nc.psum_tensor("ps_selT", [P, 2 * GT * P], BF16))
        ps_sum = [pb(f"ps_sum{k}") for k in range(2)]
        data_in = [sem(f"data_in{k}") for k in range(UNROLL)]
        gathered = [sem(f"gathered{k}") for k in range(UNROLL)]
        vec, low_ready = sem("e0_vec"), sem("low_line_ready")
        scoreT_ready, scanned, run_turned, run_top_ready, sel_ready, top_ready = (sem(n) for n in (
            "scoreT_ready", "scanned", "run_turned", "run_top_ready", "sel_ready", "top_ready"))
        selT_turned, selT_ready, node_ready, scale_ready, edge_ready, z_ready, p_ready, msg_ready = (
            sem(n) for n in ("selT_turned", "selT_ready", "node_ready", "scale_ready", "edge_ready",
                             "z_ready", "p_ready", "msg_ready"))
        sum_ready, acc_ready, sel_f_ready, parts_ready = (sem(n) for n in (
            "sum_ready", "acc_ready", "sel_f_ready", "parts_ready"))
        data_wanted, rows_wanted, dst_ready = sem("data_wanted"), sem("rows_wanted"), sem("dst_ready")
        block = ctx.enter_context(nc.Block())
        heads = lambda ap: ap.rearrange("p t (h c) -> p t h c", c=DH0 + 1)


        @block.sync
        def _(sp):
            groups = []

            def slot(s, k, i):
                if k == 0:
                    groups[:] = load_list(nc, K, 0, UNROLL + i * UNROLL, UNROLL, GROUPS - 1, ENG.SP)
                g = groups[k]
                edges = sp.snap(g * (5 * GT), min_val=0, max_val=(GROUPS - 1) * 5 * GT)
                marks = sp.snap(g * (GT * H0), min_val=0, max_val=(GROUPS - 1) * GT * H0)
                if not isinstance(i, int):
                    sp.wait_ge(gathered[k], i * (16 * GT))
                    sp.sem_inc(data_wanted, 1)
                    for used in (sel_ready, run_top_ready, scanned):
                        seen(sp, used, s - UNROLL)
                sp.sem_inc(data_wanted, 1)
                sp.dma_start(step_data[k][:, :], K.edges[:, :, :].rearrange("p g c -> p (g c)")
                             [:, bass.ds(edges, 3 * GT)]).then_inc(data_in[k], 16)
                sp.dma_start(fresh[k][:, :], K.fresh_dram.rearrange("t h e -> (t h) e")
                             [bass.ds(marks, GT * H0), :]).then_inc(data_in[k], 16)

            slots(sp, slot)

        @block.gpsimd
        def _(pool):
            def slot(s, k, i):
                pool.wait_ge(data_in[k], (i + 1) * 32)
                seen(pool, msg_ready, s - UNROLL)
                pool.sem_inc(rows_wanted, 1)
                for t in range(GT):
                    pool.indirect_dma_start(
                        rows[k][:, t, :], None, K.table0[:, :],
                        bass.IndirectOffsetOnAxis(ap=step_data[k][:, 2 * GT + t:2 * GT + t + 1].bitcast(I32), axis=0)
                    ).then_inc(gathered[k], 16)

            slots(pool, slot)

        @block.tensor
        def _(pe):
            def turn_scores(s, k, i):
                pe.wait_ge(gathered[k], (i + 1) * (16 * GT))
                seen(pe, scanned, s - 1)
                pe.transpose(ps_scoreT[0:GT * H0, 0:P], heads(rows[k][:, :, :])[:, :, :, DH0], K.identity[:, :]) \
                  .then_inc(scoreT_ready, 1)

            def turn_maxima(s, k):
                seen(pe, scanned, s)
                seen(pe, run_top_ready, s - 1)
                pe.matmul(ps_run[:, 0:GT * H0], running[k % 2][:, :], K.identity_b[0:GT * H0, 0:GT * H0],
                          start=True, stop=False)
                pe.matmul(ps_run[:, 0:GT * H0], K.ones_b[0:1, :], low_line[:, :], start=False, stop=True) \
                  .then_inc(run_turned, 1)

            def node_maxima(s, k):
                seen(pe, sel_ready, s)
                seen(pe, run_top_ready, s)
                seen(pe, node_ready, s - 1)
                for t in range(GT):
                    mm = pe.matmul(ps_top[:, t * H0:(t + 1) * H0], sel[k][:, t, :], run_top[k % 2][:, t, :],
                                   start=True, stop=True)
                mm.then_inc(top_ready, 1)

            def turn_sel(s, k):
                seen(pe, selT_ready, s - 1)
                for t in range(GT):
                    tr = pe.transpose(ps_selT[:, t * P:(t + 1) * P], sel[k][:, t, :], K.identity_b[:, :])
                tr.then_inc(selT_turned, 1)

            def to_edges(s, k):
                seen(pe, node_ready, s)
                seen(pe, parts_ready, s)
                seen(pe, selT_ready, s)
                seen(pe, z_ready, s - 1)
                for t in range(GT):
                    pe.matmul(ps_edge[:, (GT + t) * H0:(GT + t + 1) * H0], selT[k % 2][:, t, :],
                              node[k % 2][:, 3 * H0:4 * H0], start=True, stop=True)
                    for j in range(3):
                        mm = pe.matmul(ps_edge[:, t * H0:(t + 1) * H0], selT[k % 2][:, t, :],
                                       node[k % 2][:, j * H0:(j + 1) * H0], start=(j == 0), stop=(j == 2))
                mm.then_inc(edge_ready, 1)

            def sums(s, k, part):
                if part == 0:
                    seen(pe, msg_ready, s)
                    seen(pe, sel_f_ready, s)
                    seen(pe, acc_ready, s - 2)
                for t in range(part * GT // 2, (part + 1) * GT // 2):
                    mm = pe.matmul(ps_sum[k % 2][:, 0:W0], sel_f[k][:, t, :], msg[k % 2][:, t, :],
                                   start=(t == 0), stop=(t == GT - 1))
                if part == 1:
                    mm.then_inc(sum_ready, 1)

            def slot(s, k, i):
                if exists(s):
                    turn_scores(s, k, i)
                if exists(s - 3):
                    sums(s - 3, (k - 3) % UNROLL, 0)
                if exists(s):
                    turn_maxima(s, k)
                if exists(s - 3):
                    sums(s - 3, (k - 3) % UNROLL, 1)
                if exists(s - 1):
                    to_edges(s - 1, (k - 1) % UNROLL)
                if exists(s):
                    node_maxima(s, k)
                    turn_sel(s, k)

            pe.wait_ge(low_ready, 1)
            slots(pe, slot, lag=3)

        @block.scalar
        def _(act):
            blocks = []

            def slot(s, k, i):
                if k == 0 and exists(s):
                    blocks[:] = load_list(nc, K, 1, UNROLL + i * UNROLL, UNROLL, DUMMY, ENG.Activation)
                if exists(s):
                    seen(act, edge_ready, s - 2)
                    act.activation(node[k % 2][:, 0:3 * H0], at_block(K.dst_parts, blocks[k]), ACT.Copy) \
                       .then_inc(parts_ready, 1)
                    act.wait_ge(data_in[k], (i + 1) * 32)
                    seen(act, sel_ready, s - 2)
                    act.activation(dst_here[k % 2][:, :], step_data[k][:, 0:GT], ACT.Identity,
                                   bias=K.minus_first[:, bass.ds(blocks[k], 1)]).then_inc(dst_ready, 1)
                if exists(s - 2):
                    seen(act, z_ready, s - 2)
                    seen(act, sum_ready, s - 4)
                    act.activation(heads(msg[k % 2][:, :, :])[:, :, :, DH0], z_low[k % 2][:, :, :], ACT.Exp) \
                       .then_inc(p_ready, 1)
                if exists(s - 1):
                    seen(act, node_ready, s - 1)
                    seen(act, acc_ready, s - 5)
                    act.activation(scale[(k - 1) % UNROLL][:, :], drop[(k - 1) % 2][:, :], ACT.Exp) \
                       .then_inc(scale_ready, 1)
                if exists(s):
                    seen(act, sel_ready, s)
                    seen(act, sum_ready, s - UNROLL)
                    act.activation(sel_f[k][:, :, :], sel[k][:, :, :], ACT.Copy).then_inc(sel_f_ready, 1)
                    seen(act, selT_turned, s)
                    seen(act, edge_ready, s - 2)
                    act.activation(selT[k % 2][:, :, :].rearrange("p t e -> p (t e)"), ps_selT[:, 0:GT * P],
                                   ACT.Copy).then_inc(selT_ready, 1)

            slots(act, slot, lag=2)

        @block.vector
        def _(dve):
            own = Steps(dve, vec)
            blocks = Listed(K, dve, K.step_list[0:1, 1, UNROLL:], DUMMY)

            def slot(s, k, i):
                if k == 0:
                    if not isinstance(i, int):
                        own.loop(i - 1, PER_ROUND)
                    blocks.read()
                now, node_step, edge_step, sum_step = exists(s), exists(s - 1), exists(s - 2), exists(s - 4)
                kn, ke, ks = (k - 1) % UNROLL, (k - 2) % UNROLL, (k - 4) % UNROLL
                edge = ps_edge[:, 0:2 * GT * H0].rearrange("p (j t h) -> p j t h", j=2, h=H0)
                bn, bs = blocks.of(k, 1), blocks.of(k, 4)
                top, shift, new = at_block(K.top_src, bn), at_block(K.shift, bn), node[kn % 2][:, 3 * H0:4 * H0]
                acc = at_block(K.acc, bs)
                own.settle()
                if edge_step:
                    seen(dve, edge_ready, s - 2)
                    seen(dve, z_ready, s - 3)
                    za = own.done(dve.tensor_tensor(z[:, :, :], heads(rows[ke][:, :, :])[:, :, :, DH0],
                                                    edge[:, 0, :, :], ALU.add))
                if node_step:
                    seen(dve, top_ready, s - 1)
                    na = own.done(dve.tensor_reduce(node_top[:, :], ps_top[:, 0:GT * H0]
                                                    .rearrange("p (t h) -> p h t", h=H0), AX.X, ALU.max))
                if now:
                    seen(dve, scoreT_ready, s)
                    dve.wait_ge(data_in[k], (i + 1) * 32)
                    seen(dve, run_turned, s - 2)
                    dve.tensor_tensor_scan(running[k % 2][:, :], fresh[k][:, :], ps_scoreT[0:GT * H0, 0:P],
                                           -3 * BIG, ALU.add, ALU.max).then_inc(scanned, 1)
                if edge_step:
                    own.until(za)
                    za = own.done(dve.scalar_tensor_tensor(z[:, :, :], z[:, :, :], 0.2, z[:, :, :],
                                                           ALU.mult, ALU.max))
                if node_step:
                    own.until(na)
                    na = own.done(dve.tensor_tensor(top, top, node_top[:, :], ALU.max))
                if sum_step:
                    seen(dve, scale_ready, s - 4)
                    seen(dve, acc_ready, s - 5)
                    acc_h = acc.rearrange("p (h c) -> p h c", c=DH0 + 1)
                    sa = own.done(dve.tensor_tensor(
                        acc_h, acc_h, scale[ks][:, :].rearrange("p (h a) -> p h a", a=1)
                        .to_broadcast([P, H0, DH0 + 1]), ALU.mult))
                if edge_step:
                    own.until(za)
                    za = own.done(dve.tensor_tensor(z[:, :, :], z[:, :, :], edge[:, 1, :, :], ALU.subtract))
                if node_step:
                    own.until(na)
                    na = own.done(dve.tensor_tensor(score[:, :], top, at_block(K.low_dst, bn), ALU.add))
                if now:
                    seen(dve, run_turned, s)
                    seen(dve, top_ready, s - 2)
                    last = step_data[k][:, GT:2 * GT].rearrange("p (t a) -> p t a", a=1).to_broadcast([P, GT, H0])
                    dve.tensor_tensor(run_top[k % 2][:, :, :],
                                      ps_run[:, 0:GT * H0].rearrange("p (t h) -> p t h", h=H0),
                                      last, ALU.mult).then_inc(run_top_ready, 1)
                if edge_step:
                    own.until(za)
                    seen(dve, p_ready, s - 4)
                    dve.tensor_scalar(z_low[ke % 2][:, :, :], z[:, :, :], SAFE, None, ALU.min).then_inc(z_ready, 1)
                if node_step:
                    own.until(na)
                    seen(dve, edge_ready, s - 3)
                    na = own.done(dve.scalar_tensor_tensor(new, score[:, :], 0.2, score[:, :], ALU.mult, ALU.max))
                if sum_step:
                    own.until(sa)
                    seen(dve, sum_ready, s - 4)
                    dve.tensor_tensor(acc, acc, ps_sum[ks % 2][:, 0:W0], ALU.add).then_inc(acc_ready, 1)
                if node_step:
                    own.until(na)
                    seen(dve, scale_ready, s - 3)
                    dve.tensor_tensor(drop[kn % 2][:, :], shift, new, ALU.subtract).then_inc(node_ready, 1)
                if now:
                    for used in (sel_f_ready, selT_turned, top_ready):
                        seen(dve, used, s - UNROLL)
                    seen(dve, dst_ready, s)
                    dve.tensor_tensor(
                        sel[k][:, :, :],
                        dst_here[k % 2][:, :].rearrange("p (t a) -> p t a", a=1).to_broadcast([P, GT, P]),
                        K.iota[:, 0:P].rearrange("p (a n) -> p a n", a=1).to_broadcast([P, GT, P]),
                        ALU.is_equal).then_inc(sel_ready, 1)
                if node_step:
                    seen(dve, node_ready, s - 1)
                    own.done(dve.tensor_scalar(shift, new, 0.0, None, ALU.add))
                if edge_step:
                    seen(dve, p_ready, s - 2)
                    dve.tensor_tensor(heads(msg[ke % 2][:, :, :])[:, :, :, 0:DH0],
                                      heads(rows[ke][:, :, :])[:, :, :, 0:DH0],
                                      heads(msg[ke % 2][:, :, :])[:, :, :, DH0:DH0 + 1]
                                      .to_broadcast([P, GT, H0, DH0]), ALU.mult).then_inc(msg_ready, 1)
                if k == UNROLL - 1:
                    blocks.fetch(i)

            PER_ROUND = UNROLL * 9
            dve.tensor_copy(low_line[:, :], K.low_row[0:1, :, :].rearrange("p t h -> p (t h)")).then_inc(low_ready, 1)
            slots(dve, slot, lag=4, after_loop=lambda: own.left(STEPS // UNROLL - 1))


def batch_norm(nc, K, bias, gamma, beta):
    CH = 10
    CHS = TILES // CH
    TAIL = N_NODES - (BLOCKS - 1) * P
    with ExitStack() as ctx:
        sb = lambda name, shape, dt=F32: ctx.enter_context(nc.sbuf_tensor(name, shape, dt))
        sem = ctx.enter_context(semaphores(nc))
        affine = sb("bn_affine", [P, 3, D])
        square = sb("bn_square", [P, 4, D])
        mean = sb("bn_mean", [P, D])
        factor = sb("bn_factor", [P, D])
        tail = sb("tail_ones", [P, P])
        zero = sb("zero_rows", [P, D])
        ps_mean = ctx.enter_context(nc.psum_tensor("ps_mean", [P, 512], F32))
        ps_var = ctx.enter_context(nc.psum_tensor("ps_var", [P, 512], F32))
        affine_in, tail_ready, zero_ready, zeroed, beta_added = (sem(n) for n in (
            "affine_in", "tail_ready", "zero_ready", "zeroed", "beta_added"))
        vec, out_ready, mean_ready, centred, squared, square_used, var_ready, vareps, root = (sem(n) for n in (
            "bn_vec", "out_ready", "mean_ready", "centred", "squared", "square_used", "var_ready", "vareps", "root"))
        block = ctx.enter_context(nc.Block())
        ZT = 12
        heads = lambda ap: ap.rearrange("p t (h c) -> p t h c", c=DH0 + 1)
        of_heads = lambda ap: ap.rearrange("p (a h c) -> p a h c", a=1, c=DH0)

        @block.sync
        def _(sp):
            for j, v in enumerate((bias, gamma, beta)):
                sp.dma_start(affine[:, j, :], v.rearrange("(a n) -> a n", a=1).to_broadcast([P, D])) \
                  .then_inc(affine_in, 16)
            sp.wait_ge(zero_ready, 1)
            slots_v = K.slot_x.rearrange("(t p) d -> p t d", p=P)
            for t in range(0, SLOT_TILES, ZT):
                sp.dma_start(slots_v[:, t:t + ZT, :],
                             zero[:, :].rearrange("p (a d) -> p a d", a=1).to_broadcast([P, ZT, D])) \
                  .then_inc(zeroed, 16)
            sp.wait_ge(zeroed, 16 * (SLOT_TILES // ZT))

        @block.gpsimd
        def _(pool):
            pool.memset(zero[:, :], 0.0).then_inc(zero_ready, 1)
            pool.affine_select(out=tail[:, :], in_=K.ones[:, :], compare_op=ALU.is_ge, fill=0.0,
                               base=TAIL - 1, pattern=[[0, P]], channel_multiplier=-1).then_inc(tail_ready, 1)
            pool.wait_ge(affine_in, 48)
            for c in range(CHS):
                r = K.R[:, c * CH:(c + 1) * CH, :]
                pool.tensor_tensor(r, r, affine[:, 2:3, :].to_broadcast([P, CH, D]), ALU.add).then_inc(beta_added, 1)

        @block.vector
        def _(dve):
            own = Steps(dve, vec)
            weight = heads(K.acc[:, :, :])[:, :, :, DH0:DH0 + 1]
            own.chained(dve.reciprocal(weight, weight))
            dve.wait_ge(affine_in, 48)
            for c in range(CHS):
                part = heads(K.acc[:, c * CH:(c + 1) * CH, :])
                out = part[:, :, :, 0:DH0].rearrange("p t h c -> p (t h) c")
                own.chained(dve.tensor_tensor(out, out, part[:, :, :, DH0:DH0 + 1].rearrange("p t h c -> p (t h) c")
                                              .to_broadcast([P, CH * H0, DH0]), ALU.mult))
                out = part[:, :, :, 0:DH0]
                dve.tensor_tensor(out, out, of_heads(affine[:, 0, :]).to_broadcast([P, CH, H0, DH0]), ALU.add) \
                   .then_inc(out_ready, 1)
            dve.wait_ge(mean_ready, 1)
            own.chained(dve.tensor_scalar(mean[:, :], ps_mean[:, 0:D], 1.0 / N_NODES, None, ALU.mult))
            dve.wait_ge(out_ready, CHS)
            for c in range(CHS):
                out = heads(K.acc[:, c * CH:(c + 1) * CH, :])[:, :, :, 0:DH0]
                dve.tensor_tensor(out, out, of_heads(mean[:, :]).to_broadcast([P, CH, H0, DH0]), ALU.subtract) \
                   .then_inc(centred, 1)
            dve.wait_ge(var_ready, 1)
            dve.tensor_scalar(factor[:, :], ps_var[:, 0:D], 1.0 / N_NODES, LN_EPS, ALU.mult, ALU.add) \
               .then_inc(vareps, 1)
            dve.wait_ge(root, 1)
            own.chained(dve.reciprocal(factor[:, :], factor[:, :]))
            own.chained(dve.tensor_tensor(factor[:, :], factor[:, :], affine[:, 1, :], ALU.mult))
            dve.wait_ge(centred, CHS)
            dve.wait_ge(squared, BLOCKS)
            for c in range(CHS):
                out = heads(K.acc[:, c * CH:(c + 1) * CH, :])[:, :, :, 0:DH0]
                own.done(dve.tensor_tensor(out, out, of_heads(factor[:, :]).to_broadcast([P, CH, H0, DH0]), ALU.mult))
            for c in range(CHS):
                if c == 0:
                    own.settle()
                dve.wait_ge(beta_added, c + 1)
                r = K.R[:, c * CH:(c + 1) * CH, :].rearrange("p t (h c) -> p t h c", c=DH0)
                own.done(dve.tensor_tensor(r, r, heads(K.acc[:, c * CH:(c + 1) * CH, :])[:, :, :, 0:DH0], ALU.add))
            own.settle()

        @block.scalar
        def _(act):
            for t in range(BLOCKS):
                act.wait_ge(centred, t // CH + 1)
                if t >= 4:
                    act.wait_ge(square_used, t - 3)
                act.activation(square[:, t % 4, :].rearrange("p (h c) -> p h c", c=DH0),
                               heads(K.acc[:, t:t + 1, :])[:, 0, :, 0:DH0], ACT.Square).then_inc(squared, 1)
            act.wait_ge(vareps, 1)
            act.activation(factor[:, :], factor[:, :], ACT.Sqrt).then_inc(root, 1)

        @block.tensor
        def _(pe):
            pe.wait_ge(tail_ready, 1)
            for t in range(BLOCKS):
                pe.wait_ge(out_ready, t // CH + 1)
                mm = pe.matmul(ps_mean[:, 0:D], (tail if t == BLOCKS - 1 else K.ones)[:, :],
                               heads(K.acc[:, t:t + 1, :])[:, 0, :, 0:DH0], start=(t == 0), stop=(t == BLOCKS - 1))
            mm.then_inc(mean_ready, 1)
            for t in range(BLOCKS):
                pe.wait_ge(squared, t + 1)
                mm = pe.matmul(ps_var[:, 0:D], (tail if t == BLOCKS - 1 else K.ones)[:, :], square[:, t % 4, :],
                               start=(t == 0), stop=(t == BLOCKS - 1)).then_inc(square_used, 1)
            pe.wait_ge(square_used, BLOCKS)
            pe.sem_inc(var_ready, 1)


class Normalised:

    def __init__(self, nc, ctx, name, x):
        self.x = x
        self.stats = ctx.enter_context(nc.sbuf_tensor(f"{name}_stats", [P, TILES, 6], F32))
        self.mv = ctx.enter_context(nc.sbuf_tensor(f"{name}_mean_var", [P, TILES, 2], F32))
        sem = ctx.enter_context(semaphores(nc))
        self.stats_ready, self.root_ready = sem(f"{name}_stats_ready"), sem(f"{name}_root_ready")

    def statistics(self, dve, own):
        for t in range(TILES):
            own.done(dve.bn_stats(self.stats[:, t, :], self.x[:, t, :]))
        own.settle()
        for t in range(TILES):
            own.done(dve.bn_aggr(self.mv[:, t, :], self.stats[:, t, :]))
        own.settle()
        dve.tensor_scalar(self.mv[:, :, 1], self.mv[:, :, 1], LN_EPS, None, ALU.add).then_inc(self.stats_ready, 1)
        dve.wait_ge(self.root_ready, 1)
        own.chained(dve.reciprocal(self.mv[:, :, 1], self.mv[:, :, 1]))

    def roots(self, act):
        act.wait_ge(self.stats_ready, 1)
        act.activation(self.mv[:, :, 1], self.mv[:, :, 1], ACT.Sqrt).then_inc(self.root_ready, 1)

    def tile(self, dve, y, t):
        return dve.tensor_scalar(y, at_block(self.x, t), self.mv[:, bass.ds(t, 1), 0], self.mv[:, bass.ds(t, 1), 1],
                                 ALU.subtract, ALU.mult)


def gate(nc, K, norm, wg, bg, bias):
    with ExitStack() as ctx:
        sb = lambda name, shape, dt=F32: ctx.enter_context(nc.sbuf_tensor(name, shape, dt))
        sem = ctx.enter_context(semaphores(nc))
        E = EXPERTS
        y = sb("gate_y", [P, FLOW, D])
        yT = sb("gate_yT", [P, FLOW, 2, P])
        wg_sb = sb("wg_sb", [P, 2, E])
        offset = sb("gate_offset", [P, 2, E])
        logits = sb("logits", [P, TILES, E])
        best = sb("best", [P, TILES, E])
        best_i = sb("best_i", [P, TILES, E], mybir.dt.uint32)
        choice = sb("choice", [P, TILES, 2])
        gap = sb("gap", [P, TILES])
        one_hot = sb("one_hot", [P, 2, TILES, E])
        taken = sb("taken", [P, TILES, E])
        before = sb("before", [P, P])
        keep = sb("keep", [P, E, TILES])
        by_tile = sb("by_tile", [P, E, TILES])
        upto = sb("upto", [P, E, TILES])
        tiles_i = sb("expert_tiles_i", [P, E], I32)
        tiles_f = sb("expert_tiles", [P, E])
        zero8 = sb("zero8", [P, E])
        ends = sb("expert_ends", [P, E])
        place = sb("place", [P, TILES, E])
        owner = sb("owner_f", [1, OWNERS])
        slot_f = sb("slot_f", [P, 2, TILES])
        psT = [ctx.enter_context(nc.psum_tensor(f"gate_psT{k}", [P, 512], F32)) for k in range(3)]
        psL = [ctx.enter_context(nc.psum_tensor(f"gate_psL{k}", [P, 512], F32)) for k in range(3)]
        vec, w_in, y_ready, turned, yT_ready, logit_ready, logit_kept = (sem(n) for n in (
            "gate_vec", "wg_in", "gate_y_ready", "gate_turned", "gate_yT_ready", "logit_ready", "logit_kept"))
        before_ready, taken_ready, ranked, gap_ready, gap_exp = (sem(n) for n in (
            "before_ready", "taken_ready", "ranked", "gap_ready", "gap_exp"))
        NB = 3
        block = ctx.enter_context(nc.Block())

        @block.sync
        def _(sp):
            for k in range(2):
                sp.dma_start(wg_sb[:, k, :], wg[k * P:(k + 1) * P, :]).then_inc(w_in, 16)
            for j, v in enumerate((bg, bias)):
                sp.dma_start(offset[:, j, :], v.rearrange("(a n) -> a n", a=1).to_broadcast([P, E])).then_inc(w_in, 16)

        @block.gpsimd
        def _(pool):
            pool.affine_select(out=before[:, :], in_=K.ones[:, :], compare_op=ALU.is_ge, fill=0.0,
                               base=-1, pattern=[[1, P]], channel_multiplier=-1).then_inc(before_ready, 1)

        @block.scalar
        def _(act):
            norm.roots(act)
            with act.Fori(0, TILES // FLOW) as i:
                for k in range(FLOW):
                    act.wait_ge(turned, i * FLOW + (k + 1))
                    act.wait_ge(logit_ready, i * FLOW)
                    act.activation(yT[:, k, :, :].rearrange("p j e -> p (j e)"), psT[k % NB][:, 0:D], ACT.Copy) \
                       .then_inc(yT_ready, 1)
                for k in range(FLOW):
                    act.wait_ge(logit_ready, i * FLOW + (k + 1))
                    act.activation(at_block(logits, i * FLOW + k), psL[k % NB][:, 0:E], ACT.Copy) \
                       .then_inc(logit_kept, 1)
            act.wait_ge(gap_ready, 1)
            act.activation(gap[:, :], gap[:, :], ACT.Exp).then_inc(gap_exp, 1)

        @block.tensor
        def _(pe):
            pe.wait_ge(w_in, 64)
            with pe.Fori(0, TILES // FLOW) as i:
                for k in range(FLOW):
                    pe.wait_ge(y_ready, i * FLOW + (k + 1))
                    pe.wait_ge(yT_ready, i * FLOW + max(0, k + 1 - NB))
                    for j in range(2):
                        tr = pe.transpose(psT[k % NB][:, j * P:(j + 1) * P], y[:, k, j * P:(j + 1) * P],
                                          K.identity[:, :])
                    tr.then_inc(turned, 1)
                for k in range(FLOW):
                    pe.wait_ge(yT_ready, i * FLOW + (k + 1))
                    pe.wait_ge(logit_kept, i * FLOW + max(0, k + 1 - NB))
                    for j in range(2):
                        mm = pe.matmul(psL[k % NB][:, 0:E], yT[:, k, j, :], wg_sb[:, j, :],
                                       start=(j == 0), stop=(j == 1))
                    mm.then_inc(logit_ready, 1)
            pe.wait_ge(before_ready, 1)
            pe.wait_ge(taken_ready, 1)
            pe.wait_ge(logit_kept, TILES)
            flat = taken[:, :, :].rearrange("p t e -> p (t e)")
            pe.matmul(psL[0][:, 0:TILES * E], before[:, :], flat, start=True, stop=True).then_inc(ranked, 1)
            pe.matmul(psL[1][:, 0:TILES * E], K.ones[:, :], flat, start=True, stop=True).then_inc(ranked, 1)

        @block.vector
        def _(dve):
            own = Steps(dve, vec)
            norm.statistics(dve, own)
            with dve.Fori(0, TILES // FLOW) as i:
                for k in range(FLOW):
                    dve.wait_ge(turned, i * FLOW)
                    norm.tile(dve, y[:, k, :], i * FLOW + k).then_inc(y_ready, 1)
            dve.wait_ge(logit_kept, TILES)
            dve.wait_ge(w_in, 64)
            for j in range(2):
                own.chained(dve.tensor_tensor(logits[:, :, :], logits[:, :, :],
                                              offset[:, j:j + 1, :].to_broadcast([P, TILES, E]), ALU.add))
            for t in range(TILES):
                own.done(dve.max(best[:, t, :], logits[:, t, :]))
            own.settle()
            for t in range(TILES):
                own.done(dve.max_index(best_i[:, t, :], best[:, t, :], logits[:, t, :]))
            own.done(dve.memset(keep[:, :, :], 1.0))
            own.done(dve.memset(zero8[:, :], 0.0))
            own.settle()
            dve.tensor_tensor(gap[:, :], best[:, :, 1], best[:, :, 0], ALU.subtract).then_inc(gap_ready, 1)
            own.done(dve.memset(keep[:, :, 0:1], 0.0))
            own.chained(dve.tensor_copy(choice[:, :, :], best_i[:, :, 0:2]))
            for j in range(2):
                own.done(dve.tensor_tensor(
                    one_hot[:, j, :, :], choice[:, :, j:j + 1].to_broadcast([P, TILES, E]),
                    K.iota[:, 0:E].rearrange("p (a e) -> p a e", a=1).to_broadcast([P, TILES, E]), ALU.is_equal))
            own.settle()
            dve.tensor_tensor(taken[:, :, :], one_hot[:, 0, :, :], one_hot[:, 1, :, :], ALU.add) \
               .then_inc(taken_ready, 1)
            dve.wait_ge(gap_exp, 1)
            own.chained(dve.tensor_scalar(K.share[:, :, 0], gap[:, :], 1.0, None, ALU.add))
            own.chained(dve.reciprocal(K.share[:, :, 0], K.share[:, :, 0]))
            own.done(dve.tensor_tensor(K.share[:, :, 1], gap[:, :], K.share[:, :, 0], ALU.mult))
            dve.wait_ge(ranked, 2)
            own.chained(dve.tensor_copy(by_tile[:, :, :], psL[1][:, 0:TILES * E].rearrange("p (t e) -> p e t", e=E)))
            flat = lambda x: x[:, :, :].rearrange("p e t -> p (e t)")
            own.chained(dve.tensor_tensor_scan(flat(upto), flat(keep), flat(by_tile), 0.0, ALU.mult, ALU.add))
            own.chained(dve.tensor_scalar(tiles_f[:, :], upto[:, :, TILES - 1], float(P - 1), None, ALU.add))
            own.chained(dve.tensor_copy(tiles_i[:, :], tiles_f[:, :]))
            own.chained(dve.tensor_single_scalar(tiles_i[:, :], tiles_i[:, :], 7, ALU.arith_shift_right))
            own.chained(dve.tensor_copy(tiles_f[:, :], tiles_i[:, :]))
            own.chained(dve.tensor_tensor_scan(ends[:, :], zero8[:, :], tiles_f[:, :], 0.0, ALU.add, ALU.add))
            own.chained(dve.tensor_tensor(tiles_f[:, :], ends[:, :], tiles_f[:, :], ALU.subtract))
            own.chained(dve.tensor_scalar(tiles_f[:, :], tiles_f[:, :], float(P), None, ALU.mult))
            own.chained(dve.tensor_tensor(upto[:, :, :], upto[:, :, :], by_tile[:, :, :], ALU.subtract))
            own.chained(dve.tensor_tensor(place[:, :, :], psL[0][:, 0:TILES * E].rearrange("p (t e) -> p t e", e=E),
                                          upto[:, :, :].rearrange("p e t -> p t e"), ALU.add))
            own.chained(dve.tensor_tensor(place[:, :, :], place[:, :, :],
                                          tiles_f[:, :].rearrange("p (a e) -> p a e", a=1)
                                          .to_broadcast([P, TILES, E]), ALU.add))
            for j in range(2):
                own.chained(dve.tensor_tensor(one_hot[:, j, :, :], one_hot[:, j, :, :], place[:, :, :], ALU.mult))
                own.chained(dve.tensor_reduce(slot_f[:, j, :], one_hot[:, j, :, :], AX.X, ALU.add))
                own.done(dve.tensor_copy(K.slot[:, :, j], slot_f[:, j, :]))
            own.chained(dve.memset(owner[:, :], 0.0))
            for e in range(E - 1):
                own.chained(dve.scalar_tensor_tensor(owner[:, :], K.iota[0:1, 0:OWNERS], ends[0:1, e:e + 1],
                                                     owner[:, :], ALU.is_ge, ALU.add))
            own.chained(dve.tensor_copy(K.owner[:, :], owner[:, :]))


def dispatch(nc, K, norm):
    with ExitStack() as ctx:
        sem = ctx.enter_context(semaphores(nc))
        y = ctx.enter_context(nc.sbuf_tensor("send_y", [P, FLOW, D], F32))
        where = ctx.enter_context(nc.sbuf_tensor("send_where", [P, FLOW, 2], I32))
        y_ready, where_ready, pool_turn = sem("send_y_ready"), sem("where_ready"), sem("send_turn")
        sent = [sem(f"sent{k}") for k in range(FLOW)]
        block = ctx.enter_context(nc.Block())

        @block.vector
        def _(dve):
            with dve.Fori(0, TILES // FLOW) as i:
                for k in range(FLOW):
                    dve.wait_ge(sent[k], i * 32)
                    norm.tile(dve, y[:, k, :], i * FLOW + k).then_inc(y_ready, 1)
                    dve.tensor_scalar(where[:, k, :], at_block(K.slot, i * FLOW + k), 0.0, None, ALU.add) \
                       .then_inc(where_ready, 1)

        @block.gpsimd
        def _(pool):
            with pool.Fori(0, TILES // FLOW) as i:
                for k in range(FLOW):
                    pool.wait_ge(y_ready, i * FLOW + (k + 1))
                    pool.wait_ge(where_ready, i * FLOW + (k + 1))
                    pool.sem_inc(pool_turn, 1)
                    for j in range(2):
                        pool.indirect_dma_start(K.slot_x[:, :],
                                                bass.IndirectOffsetOnAxis(ap=where[:, k, j:j + 1], axis=0),
                                                y[:, k, :], None).then_inc(sent[k], 16)
            for k in range(FLOW):
                pool.wait_ge(sent[k], 32 * (TILES // FLOW))




def experts(nc, K, w1, b1, w2, b2):
    KF = DFF // P
    with ExitStack() as ctx:
        sb = lambda name, shape, dt=F32: ctx.enter_context(nc.sbuf_tensor(name, shape, dt))
        sem = ctx.enter_context(semaphores(nc))
        ps = lambda name: ctx.enter_context(nc.psum_tensor(name, [P, 512], F32))
        w1_sb = sb("experts_w1", [P, EXPERTS * 2, DFF])
        w2_sb = sb("experts_w2", [P, EXPERTS * KF, D])
        b1_sb = sb("experts_b1", [P, EXPERTS * KF])
        b2_sb = sb("experts_b2", [P, EXPERTS, D])
        b1_rows = sb("experts_b1_rows", [EXPERTS * KF, P])
        x = [sb(f"slot_rows{k}", [P, D]) for k in range(UNROLL)]
        xT = [sb(f"slot_rowsT{k}", [P, 2 * P]) for k in range(2)]
        h = [sb(f"hidden{k}", [P, DFF]) for k in range(2)]
        hT = [sb(f"hiddenT{k}", [P, KF * P]) for k in range(2)]
        o = [sb(f"slot_out{k}", [P, D]) for k in range(UNROLL)]
        psX, psH, psHT, psO = ([ps(f"ps_{n}{k}") for k in range(2)] for n in ("rowsT", "hidden", "hiddenT", "out"))
        x_in = [sem(f"slot_in{k}") for k in range(UNROLL)]
        o_out = [sem(f"slot_out{k}") for k in range(UNROLL)]
        xT_turned, xT_ready, h_ready, h_kept, hT_turned, hT_ready, o_ready, o_kept = (sem(n) for n in (
            "xT_turned", "xT_ready", "h_ready", "h_kept", "hT_turned", "hT_ready", "o_ready", "o_kept"))
        turn, weights_in, b1_in, b1_turned, b1_ready = (sem(n) for n in (
            "expert_turn", "weights_in", "b1_in", "b1_turned", "b1_ready"))
        block = ctx.enter_context(nc.Block())
        x_v = K.slot_x.rearrange("(t p) d -> p t d", p=P)
        y_v = K.slot_y.rearrange("(t p) d -> p t d", p=P)
        flat = lambda t: t.rearrange("p (a d) -> p a d", a=1)
        own_list = K.owner[0:1, :]
        STORE_LAG = 5

        @block.sync
        def _(sp):
            def slot(s, k, i):
                if exists(s, SLOT_TILES):
                    seen(sp, xT_turned, s - UNROLL)
                    sp.sem_inc(turn, 1)
                    sp.dma_start(flat(x[k][:, :]), x_v[:, bass.ds(s, 1), :]).then_inc(x_in[k], 16)
                if exists(s - STORE_LAG, SLOT_TILES):
                    seen(sp, o_kept, s - STORE_LAG)
                    sp.sem_inc(turn, 1)
                    ko = (k - STORE_LAG) % UNROLL
                    sp.dma_start(y_v[:, bass.ds(s - STORE_LAG, 1), :], flat(o[ko][:, :])).then_inc(o_out[ko], 16)

            sp.dma_start(b1_rows[:, :], b1.rearrange("e (f p) -> (e f) p", p=P)).then_inc(b1_in, 16)
            sp.dma_start(b2_sb[:, :, :], b2.rearrange("(a e) d -> a e d", a=1).to_broadcast([P, EXPERTS, D])) \
              .then_inc(weights_in, 16)
            for e in range(EXPERTS):
                sp.dma_start(w1_sb[:, 2 * e:2 * e + 2, :], w1[e].rearrange("(j p) f -> p j f", p=P)) \
                  .then_inc(weights_in, 16)
                sp.dma_start(w2_sb[:, KF * e:KF * (e + 1), :], w2[e].rearrange("(j p) f -> p j f", p=P)) \
                  .then_inc(weights_in, 16)
            slots(sp, slot, lag=STORE_LAG, steps=SLOT_TILES)
            for k in range(UNROLL):
                sp.wait_ge(o_out[k], 16 * (SLOT_TILES // UNROLL))

        @block.tensor
        def _(pe):
            owners = Listed(K, pe, own_list, EXPERTS - 1)

            def slot(s, k, i):
                if k == 0:
                    owners.read()
                if exists(s, SLOT_TILES):
                    pe.wait_ge(x_in[k], (i + 1) * 16)
                    seen(pe, xT_ready, s - 2)
                    for j in range(2):
                        tr = pe.transpose(psX[k % 2][:, j * P:(j + 1) * P], x[k][:, j * P:(j + 1) * P],
                                          K.identity[:, :])
                    tr.then_inc(xT_turned, 1)
                if exists(s - 1, SLOT_TILES):
                    e = owners.of(k, 1)
                    q = (k - 1) % 2
                    seen(pe, xT_ready, s - 1)
                    seen(pe, h_kept, s - 3)
                    for j in range(2):
                        mm = pe.matmul(psH[q][:, :], xT[q][:, j * P:(j + 1) * P], at_block(w1_sb, e * 2 + j),
                                       start=(j == 0), stop=(j == 1))
                    mm.then_inc(h_ready, 1)
                if exists(s - 2, SLOT_TILES):
                    q = (k - 2) % 2
                    seen(pe, h_kept, s - 2)
                    seen(pe, hT_ready, s - 4)
                    for j in range(KF):
                        tr = pe.transpose(psHT[q][:, j * P:(j + 1) * P], h[q][:, j * P:(j + 1) * P],
                                          K.identity[:, :])
                    tr.then_inc(hT_turned, 1)
                if exists(s - 3, SLOT_TILES):
                    e = owners.of(k, 3)
                    q = (k - 3) % 2
                    seen(pe, hT_ready, s - 3)
                    seen(pe, o_kept, s - 5)
                    for j in range(KF):
                        mm = pe.matmul(psO[q][:, 0:D], hT[q][:, j * P:(j + 1) * P], at_block(w2_sb, e * KF + j),
                                       start=(j == 0), stop=(j == KF - 1))
                    mm.then_inc(o_ready, 1)
                if k == UNROLL - 1:
                    owners.fetch(i)

            pe.wait_ge(b1_in, 16)
            pe.transpose(psX[0][:, 0:EXPERTS * KF], b1_rows[:, :], K.identity[0:EXPERTS * KF, 0:EXPERTS * KF]) \
              .then_inc(b1_turned, 1)
            pe.wait_ge(weights_in, 16 * (2 * EXPERTS + 1))
            pe.wait_ge(b1_ready, 1)
            slots(pe, slot, lag=3, steps=SLOT_TILES)

        @block.scalar
        def _(act):
            owners = Listed(K, act, own_list, EXPERTS - 1)

            def slot(s, k, i):
                if k == 0:
                    owners.read()
                if exists(s, SLOT_TILES):
                    seen(act, xT_turned, s)
                    seen(act, h_ready, s - 2)
                    act.activation(xT[k % 2][:, :], psX[k % 2][:, 0:2 * P], ACT.Copy).then_inc(xT_ready, 1)
                if exists(s - 2, SLOT_TILES):
                    e = owners.of(k, 2)
                    q = (k - 2) % 2
                    seen(act, hT_turned, s - 2)
                    seen(act, o_ready, s - 4)
                    for j in range(KF):
                        r = act.activation(hT[q][:, j * P:(j + 1) * P], psHT[q][:, j * P:(j + 1) * P], ACT.Relu,
                                           bias=b1_sb[:, bass.ds(e * KF + j, 1)])
                    r.then_inc(hT_ready, 1)
                if k == UNROLL - 1:
                    owners.fetch(i)

            act.wait_ge(b1_turned, 1)
            act.activation(b1_sb[:, :], psX[0][:, 0:EXPERTS * KF], ACT.Copy).then_inc(b1_ready, 1)
            act.wait_ge(b1_ready, 1)
            slots(act, slot, lag=2, steps=SLOT_TILES)

        @block.vector
        def _(dve):
            owners = Listed(K, dve, own_list, EXPERTS - 1)

            def slot(s, k, i):
                if k == 0:
                    owners.read()
                if exists(s - 1, SLOT_TILES):
                    seen(dve, h_ready, s - 1)
                    seen(dve, hT_turned, s - 3)
                    dve.tensor_copy(h[(k - 1) % 2][:, :], psH[(k - 1) % 2][:, :]).then_inc(h_kept, 1)
                if exists(s - 3, SLOT_TILES):
                    ko = (k - 3) % UNROLL
                    seen(dve, o_ready, s - 3)
                    turns = i - (1 if k < 3 else 0)
                    if not isinstance(turns, int) or turns > 0:
                        dve.wait_ge(o_out[ko], turns * 16)
                    dve.tensor_tensor(o[ko][:, :], psO[(k - 3) % 2][:, 0:D], at_block(b2_sb, owners.of(k, 3)),
                                      ALU.add).then_inc(o_kept, 1)
                if k == UNROLL - 1:
                    owners.fetch(i)

            dve.wait_ge(weights_in, 16 * (2 * EXPERTS + 1))
            slots(dve, slot, lag=3, steps=SLOT_TILES)


def combine(nc, K):
    TURNS = TILES // FLOW
    with ExitStack() as ctx:
        sem = ctx.enter_context(semaphores(nc))
        y = ctx.enter_context(nc.sbuf_tensor("fetched", [P, FLOW, 2, D], F32))
        where = ctx.enter_context(nc.sbuf_tensor("fetch_where", [P, FLOW, 2], I32))
        where_ready, pool_turn, half, added = sem("fetch_where_ready"), sem("fetch_turn"), sem("half_added"), sem("added")
        fetched = [sem(f"fetched{k}") for k in range(FLOW)]
        block = ctx.enter_context(nc.Block())

        @block.gpsimd
        def _(pool):
            with pool.Fori(0, TURNS) as i:
                for k in range(FLOW):
                    pool.wait_ge(added, i * FLOW)
                    pool.wait_ge(where_ready, i * FLOW + (k + 1))
                    pool.sem_inc(pool_turn, 1)
                    for j in range(2):
                        pool.indirect_dma_start(y[:, k, j, :], None, K.slot_y[:, :],
                                                bass.IndirectOffsetOnAxis(ap=where[:, k, j:j + 1], axis=0)) \
                            .then_inc(fetched[k], 16)

        @block.vector
        def _(dve):
            with dve.Fori(0, TURNS) as i:
                for k in range(FLOW):
                    dve.wait_ge(fetched[k], i * 32)
                    dve.tensor_scalar(where[:, k, :], at_block(K.slot, i * FLOW + k), 0.0, None, ALU.add) \
                       .then_inc(where_ready, 1)
                for j in range(2):
                    for k in range(FLOW):
                        t = i * FLOW + k
                        if j == 0:
                            dve.wait_ge(fetched[k], (i + 1) * 32)
                        else:
                            dve.wait_ge(half, t + 1)
                        r = at_block(K.R, t)
                        dve.scalar_tensor_tensor(r, y[:, k, j, :], K.share[:, bass.ds(t, 1), j], r,
                                                 ALU.mult, ALU.add).then_inc((half, added)[j], 1)


def second_tables(nc, K, norm, w_forward, w_reverse, attn):
    FS = F1 + H1
    with ExitStack() as ctx:
        sb = lambda name, shape, dt=F32: ctx.enter_context(nc.sbuf_tensor(name, shape, dt))
        sem = ctx.enter_context(semaphores(nc))
        y = sb("t1_y", [P, FLOW, D])
        yT = sb("t1_yT", [P, FLOW, 2 * P])
        w_raw = sb("t1_w_raw", [F1, 2, D])
        attT = sb("t1_attT", [F1, H1])
        w = sb("t1_w", [P, 2, W1C])
        rows = sb("t1_rows", [P, FLOW, W1C])
        psT = [ctx.enter_context(nc.psum_tensor(f"t1_psT{k}", [P, 512], F32)) for k in range(BANKS)]
        psX = [ctx.enter_context(nc.psum_tensor(f"t1_psX{k}", [P, 512], F32)) for k in range(BANKS)]
        vec, w_in, w_turned, w_ready, y_ready, turned, yT_ready, row_ready, row_kept, row_turn = (sem(n) for n in (
            "t1_vec", "t1_w_in", "t1_w_turned", "t1_w_ready", "t1_y_ready", "t1_turned", "t1_yT_ready",
            "t1_row_ready", "t1_row_kept", "t1_row_turn"))
        rows_out = [sem(f"t1_rows_out{k}") for k in range(FLOW)]
        block = ctx.enter_context(nc.Block())
        table_v = K.table1.rearrange("(t p) w -> p t w", p=P)
        TURNS = TILES // FLOW

        @block.sync
        def _(sp):
            for j, v in enumerate((w_forward, w_reverse)):
                sp.dma_start(w_raw[:, j, :], v[:, :]).then_inc(w_in, 16)
            with nc.allow_non_contiguous_dma(reason="256 numbers, once"):
                sp.dma_start(attT[:, :], attn.rearrange("a h f -> f (a h)")).then_inc(w_in, 16)
            with sp.Fori(0, TURNS) as i:
                for k in range(FLOW):
                    sp.wait_ge(row_kept, i * FLOW + (k + 1))
                    sp.sem_inc(row_turn, 1)
                    sp.dma_start(table_v[:, bass.ds(i * FLOW + k, 1), :], rows[:, k:k + 1, :]).then_inc(rows_out[k], 16)
            for k in range(FLOW):
                sp.wait_ge(rows_out[k], 16 * TURNS)

        @block.vector
        def _(dve):
            own = Steps(dve, vec)
            norm.statistics(dve, own)
            with dve.Fori(0, TURNS) as i:
                for k in range(FLOW):
                    dve.wait_ge(turned, i * FLOW)
                    norm.tile(dve, y[:, k, :], i * FLOW + k).then_inc(y_ready, 1)

        @block.tensor
        def _(pe):
            pe.wait_ge(w_in, 48)
            for j in range(2):
                for k in range(2):
                    pe.transpose(psT[k][:, j * FS:j * FS + F1], w_raw[:, j, k * P:(k + 1) * P],
                                 K.identity[0:F1, 0:F1]).then_inc(w_turned, 1)
                    pe.matmul(psT[k][:, j * FS + F1:(j + 1) * FS], w_raw[:, j, k * P:(k + 1) * P], attT[:, :],
                              start=True, stop=True).then_inc(w_turned, 1)
            pe.wait_ge(w_ready, 2)
            with pe.Fori(0, TURNS) as i:
                for k in range(FLOW):
                    pe.wait_ge(y_ready, i * FLOW + (k + 1))
                    pe.wait_ge(yT_ready, i * FLOW + max(0, k + 1 - BANKS))
                    for j in range(2):
                        tr = pe.transpose(psT[k % BANKS][:, j * P:(j + 1) * P], y[:, k, j * P:(j + 1) * P],
                                          K.identity[:, :])
                    tr.then_inc(turned, 1)
                for k in range(FLOW):
                    pe.wait_ge(yT_ready, i * FLOW + (k + 1))
                    pe.wait_ge(row_kept, i * FLOW + max(0, k + 1 - BANKS))
                    for j in range(2):
                        mm = pe.matmul(psX[k % BANKS][:, 0:W1C], yT[:, k, j * P:(j + 1) * P], w[:, j, :],
                                       start=(j == 0), stop=(j == 1))
                    mm.then_inc(row_ready, 1)

        @block.scalar
        def _(act):
            act.wait_ge(w_turned, 8)
            for k in range(2):
                act.activation(w[:, k, :], psT[k][:, 0:W1C], ACT.Copy).then_inc(w_ready, 1)
            norm.roots(act)
            with act.Fori(0, TURNS) as i:
                for k in range(FLOW):
                    act.wait_ge(turned, i * FLOW + (k + 1))
                    act.wait_ge(row_ready, i * FLOW)
                    act.activation(yT[:, k, :], psT[k % BANKS][:, 0:2 * P], ACT.Copy).then_inc(yT_ready, 1)
                for k in range(FLOW):
                    act.wait_ge(row_ready, i * FLOW + (k + 1))
                    act.wait_ge(rows_out[k], i * 16)
                    act.activation(rows[:, k, :], psX[k % BANKS][:, 0:W1C], ACT.Copy).then_inc(row_kept, 1)


def second_edges(nc, K):
    FS = F1 + H1
    with ExitStack() as ctx:
        sb = lambda name, shape, dt=F32: ctx.enter_context(nc.sbuf_tensor(name, shape, dt))
        sem = ctx.enter_context(semaphores(nc))
        pb = lambda name: ctx.enter_context(nc.psum_tensor(name, [P, 512], F32))
        step_data = [sb(f"e1_data{k}", [P, 5 * GT]) for k in range(UNROLL)]
        dst_here = [sb(f"e1_dst{k}", [P, GT]) for k in range(2)]
        rows = [sb(f"e1_rows{k}", [P, GT, W1C]) for k in range(UNROLL)]
        sel = [sb(f"e1_sel{k}", [P, GT, P]) for k in range(UNROLL)]
        both = [sb(f"e1_both{k}", [P, 2 * GT, FS]) for k in range(2)]
        plain = [sb(f"e1_plain{k}", [P, GT, FS]) for k in range(UNROLL)]
        sc = [sb(f"e1_sc{k}", [P, GT, H1]) for k in range(UNROLL)]
        lane_top = [sb(f"e1_lane_top{k}", [P, H1]) for k in range(2)]
        head_top = sb("e1_head_top", [H1, 1])
        diag = [sb(f"e1_diag{k}", [H1, H1]) for k in range(2)]
        z = [sb(f"e1_z{k}", [P, GT, H1]) for k in range(2)]
        drop = [sb(f"e1_drop{k}", [P, H1]) for k in range(2)]
        scale = [sb(f"e1_scale{k}", [P, H1]) for k in range(UNROLL)]
        msg = [sb(f"e1_msg{k}", [P, GT, A1]) for k in range(2)]
        rest = sb("e1_rest", [P, TILES, H1])
        ps_turned = [pb(f"e1_ps_turned{k}") for k in range(2)]
        ps_top = [pb(f"e1_ps_top{k}") for k in range(2)]
        ps_sum = [pb(f"e1_ps_sum{k}") for k in range(2)]
        data_in = [sem(f"e1_data_in{k}") for k in range(UNROLL)]
        gathered = [sem(f"e1_gathered{k}") for k in range(UNROLL)]
        vec, data_wanted, rows_wanted, start, rest_ready, rest_exp = (sem(n) for n in (
            "e1_vec", "e1_data_wanted", "e1_rows_wanted", "e1_start", "e1_rest_ready", "e1_rest_exp"))
        dst_ready, sel_ready, plain_ready, lane_ready, turned, diag_ready, top_ready = (sem("e1_" + n) for n in (
            "dst_ready", "sel_ready", "plain_ready", "lane_ready", "turned", "diag_ready", "top_ready"))
        z_ready, drop_ready, p_ready, scale_ready, msg_ready, sum_ready, acc_ready = (sem("e1_" + n) for n in (
            "z_ready", "drop_ready", "p_ready", "scale_ready", "msg_ready", "sum_ready", "acc_ready"))
        block = ctx.enter_context(nc.Block())
        heads = lambda ap: ap.rearrange("p t (h c) -> p t h c", c=F1 + 1)

        @block.sync
        def _(sp):
            groups = []

            def slot(s, k, i):
                if k == 0:
                    groups[:] = load_list(nc, K, 0, UNROLL + i * UNROLL, UNROLL, GROUPS - 1, ENG.SP)
                edges = sp.snap(groups[k] * (5 * GT), min_val=0, max_val=(GROUPS - 1) * 5 * GT)
                if not isinstance(i, int):
                    sp.wait_ge(gathered[k], i * (16 * GT))
                    sp.sem_inc(data_wanted, 1)
                    for used in (plain_ready, dst_ready):
                        seen(sp, used, s - UNROLL)
                sp.sem_inc(data_wanted, 1)
                sp.dma_start(step_data[k][:, :], K.edges[:, :, :].rearrange("p g c -> p (g c)")
                             [:, bass.ds(edges, 5 * GT)]).then_inc(data_in[k], 16)

            slots(sp, slot)

        @block.gpsimd
        def _(pool):
            def slot(s, k, i):
                pool.wait_ge(data_in[k], (i + 1) * 16)
                seen(pool, plain_ready, s - UNROLL)
                pool.sem_inc(rows_wanted, 1)
                for t in range(GT):
                    pool.indirect_dma_start(
                        rows[k][:, t, :], None, K.table1[:, :],
                        bass.IndirectOffsetOnAxis(ap=step_data[k][:, 2 * GT + t:2 * GT + t + 1].bitcast(I32), axis=0)
                    ).then_inc(gathered[k], 16)

            slots(pool, slot)

        @block.tensor
        def _(pe):
            def slot(s, k, i):
                if exists(s):
                    seen(pe, lane_ready, s)
                    seen(pe, diag_ready, s - 2)
                    pe.transpose(ps_turned[k % 2][0:H1, 0:P], lane_top[k % 2][:, :], K.identity[:, :]) \
                      .then_inc(turned, 1)
                if exists(s - 1):
                    q = (k - 1) % 2
                    seen(pe, diag_ready, s - 1)
                    seen(pe, z_ready, s - 3)
                    pe.matmul(ps_top[q][:, 0:H1], K.ones[0:H1, :], diag[q][:, :], start=True, stop=True) \
                      .then_inc(top_ready, 1)
                if exists(s - 3):
                    q = (k - 3) % 2
                    seen(pe, msg_ready, s - 3)
                    seen(pe, sel_ready, s - 3)
                    seen(pe, acc_ready, s - 5)
                    for t in range(GT):
                        mm = pe.matmul(ps_sum[q][:, 0:A1], sel[(k - 3) % UNROLL][:, t, :], msg[q][:, t, :],
                                       start=(t == 0), stop=(t == GT - 1))
                    mm.then_inc(sum_ready, 1)

            slots(pe, slot, lag=3)

        @block.scalar
        def _(act):
            blocks = Listed(K, act, K.step_list[0:1, 1, UNROLL:], DUMMY)

            def slot(s, k, i):
                if k == 0:
                    blocks.read()
                if exists(s):
                    act.wait_ge(data_in[k], (i + 1) * 16)
                    seen(act, sel_ready, s - 2)
                    act.activation(dst_here[k % 2][:, :], step_data[k][:, 0:GT], ACT.Identity,
                                   bias=K.minus_first[:, bass.ds(blocks.of(k, 0), 1)]).then_inc(dst_ready, 1)
                if exists(s - 2):
                    seen(act, z_ready, s - 2)
                    seen(act, sum_ready, s - 4)
                    act.activation(heads(msg[k % 2][:, :, :])[:, :, :, F1], z[k % 2][:, :, :], ACT.Exp) \
                       .then_inc(p_ready, 1)
                    seen(act, drop_ready, s - 2)
                    seen(act, acc_ready, s - UNROLL)
                    act.activation(scale[(k - 2) % UNROLL][:, :], drop[k % 2][:, :], ACT.Exp).then_inc(scale_ready, 1)
                if k == UNROLL - 1:
                    blocks.fetch(i)

            slots(act, slot, lag=2)
            act.wait_ge(rest_ready, 1)
            act.activation(rest[:, :, :], rest[:, :, :], ACT.Exp).then_inc(rest_exp, 1)

        @block.vector
        def _(dve):
            own = Steps(dve, vec)
            blocks = Listed(K, dve, K.step_list[0:1, 1, UNROLL:], DUMMY)
            own.done(dve.memset(K.acc1[:, :, :], 0.0))
            own.done(dve.memset(K.against[:, :, :], -BIG))
            own.done(dve.memset(K.all_top[:, :], -BIG))
            own.settle()

            def slot(s, k, i):
                if k == 0:
                    if not isinstance(i, int):
                        own.loop(i - 1, PER_ROUND)
                    blocks.read()
                kt, kz, km, ks = ((k - n) % UNROLL for n in (1, 2, 3, 4))
                now, tops, zs, ms, sums = (exists(s - n) for n in range(5))
                against = at_block(K.against, blocks.of(k, 2))
                acc = at_block(K.acc1, blocks.of(k, 4))
                acc_h = acc.rearrange("p (h c) -> p h c", c=F1 + 1)
                own.settle()
                if tops:
                    seen(dve, turned, s - 1)
                    ta = own.done(dve.tensor_reduce(head_top[:, :], ps_turned[kt % 2][0:H1, 0:P], AX.X, ALU.max))
                if now:
                    dve.wait_ge(gathered[k], (i + 1) * (16 * GT))
                    pa = own.done(dve.tensor_tensor(
                        both[k % 2][:, :, :], rows[k][:, :, :].rearrange("p t (j c) -> p (t j) c", j=2),
                        step_data[k][:, 3 * GT:5 * GT].rearrange("p (c a) -> p c a", a=1)
                        .to_broadcast([P, 2 * GT, FS]), ALU.mult))
                if zs:
                    seen(dve, top_ready, s - 2)
                    za = own.done(dve.tensor_tensor(K.all_top[:, :], K.all_top[:, :], ps_top[kz % 2][:, 0:H1], ALU.max))
                if tops:
                    own.until(ta)
                    seen(dve, top_ready, s - 3)
                    dve.tensor_scalar(diag[kt % 2][:, :], K.identity[0:H1, 0:H1], head_top[:, 0:1], None, ALU.mult) \
                       .then_inc(diag_ready, 1)
                if sums:
                    seen(dve, scale_ready, s - 4)
                    seen(dve, acc_ready, s - 5)
                    sa = own.done(dve.tensor_tensor(
                        acc_h, acc_h, scale[ks][:, :].rearrange("p (h a) -> p h a", a=1)
                        .to_broadcast([P, H1, F1 + 1]), ALU.mult))
                if now:
                    own.until(pa)
                    seen(dve, msg_ready, s - UNROLL)
                    halves = both[k % 2][:, :, :].rearrange("p (t j) c -> p t j c", j=2)
                    dve.tensor_tensor(plain[k][:, :, :], halves[:, :, 0, :], halves[:, :, 1, :], ALU.add) \
                       .then_inc(plain_ready, 1)
                if zs:
                    own.until(za)
                    seen(dve, p_ready, s - 4)
                    dve.tensor_tensor(z[kz % 2][:, :, :], sc[kz][:, :, :],
                                      K.all_top[:, :].rearrange("p (a h) -> p a h", a=1).to_broadcast([P, GT, H1]),
                                      ALU.subtract).then_inc(z_ready, 1)
                    seen(dve, scale_ready, s - 4)
                    dve.tensor_tensor(drop[kz % 2][:, :], against, K.all_top[:, :], ALU.subtract) \
                       .then_inc(drop_ready, 1)
                if now:
                    seen(dve, plain_ready, s)
                    seen(dve, z_ready, s - UNROLL)
                    scores = plain[k][:, :, F1:FS]
                    na = own.done(dve.scalar_tensor_tensor(sc[k][:, :, :], scores, 0.2, scores, ALU.mult, ALU.max))
                if sums:
                    own.until(sa)
                    seen(dve, sum_ready, s - 4)
                    dve.tensor_tensor(acc, acc, ps_sum[ks % 2][:, 0:A1], ALU.add).then_inc(acc_ready, 1)
                if now:
                    own.until(na)
                    seen(dve, turned, s - 2)
                    dve.tensor_reduce(lane_top[k % 2][:, :], sc[k][:, :, :].rearrange("p t h -> p h t"), AX.X, ALU.max) \
                       .then_inc(lane_ready, 1)
                if zs:
                    seen(dve, drop_ready, s - 2)
                    own.done(dve.tensor_scalar(against, K.all_top[:, :], 0.0, None, ALU.add))
                if ms:
                    seen(dve, p_ready, s - 3)
                    dve.tensor_tensor(
                        heads(msg[km % 2][:, :, :])[:, :, :, 0:F1],
                        plain[km][:, :, 0:F1].rearrange("p t (a f) -> p t a f", a=1).to_broadcast([P, GT, H1, F1]),
                        heads(msg[km % 2][:, :, :])[:, :, :, F1:F1 + 1].to_broadcast([P, GT, H1, F1]),
                        ALU.mult).then_inc(msg_ready, 1)
                if now:
                    seen(dve, sum_ready, s - UNROLL)
                    seen(dve, dst_ready, s)
                    dve.tensor_tensor(
                        sel[k][:, :, :],
                        dst_here[k % 2][:, :].rearrange("p (t a) -> p t a", a=1).to_broadcast([P, GT, P]),
                        K.iota[:, 0:P].rearrange("p (a n) -> p a n", a=1).to_broadcast([P, GT, P]),
                        ALU.is_equal).then_inc(sel_ready, 1)
                if k == UNROLL - 1:
                    blocks.fetch(i)

            PER_ROUND = UNROLL * 6
            slots(dve, slot, lag=4, after_loop=lambda: own.left(STEPS // UNROLL - 1))
            own.settle()
            dve.wait_ge(acc_ready, STEPS)
            dve.wait_ge(drop_ready, STEPS)
            own.chained(dve.tensor_tensor(rest[:, :, :], K.all_top[:, :].rearrange("p (a h) -> p a h", a=1)
                                          .to_broadcast([P, TILES, H1]), K.against[:, :, :], ALU.subtract))
            dve.tensor_scalar(rest[:, :, :], rest[:, :, :], 2 * SAFE, None, ALU.min).then_inc(rest_ready, 1)
            dve.wait_ge(rest_exp, 1)
            all_h = K.acc1[:, :, :].rearrange("p t (h c) -> p t h c", c=F1 + 1)
            weight = all_h[:, :, :, F1]
            own.chained(dve.scalar_tensor_tensor(weight, rest[:, :, :], 1e-10, weight, ALU.mult, ALU.add))
            own.chained(dve.reciprocal(weight, weight))
            by_head = K.acc1[:, :, :].rearrange("p t (h c) -> p (t h) c", c=F1 + 1)
            own.chained(dve.tensor_tensor(by_head[:, :, 0:F1], by_head[:, :, 0:F1],
                                          by_head[:, :, F1:F1 + 1].to_broadcast([P, TILES * H1, F1]), ALU.mult))
            r = K.R[:, :, :].rearrange("p t (h c) -> p (t h) c", c=F1)
            own.chained(dve.tensor_tensor(r, r, by_head[:, :, 0:F1], ALU.add))


def route(nc, K, norm, wr, br):
    E = EXPERTS
    TAIL = N_NODES - (BLOCKS - 1) * P
    CAPACITY = float(-(-N_NODES * 5 // (4 * EXPERTS)))
    with ExitStack() as ctx:
        sb = lambda name, shape, dt=F32: ctx.enter_context(nc.sbuf_tensor(name, shape, dt))
        sem = ctx.enter_context(semaphores(nc))
        tail = sb("r_tail", [P, 1])
        wr_sb = sb("r_wr", [P, 2, E])
        br_sb = sb("r_br", [P, E])
        mean = sb("r_mean", [P, 2])
        spread = sb("r_spread", [P, 2, P])
        q = sb("r_q", [P, E])
        load = sb("r_load", [P, E])
        over = sb("r_over", [P, E])
        top = sb("r_top", [P, 1])
        total = sb("r_total", [P, 1])
        best = sb("r_best", [P, 8])
        best_i = sb("r_best_i", [P, 8], mybir.dt.uint32)
        ps_mean = [ctx.enter_context(nc.psum_tensor(f"r_ps_mean{j}", [P, 512], F32)) for j in range(2)]
        ps_logit = ctx.enter_context(nc.psum_tensor("r_ps_logit", [P, 512], F32))
        psT = [ctx.enter_context(nc.psum_tensor(f"r_psT{k}", [P, 512], F32)) for k in range(BANKS)]
        turned, yT_ready = sem("r_turned"), sem("r_yT_ready")
        w_in, vec, y_ready, tail_ready, summed, spread_ready, logit_ready, exp_wanted, exp_ready = (sem(n) for n in (
            "r_w_in", "r_vec", "r_y_ready", "r_tail_ready", "r_summed", "r_spread_ready", "r_logit_ready",
            "r_exp_wanted", "r_exp_ready"))
        block = ctx.enter_context(nc.Block())

        @block.sync
        def _(sp):
            for k in range(2):
                sp.dma_start(wr_sb[:, k, :], wr[k * P:(k + 1) * P, :]).then_inc(w_in, 16)
            sp.dma_start(br_sb[:, :], br.rearrange("(a n) -> a n", a=1).to_broadcast([P, E])).then_inc(w_in, 16)

        @block.gpsimd
        def _(pool):
            pool.affine_select(out=tail[:, :], in_=K.ones[:, 0:1], compare_op=ALU.is_ge, fill=0.0,
                               base=TAIL - 1, pattern=[[0, 1]], channel_multiplier=-1).then_inc(tail_ready, 1)

        @block.tensor
        def _(pe):
            pe.wait_ge(tail_ready, 1)
            for t in range(TILES):
                pe.wait_ge(y_ready, t + 1)
                for j in range(2):
                    if t < BLOCKS:
                        mm = pe.matmul(ps_mean[j][:, 0:1], K.Y[:, t, j * P:(j + 1) * P],
                                       (tail if t == BLOCKS - 1 else K.ones)[:, 0:1],
                                       start=(t == 0), stop=(t == BLOCKS - 1))
                if t == BLOCKS - 1:
                    mm.then_inc(summed, 1)
                if t >= BANKS:
                    pe.wait_ge(yT_ready, t + 1 - BANKS)
                for j in range(2):
                    tr = pe.transpose(psT[t % BANKS][:, j * P:(j + 1) * P], K.Y[:, t, j * P:(j + 1) * P],
                                      K.identity[:, :])
                tr.then_inc(turned, 1)
            pe.wait_ge(w_in, 48)
            pe.wait_ge(spread_ready, 2)
            for j in range(2):
                mm = pe.matmul(ps_logit[:, 0:E], spread[:, j, :], wr_sb[:, j, :], start=(j == 0), stop=(j == 1))
            mm.then_inc(logit_ready, 1)

        @block.scalar
        def _(act):
            norm.roots(act)
            for t in range(TILES):
                act.wait_ge(turned, t + 1)
                act.activation(K.YT[:, :, t * P:(t + 1) * P],
                               psT[t % BANKS][:, 0:2 * P].rearrange("p (j e) -> p j e", j=2), ACT.Copy) \
                   .then_inc(yT_ready, 1)
            for n in range(2):
                act.wait_ge(exp_wanted, n + 1)
                act.activation(q[:, :], q[:, :], ACT.Exp).then_inc(exp_ready, 1)
            act.wait_ge(exp_wanted, 3)
            act.activation(K.pair[:, 1:2], K.pair[:, 1:2], ACT.Exp).then_inc(exp_ready, 1)

        @block.vector
        def _(dve):
            own = Steps(dve, vec)
            norm.statistics(dve, own)
            for t in range(TILES):
                norm.tile(dve, K.Y[:, t, :], t).then_inc(y_ready, 1)
            dve.wait_ge(summed, 1)
            for j in range(2):
                own.done(dve.tensor_scalar(mean[:, j:j + 1], ps_mean[j][:, 0:1], 1.0 / N_NODES, None, ALU.mult))
            own.settle()
            for j in range(2):
                dve.tensor_scalar(spread[:, j, :], K.ones[:, :], mean[:, j:j + 1], None, ALU.mult) \
                   .then_inc(spread_ready, 1)
            dve.wait_ge(w_in, 48)
            dve.wait_ge(logit_ready, 1)
            own.chained(dve.tensor_tensor(q[:, :], ps_logit[:, 0:E], br_sb[:, :], ALU.add))
            for n in range(2):
                own.chained(dve.tensor_reduce(top[:, :], q[:, :], AX.X, ALU.max))
                dve.tensor_scalar(q[:, :], q[:, :], top[:, 0:1], None, ALU.subtract).then_inc(exp_wanted, 1)
                dve.wait_ge(exp_ready, n + 1)
                own.chained(dve.tensor_reduce(total[:, :], q[:, :], AX.X, ALU.add))
                own.chained(dve.reciprocal(total[:, :], total[:, :]))
                own.chained(dve.tensor_scalar(q[:, :], q[:, :], total[:, 0:1], None, ALU.mult))
                if n == 0:
                    own.chained(dve.tensor_scalar(load[:, :], q[:, :], float(N_NODES), None, ALU.mult))
                    own.done(dve.tensor_scalar(over[:, :], load[:, :], CAPACITY, None, ALU.is_gt))
                    own.chained(dve.tensor_scalar(load[:, :], load[:, :], CAPACITY, None, ALU.max))
                    own.chained(dve.reciprocal(load[:, :], load[:, :]))
                    own.chained(dve.tensor_scalar(load[:, :], load[:, :], CAPACITY, -1.0, ALU.mult, ALU.add))
                    own.chained(dve.tensor_tensor(load[:, :], load[:, :], over[:, :], ALU.mult))
                    own.chained(dve.tensor_scalar(load[:, :], load[:, :], 1.0, None, ALU.add))
                    own.chained(dve.tensor_tensor(q[:, :], q[:, :], load[:, :], ALU.mult))
            own.chained(dve.max(best[:, :], q[:, :]))
            own.chained(dve.max_index(best_i[:, :], best[:, :], q[:, :]))
            own.done(dve.tensor_copy(K.chosen[:, :], best_i[0:1, 0:2]))
            dve.tensor_tensor(K.pair[:, 1:2], best[:, 1:2], best[:, 0:1], ALU.subtract).then_inc(exp_wanted, 1)
            dve.wait_ge(exp_ready, 3)
            own.chained(dve.tensor_scalar(K.pair[:, 0:1], K.pair[:, 1:2], 1.0, None, ALU.add))
            own.chained(dve.reciprocal(K.pair[:, 0:1], K.pair[:, 0:1]))
            own.chained(dve.tensor_tensor(K.pair[:, 1:2], K.pair[:, 1:2], K.pair[:, 0:1], ALU.mult))


def last_experts(nc, K, w1, b1, w2, b2, beta):
    KF = DFF // P
    PAIR = 2
    HT = 2 * KF
    HB = 4
    TURNS = TILES // PAIR
    assert TURNS % 2 == 1
    CH = 10
    with ExitStack() as ctx:
        sb = lambda name, shape, dt=F32: ctx.enter_context(nc.sbuf_tensor(name, shape, dt))
        sem = ctx.enter_context(semaphores(nc))
        ps = lambda name: ctx.enter_context(nc.psum_tensor(name, [P, 512], F32))
        w1_sb = sb("l_w1", [P, 2 * 2, DFF])
        w2_sb = sb("l_w2", [P, HT, D])
        b1_rows = sb("l_b1_rows", [HT, P])
        b1_sb = sb("l_b1", [P, HT])
        b2_sb = sb("l_b2", [P, 2, D])
        beta_sb = sb("l_beta", [P, 1, D])
        stats = sb("l_stats", [P, PAIR, 6])
        hT = [sb(f"l_hT{n}", [P, HT, PAIR * P]) for n in range(2)]
        psY = ps("l_psY")
        psH = [ps(f"l_psH{n}") for n in range(HB)]
        psO = [ps(f"l_psO{a}") for a in range(PAIR)]
        weights_in, rows_in, beta_in, vec, b1_turned, b1_ready, w2_ready, beta_added = (sem("l_" + n) for n in (
            "weights_in", "rows_in", "beta_in", "vec", "b1_turned", "b1_ready", "w2_ready", "beta_added"))
        stats_turn = sem("l_stats_turn")
        hidden, hT_ready, out_ready, z_ready = (sem("l_" + n) for n in (
            "hidden", "hT_ready", "out_ready", "z_ready"))
        block = ctx.enter_context(nc.Block())

        def turns(eng, turn):
            turn(0, 0)
            with eng.Fori(0, TURNS // 2) as r:
                turn(r * 2 + 1, 1)
                turn(r * 2 + 2, 0)

        @block.sync
        def _(sp):
            _, e = nc.values_load_multi_w_load_instructions(K.chosen[0:1, 0:2], engines=(ENG.SP,), min_val=0,
                                                            max_val=EXPERTS - 1)
            for n in range(2):
                sp.dma_start(b1_rows[n * KF:(n + 1) * KF, :],
                             b1.rearrange("e (f p) -> e f p", p=P)[bass.ds(e[n], 1), :, :]
                             .rearrange("e f p -> (e f) p")).then_inc(rows_in, 16)
                sp.dma_start(b2_sb[:, n, :], b2[bass.ds(e[n], 1), :].to_broadcast([P, D])).then_inc(rows_in, 16)
                sp.dma_start(w1_sb[:, 2 * n:2 * n + 2, :],
                             w1[bass.ds(e[n], 1), :, :].rearrange("e (j p) f -> p (e j) f", p=P)) \
                  .then_inc(weights_in, 16)
                sp.dma_start(w2_sb[:, KF * n:KF * (n + 1), :],
                             w2[bass.ds(e[n], 1), :, :].rearrange("e (j p) f -> p (e j) f", p=P)) \
                  .then_inc(weights_in, 16)
            sp.dma_start(beta_sb[:, 0, :], beta.rearrange("(a n) -> a n", a=1).to_broadcast([P, D])).then_inc(beta_in, 16)

        @block.gpsimd
        def _(pool):
            pool.wait_ge(beta_in, 16)
            for c in range(TILES // CH):
                r = K.R[:, c * CH:(c + 1) * CH, :]
                pool.tensor_tensor(r, r, beta_sb[:, :, :].to_broadcast([P, CH, D]), ALU.add).then_inc(beta_added, 1)
            pool.wait_ge(beta_added, TILES // CH)

        @block.tensor
        def _(pe):
            def give(i, n):
                pe.wait_ge(hT_ready, i * HT + HT)
                pe.wait_ge(z_ready, i * PAIR)
                for a in range(PAIR):
                    for m in range(HT):
                        mm = pe.matmul(psO[a][:, 0:D], hT[n][:, m, a * P:(a + 1) * P], w2_sb[:, m, :],
                                       start=(m == 0), stop=(m == HT - 1))
                    mm.then_inc(out_ready, 1)

            def turn(i, n):
                for m in range(HT):
                    if m >= HB or not isinstance(i, int):
                        pe.wait_ge(hT_ready, i * HT + (m + 1 - HB))
                    for j in range(2):
                        mm = pe.matmul(psH[m % HB][:, 0:PAIR * P],
                                       w1_sb[:, (m // KF) * 2 + j, (m % KF) * P:(m % KF + 1) * P],
                                       K.YT[:, j, bass.ds(i * (PAIR * P), PAIR * P)],
                                       start=(j == 0), stop=(j == 1))
                    mm.then_inc(hidden, 1)
                if not isinstance(i, int):
                    give(i - 1, 1 - n)

            pe.wait_ge(rows_in, 64)
            pe.transpose(psY[:, 0:HT], b1_rows[:, :], K.identity[0:HT, 0:HT]).then_inc(b1_turned, 1)
            pe.wait_ge(weights_in, 64)
            pe.wait_ge(b1_ready, 1)
            pe.wait_ge(w2_ready, 1)
            turns(pe, turn)
            give(TURNS - 1, 0)

        @block.scalar
        def _(act):
            def turn(i, n):
                if not isinstance(i, int):
                    act.wait_ge(out_ready, (i - 1) * PAIR)
                for m in range(HT):
                    act.wait_ge(hidden, i * HT + (m + 1))
                    act.activation(hT[n][:, m, :], psH[m % HB][:, 0:PAIR * P], ACT.Gelu, bias=b1_sb[:, m:m + 1]) \
                       .then_inc(hT_ready, 1)

            act.wait_ge(b1_turned, 1)
            act.activation(b1_sb[:, :], psY[:, 0:HT], ACT.Copy).then_inc(b1_ready, 1)
            act.wait_ge(b1_ready, 1)
            turns(act, turn)

        @block.vector
        def _(dve):
            own = Steps(dve, vec)
            dve.wait_ge(weights_in, 64)
            dve.wait_ge(rows_in, 64)
            for n in range(2):
                w = w2_sb[:, n * KF:(n + 1) * KF, :]
                own.done(dve.tensor_scalar(w, w, K.pair[:, n:n + 1], None, ALU.mult))
            own.chained(dve.tensor_scalar(b2_sb[:, 1, :], b2_sb[:, 1, :], K.pair[:, 1:2], None, ALU.mult))
            own.chained(dve.scalar_tensor_tensor(b2_sb[:, 0, :], b2_sb[:, 0, :], K.pair[:, 0:1], b2_sb[:, 1, :],
                                                 ALU.mult, ALU.add))
            dve.sem_inc(w2_ready, 1)

            def turn(i, n):
                for a in range(PAIR):
                    y = at_block(K.Y, i * PAIR + a)
                    own.done(dve.tensor_tensor(y, y, b2_sb[:, 0, :], ALU.add))
                own.settle()
                for a in range(PAIR):
                    y = at_block(K.Y, i * PAIR + a)
                    dve.wait_ge(out_ready, i * PAIR + (a + 1))
                    dve.tensor_tensor(y, y, psO[a][:, 0:D], ALU.add).then_inc(z_ready, 1)
                for a in range(PAIR):
                    dve.wait_ge(z_ready, i * PAIR + (a + 1))
                    dve.sem_inc(stats_turn, 1)
                    own.done(dve.bn_stats(stats[:, a, :], at_block(K.Y, i * PAIR + a)))
                own.settle()
                for a in range(PAIR):
                    own.done(dve.tensor_scalar(at_block(K.stats, i * PAIR + a), stats[:, a, :], 0.0, None, ALU.add))
                own.settle()

            PER_ROUND = 2 * 3 * PAIR
            turn(0, 0)
            with dve.Fori(0, TURNS // 2) as r:
                own.loop(r, PER_ROUND)
                turn(r * 2 + 1, 1)
                turn(r * 2 + 2, 0)
            own.left(TURNS // 2)


def finish(nc, K, gamma, out_rows):
    CH = 5
    with ExitStack() as ctx:
        sem = ctx.enter_context(semaphores(nc))
        g = ctx.enter_context(nc.sbuf_tensor("f_gamma", [P, 1, D], F32))
        minus = ctx.enter_context(nc.sbuf_tensor("f_minus", [P, TILES], F32))
        gamma_in, vec, var_ready, root_ready, norm_ready, z_ready, scaled, added, out_done = (sem("f_" + n) for n in (
            "gamma_in", "vec", "var_ready", "root_ready", "norm_ready", "z_ready", "scaled", "added", "out_done"))
        block = ctx.enter_context(nc.Block())

        @block.sync
        def _(sp):
            sp.dma_start(g[:, 0, :], gamma.rearrange("(a n) -> a n", a=1).to_broadcast([P, D])).then_inc(gamma_in, 16)
            for c in range(TILES // CH):
                sp.wait_ge(added, c + 1)
                sp.dma_start(out_rows.rearrange("(t p) d -> p t d", p=P)[:, c * CH:(c + 1) * CH, :],
                             K.Y[:, c * CH:(c + 1) * CH, :]).then_inc(out_done, 16)
            sp.wait_ge(out_done, 16 * (TILES // CH))

        @block.scalar
        def _(act):
            act.wait_ge(var_ready, 1)
            act.activation(K.mean_var[:, :, 1], K.mean_var[:, :, 1], ACT.Sqrt).then_inc(root_ready, 1)
            act.wait_ge(norm_ready, 1)
            for t in range(TILES):
                act.activation(K.Y[:, t, :], K.Y[:, t, :], ACT.Identity, bias=minus[:, t:t + 1],
                               scale=K.mean_var[:, t, 1:2]).then_inc(z_ready, 1)

        @block.vector
        def _(dve):
            own = Steps(dve, vec)
            for t in range(TILES):
                own.done(dve.bn_aggr(K.mean_var[:, t, :], K.stats[:, t, :]))
            own.settle()
            var = K.mean_var[:, :, 1]
            dve.tensor_scalar(var, var, LN_EPS, None, ALU.add).then_inc(var_ready, 1)
            dve.wait_ge(root_ready, 1)
            own.chained(dve.reciprocal(var, var))
            own.chained(dve.tensor_tensor(minus[:, :], K.mean_var[:, :, 0], var, ALU.mult))
            dve.tensor_scalar(minus[:, :], minus[:, :], -1.0, None, ALU.mult).then_inc(norm_ready, 1)
            dve.wait_ge(gamma_in, 16)
            for c in range(TILES // CH):
                dve.wait_ge(z_ready, (c + 1) * CH)
                y = K.Y[:, c * CH:(c + 1) * CH, :]
                dve.tensor_tensor(y, y, g[:, :, :].to_broadcast([P, CH, D]), ALU.mult).then_inc(scaled, 1)
                dve.wait_ge(scaled, c + 1)
                dve.tensor_tensor(y, y, K.R[:, c * CH:(c + 1) * CH, :], ALU.add).then_inc(added, 1)


class Kept:
    pass


def program(nc, a, out):
    K = Kept()
    K.registers = {}
    with ExitStack() as ctx:
        sb = lambda name, shape, dt=F32: ctx.enter_context(nc.sbuf_tensor(name, shape, dt))
        dram = lambda name, shape, dt=F32: nc.dram_tensor(name, shape, dt, kind="Internal").ap()
        K.table0 = dram("table0", [N_PAD, W0])
        K.table1 = dram("table1", [N_PAD, W1C])
        K.fresh_dram = dram("fresh_marks", [EDGE_TILES, H0, P])
        K.list_dram = dram("step_list_dram", [2, HALVES * P], I32)
        K.slot_x = dram("slot_x", [SLOT_TILES * P, D])
        K.slot_y = dram("slot_y", [SLOT_TILES * P, D])
        K.R = sb("R", [P, TILES, D])
        K.identity = sb("identity", [P, P])
        K.ones = sb("ones", [P, P])
        K.identity_b = sb("identity_b", [P, P], BF16)
        K.ones_b = sb("ones_b", [P, P], BF16)
        K.iota = sb("iota", [P, 2 * P])
        with ExitStack() as edges:
            sb = lambda name, shape, dt=F32: edges.enter_context(nc.sbuf_tensor(name, shape, dt))
            K.minus_first = sb("minus_first", [P, TILES])
            K.edges = sb("edges", [P, GROUPS, 5 * GT])
            K.step_list = sb("step_list", [1, 2, 2 * UNROLL + HALVES * P], I32)
            with ExitStack() as early:
                K.iota_i = early.enter_context(nc.sbuf_tensor("iota_i", [P, 2 * P], I32))
                K.step_seed = early.enter_context(nc.sbuf_tensor("step_seed", [P, HALVES], I32))
                edge_lists(nc, K, a["dst"], a["src"], a["edge_attr_2"])
            with ExitStack() as first:
                sb = lambda name, shape, dt=F32: first.enter_context(nc.sbuf_tensor(name, shape, dt))
                K.acc = sb("acc", [P, TILES, W0])
                with ExitStack() as scores:
                    sb = lambda name, shape, dt=F32: scores.enter_context(nc.sbuf_tensor(name, shape, dt))
                    K.top_src = sb("top_src", [P, TILES, H0])
                    K.sc_dst = sb("sc_dst", [P, TILES, H0])
                    K.low_dst = sb("low_dst", [P, TILES, H0])
                    K.dst_parts = sb("dst_parts", [P, TILES, 3 * H0], BF16)
                    K.shift = sb("shift", [P, TILES, H0], BF16)
                    K.low_row = sb("low_row", [P, GT, H0])
                    first_tables(nc, K, a["x"].rearrange("(t p) d -> p t d", p=P), a["L0_gnn_W"],
                                 a["L0_gnn_att_src"], a["L0_gnn_att_dst"])
                    first_edges(nc, K)
                batch_norm(nc, K, a["L0_gnn_bias"], a["L0_gnn_gamma"], a["L0_gnn_beta"])
            with ExitStack() as ffn:
                sb = lambda name, shape, dt=F32: ffn.enter_context(nc.sbuf_tensor(name, shape, dt))
                K.share = sb("share", [P, TILES, 2])
                K.slot = sb("slot", [P, TILES, 2], I32)
                K.owner = sb("owner", [1, OWNERS], I32)
                with ExitStack() as part:
                    norm = Normalised(nc, part, "ffn0", K.R)
                    gate(nc, K, norm, a["L0_ffn_Wg"], a["L0_ffn_bg"], a["L0_ffn_bias"])
                    dispatch(nc, K, norm)
                experts(nc, K, a["L0_ffn_W1"], a["L0_ffn_b1"], a["L0_ffn_W2"], a["L0_ffn_b2"])
                combine(nc, K)
            with ExitStack() as part:
                norm = Normalised(nc, part, "gnn1", K.R)
                second_tables(nc, K, norm, a["L1_gnn_W_forward"], a["L1_gnn_W_reverse"], a["L1_gnn_attn_forward"])
            with ExitStack() as second:
                sb = lambda name, shape, dt=F32: second.enter_context(nc.sbuf_tensor(name, shape, dt))
                K.acc1 = sb("acc1", [P, TILES, A1])
                K.against = sb("against", [P, TILES, H1])
                K.all_top = sb("all_top", [P, H1])
                second_edges(nc, K)
        K.Y = ctx.enter_context(nc.sbuf_tensor("Y", [P, TILES, D], F32))
        K.YT = ctx.enter_context(nc.sbuf_tensor("YT", [P, 2, N_PAD], F32))
        K.pair = ctx.enter_context(nc.sbuf_tensor("pair", [P, 2], F32))
        K.chosen = ctx.enter_context(nc.sbuf_tensor("chosen", [1, 2], I32))
        K.stats = ctx.enter_context(nc.sbuf_tensor("stats", [P, TILES, 6], F32))
        K.mean_var = ctx.enter_context(nc.sbuf_tensor("mean_var", [P, TILES, 2], F32))
        with ExitStack() as part:
            norm = Normalised(nc, part, "ffn1", K.R)
            route(nc, K, norm, a["L1_ffn_Wr"], a["L1_ffn_br"])
        last_experts(nc, K, a["L1_ffn_W1"], a["L1_ffn_b1"], a["L1_ffn_W2"], a["L1_ffn_b2"], a["L1_ffn_beta"])
        finish(nc, K, a["L1_ffn_gamma"], out)


_INS = ['x', 'src', 'dst', 'edge_attr_2', 'L0_gnn_W', 'L0_gnn_att_src', 'L0_gnn_att_dst', 'L0_gnn_bias',
        'L0_gnn_gamma', 'L0_gnn_beta', 'L0_ffn_Wg', 'L0_ffn_bg', 'L0_ffn_bias', 'L0_ffn_W1', 'L0_ffn_b1',
        'L0_ffn_W2', 'L0_ffn_b2', 'L1_gnn_W_forward', 'L1_gnn_W_reverse', 'L1_gnn_attn_forward', 'L1_ffn_Wr',
        'L1_ffn_br', 'L1_ffn_W1', 'L1_ffn_b1', 'L1_ffn_W2', 'L1_ffn_b2', 'L1_ffn_gamma', 'L1_ffn_beta']


def kernel(**inputs):
    import numpy as _np
    import concourse.bacc as _bacc
    from concourse import mybir as _mybir
    from concourse.bass_utils import run_bass_kernel_spmd as _run

    def padded(a, rows, **how):
        return _np.pad(a, [(0, rows - a.shape[0])] + [(0, 0)] * (a.ndim - 1), **how)

    laid = {k: _np.asarray(v) for k, v in inputs.items()}
    laid['x'] = padded(laid['x'], N_PAD)
    laid['src'] = padded(laid['src'], E_PAD, mode='edge').reshape(EDGE_ROWS, ROW_EDGES)
    laid['dst'] = padded(laid['dst'], E_PAD, constant_values=PAD_DST).reshape(EDGE_ROWS, ROW_EDGES)
    laid['edge_attr_2'] = padded(laid['edge_attr_2'], E_PAD, mode='edge').reshape(EDGE_ROWS, ROW_EDGES, 2)

    nc = _bacc.Bacc("TRN2", target_bir_lowering=False, num_devices=1)
    arrays, args = {}, {}
    for name in _INS:
        a = _np.ascontiguousarray(laid[name])
        arrays[f"in_{name}_dram"] = a
        args[name] = nc.dram_tensor(f"in_{name}_dram", a.shape, _mybir.dt.from_np(a.dtype), kind="ExternalInput").ap()
    out = nc.dram_tensor("out_0_dram", (N_PAD, D), _mybir.dt.float32, kind="ExternalOutput").ap()
    program(nc, args, out)
    r = _run(nc, [arrays], core_ids=[0])
    return r.results[0]["out_0_dram"][:N_NODES]
```

```python
from contextlib import ExitStack, contextmanager

import concourse.bass as bass
from concourse import mybir

F32 = mybir.dt.float32
I32 = mybir.dt.int32
BF16 = mybir.dt.bfloat16
ALU = mybir.AluOpType
ACT = mybir.ActivationFunctionType
AX = mybir.AxisListType
ENG = mybir.EngineType

P = 128
N_NODES = 6250
N_EDGES = 100000
D = 256
TILES = 50
N_PAD = TILES * P
GROUP = 512
GT = GROUP // P
ROW_EDGES = 1024
EDGE_ROWS = -(-N_EDGES // ROW_EDGES)
E_PAD = EDGE_ROWS * ROW_EDGES
GROUPS = E_PAD // GROUP
CHUNKS = ROW_EDGES // P
EDGE_TILES = E_PAD // P
BLOCKS = -(-N_NODES // P)
PAD_DST = BLOCKS * P - 1
DUMMY = BLOCKS
UNROLL = 6
STEPS = GROUPS + BLOCKS - 1
HALVES = -(-STEPS // P)
H0, DH0 = 8, 32
W0 = H0 * (DH0 + 1)
H1, F1 = 4, 64
W1C = 2 * (F1 + H1)
A1 = H1 * (F1 + 1)
EXPERTS, DFF = 8, 512
BIG = 1e30
SAFE = 40.0
LN_EPS = 1e-5
FLOW = 5
BANKS = 4
SLOT_TILES = (2 * N_PAD + EXPERTS * (P - 1)) // P
SLOT_TILES += -SLOT_TILES % UNROLL
OWNERS = SLOT_TILES + UNROLL


class Steps:

    def __init__(self, eng, sem):
        self.eng, self.sem, self.base, self.count = eng, sem, 0, 0

    def done(self, ins):
        ins.then_inc(self.sem, 1)
        self.count += 1
        return self.base + self.count

    def until(self, value):
        self.eng.wait_ge(self.sem, value)

    def settle(self):
        self.eng.wait_ge(self.sem, self.base + self.count)

    def chained(self, ins):
        self.done(ins)
        self.settle()

    def loop(self, i, per):
        self.start, self.per = self.base + self.count, per
        self.base, self.count = self.start + i * per, 0

    def left(self, turns):
        assert self.count == self.per, (self.count, self.per)
        self.base, self.count = self.start + turns * self.per, 0


def after(i, n):
    return not isinstance(i, int) or i > n


def rounds(eng, turn, count=TILES // FLOW):
    turn(0)
    with eng.Fori(1, count) as i:
        turn(i)


def free(eng, sem, i, k, places=FLOW):
    before = [j for j in range(k) if j % places == k % places]
    if before:
        eng.wait_ge(sem, i * FLOW + (before[-1] + 1))
    elif after(i, 0):
        last = max(j for j in range(FLOW) if j % places == k % places)
        eng.wait_ge(sem, (i - 1) * FLOW + (last + 1))


@contextmanager
def semaphores(nc):
    held = []

    def take(name):
        held.append(nc.alloc_semaphore(name=name))
        return held[-1]

    yield take
    nc.clear_and_free_semaphores(held)
    nc.all_engine_barrier()


def load_nodes(sp, K, x_tiles, chunks):
    ch = TILES // len(K.x_in)
    for c in chunks:
        sp.dma_start(K.R[:, c * ch:(c + 1) * ch, :], x_tiles[:, c * ch:(c + 1) * ch, :]).then_inc(K.x_in[c], 16)


def edge_lists(nc, K, x_tiles, dst_rows, src_rows, attr_rows):
    with ExitStack() as ctx:
        sb = lambda name, shape, dt=F32: ctx.enter_context(nc.sbuf_tensor(name, shape, dt))
        sem = ctx.enter_context(semaphores(nc))
        dst_i = sb("dst_i", [EDGE_ROWS, ROW_EDGES], I32)
        src_i = sb("src_i", [EDGE_ROWS, ROW_EDGES], I32)
        rows = sb("edge_row_data", [EDGE_ROWS, 3, ROW_EDGES])
        attr = sb("attr_rows", [EDGE_ROWS, ROW_EDGES, 2])
        fresh = sb("fresh_rows", [EDGE_ROWS, ROW_EDGES])
        ends_i = sb("group_ends_i", [1, 2, GROUPS], I32)
        ends_b = sb("group_ends_block", [1, 2, GROUPS], I32)
        ends = sb("group_ends", [1, 2, GROUPS])
        count = sb("steps_of_group", [1, GROUPS])
        lines = sb("step_lines", [1, 2, GROUPS])
        zeros = sb("zeros_row", [1, GROUPS])
        step_no = sb("step_no", [P, HALVES])
        group_no = sb("group_no", [P, GROUPS])
        below = sb("groups_below", [P, HALVES, GROUPS])
        step_g = sb("step_g", [P, HALVES])
        step_b = sb("step_b", [P, HALVES])
        late = sb("step_late", [P, HALVES])
        step_i = sb("step_i", [P, 2, HALVES], I32)
        ps = ctx.enter_context(nc.psum_tensor("edge_turned", [P, 2, CHUNKS, P], F32))
        ps_lines = ctx.enter_context(nc.psum_tensor("lines_everywhere", [P, 2, GROUPS], F32))
        dst_in, src_in, attr_in, ends_in = sem("dst_in"), sem("src_in"), sem("attr_in"), sem("ends_in")
        numbers, vec = sem("numbers"), sem("edge_vec")
        rows_ready, turned, kept = sem("rows_ready"), sem("turned"), sem("edge_kept")
        fresh_ready, fresh_out = sem("fresh_ready"), sem("fresh_out")
        lines_ready, lines_spread = sem("lines_ready"), sem("lines_spread")
        list_ready, list_out, list_in = sem("list_ready"), sem("list_out"), sem("list_in")
        iota_seeds = sem("iota_seeds")
        ARRAYS = 5
        block = ctx.enter_context(nc.Block())

        @block.sync
        def _(sp):
            sp.dma_start(dst_i[:, :], dst_rows).then_inc(dst_in, 16)
            with nc.allow_non_contiguous_dma(reason="392 numbers"):
                flat = dst_rows.rearrange("r (h c) -> (r h) c", c=GROUP)
                sp.dma_start(ends_i[:, 0, :], flat[:, 0:1].rearrange("g c -> c g")).then_inc(ends_in, 16)
                sp.dma_start(ends_i[:, 1, :], flat[:, GROUP - 1:GROUP].rearrange("g c -> c g")).then_inc(ends_in, 16)
            sp.dma_start(src_i[:, :], src_rows).then_inc(src_in, 16)
            sp.dma_start(attr[:, :, :], attr_rows).then_inc(attr_in, 16)
            load_nodes(sp, K, x_tiles, range(2))
            sp.wait_ge(fresh_ready, 3)
            for h in range(H0):
                sp.dma_start(K.fresh_dram.rearrange("(r c) h e -> r c h e", c=CHUNKS)[:, :, h, :],
                             fresh[:, :].rearrange("r (c e) -> r c e", e=P)).then_inc(fresh_out, 16)
            sp.wait_ge(list_ready, 2)
            with nc.allow_non_contiguous_dma(reason="a list of 512 numbers"):
                sp.dma_start(K.list_dram.rearrange("k (h p) -> p k h", p=P), step_i[:, :, :]).then_inc(list_out, 16)
            sp.wait_ge(list_out, 16)
            sp.dma_start(K.step_list[0:1, :, UNROLL:UNROLL + HALVES * P],
                         K.list_dram.rearrange("(a k) s -> a k s", a=1)).then_inc(list_in, 16)
            sp.wait_ge(list_in, 16)
            sp.wait_ge(fresh_out, 16 * H0)

        @block.gpsimd
        def _(pool):
            pool.iota(K.iota_i[:, :], [[1, 2 * P]], channel_multiplier=0).then_inc(numbers, 1)
            pool.iota(K.step_seed[:, :], [[P, HALVES]], channel_multiplier=1).then_inc(numbers, 1)
            pool.memset(K.identity[:, :], 0.0).then_inc(iota_seeds, 1)
            pool.memset(K.ones[:, :], 1.0).then_inc(numbers, 1)
            pool.memset(K.step_list[:, :, :], 0).then_inc(numbers, 1)
            pool.wait_ge(iota_seeds, 1)
            pool.affine_select(out=K.identity[:, :], in_=K.identity[:, :], compare_op=ALU.not_equal, fill=1.0,
                               base=0, pattern=[[-1, P]], channel_multiplier=1).then_inc(numbers, 1)

        @block.vector
        def _(dve):
            own = Steps(dve, vec)
            dve.wait_ge(numbers, 5)
            own.done(dve.tensor_copy(K.iota[:, :], K.iota_i[:, :]))
            own.done(dve.tensor_copy(step_no[:, :], K.step_seed[:, :]))
            own.done(dve.tensor_scalar(K.minus_first[:, :], K.iota_i[:, 0:TILES], float(-P), None, ALU.mult))
            own.done(dve.tensor_copy(K.identity_b[:, :], K.identity[:, :]))
            own.done(dve.memset(K.ones_b[:, :], 1.0))
            own.done(dve.memset(zeros[:, :], 0.0))
            dve.wait_ge(ends_in, 32)
            own.chained(dve.tensor_single_scalar(ends_b[:, :, :], ends_i[:, :, :], 7, ALU.arith_shift_right))
            own.chained(dve.tensor_copy(ends[:, :, :], ends_b[:, :, :]))
            own.chained(dve.tensor_tensor(count[:, :], ends[:, 1, :], ends[:, 0, :], ALU.subtract))
            own.chained(dve.tensor_scalar(count[:, :], count[:, :], 1.0, None, ALU.add))
            own.chained(dve.tensor_tensor_scan(lines[:, 0, :], zeros[:, :], count[:, :], 0.0, ALU.add, ALU.add))
            own.chained(dve.tensor_tensor(lines[:, 1, :], count[:, :], lines[:, 0, :], ALU.subtract))
            dve.tensor_tensor(lines[:, 1, :], lines[:, 1, :], ends[:, 0, :], ALU.add).then_inc(lines_ready, 1)
            dve.wait_ge(dst_in, 16)
            dve.tensor_copy(rows[:, 0, :], dst_i[:, :]).then_inc(rows_ready, 1)
            dve.wait_ge(rows_ready, 1)
            own.chained(dve.tensor_tensor(rows[:, 1, 0:ROW_EDGES - 1], rows[:, 0, 0:ROW_EDGES - 1],
                                          rows[:, 0, 1:ROW_EDGES], ALU.not_equal))
            dve.tensor_scalar(fresh[:, 1:ROW_EDGES], rows[:, 1, 0:ROW_EDGES - 1], -BIG, None, ALU.mult) \
               .then_inc(fresh_ready, 1)
            dve.wait_ge(fresh_ready, 1)
            dve.memset(fresh[:, :].rearrange("r (c e) -> r c e", e=P)[:, :, 0:1], 0.0).then_inc(fresh_ready, 2)
            dve.memset(rows[:, 1, :].rearrange("r (c e) -> r c e", e=P)[:, :, P - 1:P], 1.0).then_inc(rows_ready, 1)
            dve.wait_ge(src_in, 16)
            dve.tensor_copy(rows[:, 2, :], src_i[:, :]).then_inc(rows_ready, 1)
            for a in range(ARRAYS):
                dve.wait_ge(turned, CHUNKS * (a + 1))
                if a < 3:
                    out = K.edges[:, :, a * GT:(a + 1) * GT]
                else:
                    out = K.edges[:, :, 3 * GT:5 * GT].rearrange("p g (t j) -> p g t j", j=2)[:, :, :, a - 3]
                if a == 2:
                    out = out.bitcast(I32)
                dve.tensor_copy(out.rearrange("p (r h) t -> p r h t", h=CHUNKS // GT),
                                ps[:, a % 2, :, 0:EDGE_ROWS].rearrange("p (h t) r -> p r h t", t=GT)) \
                   .then_inc(kept, 1)
            dve.wait_ge(lines_spread, 1)
            own.done(dve.tensor_copy(group_no[:, :], K.iota[:, 0:GROUPS]))
            own.settle()
            for h in range(HALVES):
                own.chained(dve.tensor_scalar(below[:, h, :], ps_lines[:, 0, :], step_no[:, h:h + 1], None, ALU.is_le))
            own.chained(dve.tensor_reduce(step_g[:, :], below[:, :, :], AX.X, ALU.add))
            for h in range(HALVES):
                own.chained(dve.tensor_scalar(below[:, h, :], group_no[:, :], step_g[:, h:h + 1], None, ALU.is_equal))
                own.chained(dve.tensor_tensor(below[:, h, :], below[:, h, :], ps_lines[:, 1, :], ALU.mult))
            own.chained(dve.tensor_reduce(step_b[:, :], below[:, :, :], AX.X, ALU.add))
            own.chained(dve.tensor_tensor(step_b[:, :], step_b[:, :], step_no[:, :], ALU.add))
            own.chained(dve.tensor_scalar(late[:, :], step_g[:, :], float(GROUPS), float(STEPS), ALU.is_ge, ALU.mult))
            own.chained(dve.tensor_tensor(step_b[:, :], step_b[:, :], late[:, :], ALU.add))
            own.chained(dve.tensor_scalar(step_g[:, :], step_g[:, :], float(GROUPS - 1), None, ALU.min))
            dve.tensor_copy(step_i[:, 0, :], step_g[:, :]).then_inc(list_ready, 1)
            own.chained(dve.tensor_scalar(step_b[:, :], step_b[:, :], float(DUMMY), None, ALU.min))
            dve.tensor_copy(step_i[:, 1, :], step_b[:, :]).then_inc(list_ready, 1)

        @block.tensor
        def _(pe):
            pe.wait_ge(numbers, 5)
            for a in range(ARRAYS):
                if a < 3:
                    pe.wait_ge(rows_ready, a + 1)
                else:
                    pe.wait_ge(attr_in, 16)
                if a >= 2:
                    pe.wait_ge(kept, a - 1)
                for c in range(CHUNKS):
                    part = rows[:, a, c * P:(c + 1) * P] if a < 3 else attr[:, c * P:(c + 1) * P, a - 3]
                    pe.transpose(ps[:, a % 2, c, 0:EDGE_ROWS], part, K.identity[0:EDGE_ROWS, 0:EDGE_ROWS]) \
                      .then_inc(turned, 1)
                if a == 0:
                    pe.wait_ge(lines_ready, 1)
                    pe.matmul(ps_lines[:, :, :], K.ones[0:1, :], lines[:, :, :], start=True, stop=True) \
                      .then_inc(lines_spread, 1)


def first_tables(nc, K, x_tiles, w, att_src, att_dst):
    WIDE = W0 + H0
    CH = 10
    with ExitStack() as ctx:
        sb = lambda name, shape, dt=F32: ctx.enter_context(nc.sbuf_tensor(name, shape, dt))
        sem = ctx.enter_context(semaphores(nc))
        pb = lambda name, shape: ctx.enter_context(nc.psum_tensor(name, shape, F32))
        stats = sb("x_stats", [P, TILES, 6])
        mv = sb("x_mean_var", [P, TILES, 2])
        w_raw = sb("w_raw", [P, 2, D])
        w_sb = sb("w_sb", [P, 2, WIDE])
        wT = sb("wT", [P, 2, D])
        att = sb("att", [P, 2, 2 * H0])
        y = sb("y_tile", [P, FLOW, D])
        yT = sb("yT", [P, FLOW, 2, P])
        low = sb("low_score", [P, H0])
        lowT = sb("low_scoreT", [H0, 1])
        low_diag = sb("low_diag", [H0, H0])
        psT = [pb(f"yT_ps{k}", [P, 2, 2, P]) for k in range(BANKS)]
        psX = [pb(f"xh_ps{k}", [P, 512]) for k in range(BANKS)]
        w_in, att_in, att_zero = sem("w_in"), sem("att_in"), sem("att_zero")
        vec, stats_ready, wT_ps, wT_ready, fold_ps, w_ready = (sem(n) for n in (
            "tab_vec", "stats_ready", "wT_ps_ready", "wT_ready", "fold_ps", "w_ready"))
        y_ready, yT_turned, yT_ready, xh_ready, xh_kept, dst_kept, rows_out = (sem(n) for n in (
            "y_ready", "yT_turned", "yT_ready", "xh_ready", "xh_kept", "dst_kept", "rows_out"))
        own_ready, own_weight = sem("own_ready"), sem("own_weight")
        root_ready, low_ready, low_turned, low_spread = (sem(n) for n in (
            "root_ready", "low_ready", "low_turned", "low_spread"))
        block = ctx.enter_context(nc.Block())
        table_v = K.table0.rearrange("(t p) w -> p t w", p=P)
        heads = lambda ap: ap.rearrange("p (h c) -> p h c", c=DH0 + 1)
        PER_CHUNK = CH // FLOW
        variances = lambda c: mv[:, c * CH:(c + 1) * CH, 1]

        @block.sync
        def _(sp):
            for k in range(2):
                sp.dma_start(w_raw[:, k, :], w[k * P:(k + 1) * P, :]).then_inc(w_in, 16)
                sp.dma_start(heads(w_sb[:, k, 0:W0])[:, :, 0:DH0],
                             w[k * P:(k + 1) * P, :].rearrange("p (h c) -> p h c", c=DH0)).then_inc(w_in, 16)
            sp.wait_ge(att_zero, 1)
            with nc.allow_non_contiguous_dma(reason="512 numbers, once"):
                for h in range(H0):
                    k, p0 = h * DH0 // P, h * DH0 % P
                    for j, src in enumerate((att_src, att_dst)):
                        sp.dma_start(att[p0:p0 + DH0, k, j * H0 + h:j * H0 + h + 1],
                                     src[h:h + 1, :].rearrange("h d -> d h")).then_inc(att_in, 16)
            load_nodes(sp, K, x_tiles, range(2, len(K.x_in)))

            def turn(i):
                for k in range(FLOW):
                    sp.wait_ge(xh_kept, i * FLOW + (k + 1))
                    sp.dma_start(table_v[:, bass.ds(i * FLOW + k, 1), :],
                                 K.acc[:, bass.ds(i * FLOW + k, 1), :]).then_inc(rows_out, 16)

            rounds(sp, turn)
            sp.wait_ge(rows_out, 16 * TILES)

        @block.vector
        def _(dve):
            own = Steps(dve, vec)
            dve.memset(att[:, :, :], 0.0).then_inc(att_zero, 1)

            def statistics(c):
                tiles = range(c * CH, (c + 1) * CH)
                dve.wait_ge(K.x_in[c], 16)
                for t in tiles:
                    own.done(dve.bn_stats(stats[:, t, :], K.R[:, t, :]))
                own.settle()
                for t in tiles:
                    own.done(dve.bn_aggr(mv[:, t, :], stats[:, t, :]))
                own.settle()
                dve.tensor_scalar(variances(c), variances(c), LN_EPS, None, ALU.add).then_inc(stats_ready, 1)

            def turn(i):
                dve.wait_ge(vec, own.base + own.count)
                for k in range(FLOW):
                    t = i * FLOW + k
                    free(dve, yT_turned, i, k)
                    dve.tensor_scalar(y[:, k, :], K.R[:, bass.ds(t, 1), :].rearrange("p t d -> p (t d)"),
                                      mv[:, bass.ds(t, 1), 0], mv[:, bass.ds(t, 1), 1],
                                      ALU.subtract, ALU.mult).then_inc(y_ready, 1)
                for k in range(FLOW):
                    t = i * FLOW + k
                    dve.wait_ge(y_ready, t + 1)
                    r = K.R[:, bass.ds(t, 1), :].rearrange("p t d -> p (t d)")
                    own.done(dve.tensor_tensor(r, r, y[:, k, :], ALU.add))

            statistics(0)
            for c in range(TILES // CH):
                if c + 1 < TILES // CH:
                    statistics(c + 1)
                dve.wait_ge(root_ready, c + 1)
                own.chained(dve.reciprocal(variances(c), variances(c)))
                if c == 0:
                    for i in range(PER_CHUNK):
                        turn(i)
                else:
                    with dve.Fori(c * PER_CHUNK, (c + 1) * PER_CHUNK) as i:
                        own.loop(i - c * PER_CHUNK, FLOW)
                        turn(i)
                    own.left(PER_CHUNK)
            score = K.acc[:, :, :].rearrange("p t (h c) -> p t h c", c=DH0 + 1)[:, :, :, DH0]
            dve.wait_ge(xh_kept, TILES)
            dve.tensor_reduce(low[:, :], score.rearrange("p t h -> p h t"), AX.X, ALU.min).then_inc(low_ready, 1)
            dve.wait_ge(low_turned, 1)
            dve.tensor_reduce(lowT[:, :], psX[0][0:H0, 0:P], AX.X, ALU.min).then_inc(low_ready, 1)
            dve.wait_ge(low_ready, 2)
            dve.tensor_scalar(low_diag[:, :], K.identity[0:H0, 0:H0], lowT[:, 0:1], None, ALU.mult) \
               .then_inc(low_ready, 1)
            dve.wait_ge(low_spread, 1)
            own.done(dve.tensor_scalar(K.low_row[:, :, :], psX[1][:, 0:H0].rearrange("p (a h) -> p a h", a=1)
                                       .to_broadcast([P, GT, H0]), -1.0, None, ALU.mult))
            own.settle()
            minus_low = K.low_row[:, 0:1, :].to_broadcast([P, TILES, H0])
            own.done(dve.tensor_tensor(K.top_src[:, :, :], score, minus_low, ALU.add))
            dve.wait_ge(dst_kept, TILES)
            own.done(dve.tensor_tensor(K.low_dst[:, :, :], K.sc_dst[:, :, :], minus_low, ALU.subtract))
            for j in range(3):
                part = K.dst_parts[:, :, j * H0:(j + 1) * H0]
                own.chained(dve.tensor_copy(part, K.sc_dst[:, :, :]))
                if j < 2:
                    own.chained(dve.tensor_tensor(K.sc_dst[:, :, :], K.sc_dst[:, :, :], part, ALU.subtract))
            dve.wait_ge(rows_out, 16 * TILES)
            own.chained(dve.tensor_tensor(K.sc_dst[:, :, :], K.top_src[:, :, :], K.low_dst[:, :, :], ALU.add))
            own.chained(dve.scalar_tensor_tensor(K.sc_dst[:, :, :], K.sc_dst[:, :, :], 0.2, K.sc_dst[:, :, :],
                                                 ALU.mult, ALU.max))
            own.chained(dve.tensor_copy(K.shift[:, :, :], K.sc_dst[:, :, :]))
            own.chained(dve.tensor_tensor(score, K.sc_dst[:, :, :], K.shift[:, :, :], ALU.subtract))
            dve.sem_inc(own_ready, 1)
            dve.wait_ge(own_weight, 1)
            all_heads = K.acc[:, :, :].rearrange("p t (h c) -> p (t h) c", c=DH0 + 1)
            own.chained(dve.tensor_tensor(all_heads[:, :, 0:DH0], all_heads[:, :, 0:DH0],
                                          all_heads[:, :, DH0:DH0 + 1].to_broadcast([P, TILES * H0, DH0]), ALU.mult))

        @block.tensor
        def _(pe):
            pe.wait_ge(w_in, 64)
            for k in range(2):
                for j in range(2):
                    pe.transpose(psT[k][:, 0, j, :], w_raw[:, k, j * P:(j + 1) * P], K.identity[:, :]) \
                      .then_inc(wT_ps, 1)
            pe.wait_ge(wT_ready, 2)
            pe.wait_ge(att_in, 16 * 2 * H0)
            for k in range(2):
                for j in range(2):
                    mm = pe.matmul(psX[k][:, 0:2 * H0], wT[:, j, k * P:(k + 1) * P], att[:, j, :],
                                   start=(j == 0), stop=(j == 1))
                mm.then_inc(fold_ps, 1)
            pe.wait_ge(w_ready, 4)

            def turn(i):
                for k in range(FLOW):
                    pe.wait_ge(y_ready, i * FLOW + (k + 1))
                    free(pe, yT_ready, i, k, BANKS)
                    for j in range(2):
                        tr = pe.transpose(psT[k % BANKS][:, 0, j, :], y[:, k, j * P:(j + 1) * P], K.identity[:, :])
                    tr.then_inc(yT_turned, 1)
                for k in range(FLOW):
                    pe.wait_ge(yT_ready, i * FLOW + (k + 1))
                    free(pe, xh_kept, i, k, BANKS)
                    free(pe, dst_kept, i, k, BANKS)
                    for j in range(2):
                        mm = pe.matmul(psX[k % BANKS][:, 0:WIDE], yT[:, k, j, :], w_sb[:, j, :],
                                       start=(j == 0), stop=(j == 1))
                    mm.then_inc(xh_ready, 1)

            rounds(pe, turn)
            pe.wait_ge(low_ready, 1)
            pe.wait_ge(dst_kept, TILES)
            pe.transpose(psX[0][0:H0, 0:P], low[:, :], K.identity[:, :]).then_inc(low_turned, 1)
            pe.wait_ge(low_ready, 3)
            pe.matmul(psX[1][:, 0:H0], K.ones[0:H0, :], low_diag[:, :], start=True, stop=True) \
              .then_inc(low_spread, 1)

        @block.scalar
        def _(act):
            def root(c):
                act.wait_ge(stats_ready, c + 1)
                act.activation(variances(c), variances(c), ACT.Sqrt).then_inc(root_ready, 1)

            root(0)
            act.wait_ge(wT_ps, 4)
            for k in range(2):
                act.activation(wT[:, :, k * P:(k + 1) * P], psT[k][:, 0, :, :], ACT.Copy).then_inc(wT_ready, 1)
            act.wait_ge(fold_ps, 2)
            act.wait_ge(w_in, 64)
            for k in range(2):
                act.activation(heads(w_sb[:, k, 0:W0])[:, :, DH0:DH0 + 1],
                               psX[k][:, 0:H0].rearrange("p (h a) -> p h a", a=1), ACT.Copy).then_inc(w_ready, 1)
                act.activation(w_sb[:, k, W0:WIDE], psX[k][:, H0:2 * H0], ACT.Copy).then_inc(w_ready, 1)

            def turn(i):
                for k in range(FLOW):
                    act.wait_ge(yT_turned, i * FLOW + (k + 1))
                    free(act, xh_ready, i, k)
                    act.activation(yT[:, k, :, :], psT[k % BANKS][:, 0, :, :], ACT.Copy).then_inc(yT_ready, 1)
                for k in range(FLOW):
                    t = i * FLOW + k
                    act.wait_ge(xh_ready, t + 1)
                    act.activation(K.acc[:, bass.ds(t, 1), :].rearrange("p t w -> p (t w)"), psX[k % BANKS][:, 0:W0],
                                   ACT.Copy).then_inc(xh_kept, 1)
                    act.activation(K.sc_dst[:, bass.ds(t, 1), :].rearrange("p t h -> p (t h)"),
                                   psX[k % BANKS][:, W0:WIDE], ACT.Copy).then_inc(dst_kept, 1)

            for c in range(TILES // CH):
                if c + 1 < TILES // CH:
                    root(c + 1)
                if c == 0:
                    for i in range(PER_CHUNK):
                        turn(i)
                else:
                    with act.Fori(c * PER_CHUNK, (c + 1) * PER_CHUNK) as i:
                        turn(i)
            score = K.acc[:, :, :].rearrange("p t (h c) -> p t h c", c=DH0 + 1)[:, :, :, DH0]
            act.wait_ge(own_ready, 1)
            act.activation(score, score, ACT.Exp).then_inc(own_weight, 1)


def at_block(ap, b):
    return ap[:, bass.ds(b, 1), :].rearrange("p t c -> p (t c)")


def seen(eng, sem, s):
    if not isinstance(s, int) or s >= 0:
        eng.wait_ge(sem, s + 1)


def exists(s, steps=STEPS):
    return not isinstance(s, int) or 0 <= s < steps


def slots(eng, slot, lag=0, after_loop=None, steps=STEPS):
    for k in range(UNROLL):
        slot(k, k, 0)
    with eng.Fori(1, steps // UNROLL) as i:
        for k in range(UNROLL):
            slot(i * UNROLL + k, k, i)
    if after_loop:
        after_loop()
    for s in range(steps - steps % UNROLL, steps + lag):
        slot(s, s % UNROLL, s // UNROLL)


def load_list(nc, K, which, first, n, top, engine):
    _, values = nc.values_load_multi_w_load_instructions(
        K.step_list[0:1, which, bass.ds(first, n)], engines=(engine,), min_val=0, max_val=top)
    return list(values)


class Listed:

    def __init__(self, K, eng, line, top):
        self.eng, self.line, self.top = eng, line, top
        if eng.engine not in K.registers:
            K.registers[eng.engine] = [[eng.alloc_register(f"listed_{n}{k}") for k in range(UNROLL)]
                                       for n in ("now", "past")]
        self.now, self.past = K.registers[eng.engine]
        eng.load(self.now, line[:, 0:UNROLL])
        for r in self.past:
            eng.reg_mov(r, 0)

    def read(self):
        self.values = [self.eng.snap(r, min_val=0, max_val=self.top) for r in self.past + self.now]

    def of(self, k, lag):
        return self.values[UNROLL + k - lag]

    def fetch(self, i):
        for p, r in zip(self.past, self.now):
            self.eng.reg_mov(p, r)
        self.eng.load(self.now, self.line[:, bass.ds((i + 1) * UNROLL, UNROLL)])


def first_edges(nc, K):
    with ExitStack() as ctx:
        sb = lambda name, shape, dt=F32: ctx.enter_context(nc.sbuf_tensor(name, shape, dt))
        sem = ctx.enter_context(semaphores(nc))
        pb = lambda name: ctx.enter_context(nc.psum_tensor(name, [P, 512], F32))
        step_data = [sb(f"step_data{k}", [P, 3 * GT]) for k in range(UNROLL)]
        fresh = [sb(f"fresh{k}", [GT * H0, P]) for k in range(UNROLL)]
        dst_here = [sb(f"dst_here{k}", [P, GT]) for k in range(2)]
        rows = [sb(f"gathered{k}", [P, GT, W0]) for k in range(UNROLL)]
        sel = [sb(f"sel{k}", [P, GT, P], BF16) for k in range(UNROLL)]
        sel_f = [sb(f"sel_f{k}", [P, GT, P]) for k in range(UNROLL)]
        selT = [sb(f"selT{k}", [P, GT, P], BF16) for k in range(2)]
        running = [sb(f"running{k}", [GT * H0, P], BF16) for k in range(2)]
        run_top = [sb(f"run_top{k}", [P, GT, H0], BF16) for k in range(2)]
        node_top = sb("node_top", [P, H0])
        score = sb("node_score", [P, H0])
        node = [sb(f"node{k}", [P, 4 * H0], BF16) for k in range(2)]
        drop = [sb(f"drop{k}", [P, H0]) for k in range(2)]
        scale = [sb(f"scale{k}", [P, H0]) for k in range(UNROLL)]
        z = sb("z", [P, GT, H0])
        z_low = [sb(f"z_low{k}", [P, GT, H0]) for k in range(2)]
        msg = [sb(f"msg{k}", [P, GT, W0]) for k in range(2)]
        low_line = sb("low_line", [1, GT * H0], BF16)
        ps_scoreT, ps_run, ps_top, ps_edge = (pb(n) for n in ("ps_scoreT", "ps_run", "ps_top", "ps_edge"))
        ps_selT = ctx.enter_context(nc.psum_tensor("ps_selT", [P, 2 * GT * P], BF16))
        ps_sum = [pb(f"ps_sum{k}") for k in range(2)]
        data_in = [sem(f"data_in{k}") for k in range(UNROLL)]
        gathered = [sem(f"gathered{k}") for k in range(UNROLL)]
        vec, low_ready = sem("e0_vec"), sem("low_line_ready")
        scoreT_ready, scanned, run_turned, run_top_ready, sel_ready, top_ready = (sem(n) for n in (
            "scoreT_ready", "scanned", "run_turned", "run_top_ready", "sel_ready", "top_ready"))
        selT_turned, selT_ready, node_ready, scale_ready, edge_ready, z_ready, p_ready, msg_ready = (
            sem(n) for n in ("selT_turned", "selT_ready", "node_ready", "scale_ready", "edge_ready",
                             "z_ready", "p_ready", "msg_ready"))
        sum_ready, acc_ready, sel_f_ready, parts_ready = (sem(n) for n in (
            "sum_ready", "acc_ready", "sel_f_ready", "parts_ready"))
        data_wanted, rows_wanted, dst_ready = sem("data_wanted"), sem("rows_wanted"), sem("dst_ready")
        block = ctx.enter_context(nc.Block())
        heads = lambda ap: ap.rearrange("p t (h c) -> p t h c", c=DH0 + 1)


        @block.sync
        def _(sp):
            groups = []

            def slot(s, k, i):
                if k == 0:
                    groups[:] = load_list(nc, K, 0, UNROLL + i * UNROLL, UNROLL, GROUPS - 1, ENG.SP)
                g = groups[k]
                edges = sp.snap(g * (5 * GT), min_val=0, max_val=(GROUPS - 1) * 5 * GT)
                marks = sp.snap(g * (GT * H0), min_val=0, max_val=(GROUPS - 1) * GT * H0)
                if after(i, 0):
                    sp.wait_ge(gathered[k], i * (16 * GT))
                    sp.sem_inc(data_wanted, 1)
                    for used in (sel_ready, run_top_ready, scanned):
                        seen(sp, used, s - UNROLL)
                sp.sem_inc(data_wanted, 1)
                sp.dma_start(step_data[k][:, :], K.edges[:, :, :].rearrange("p g c -> p (g c)")
                             [:, bass.ds(edges, 3 * GT)]).then_inc(data_in[k], 16)
                sp.dma_start(fresh[k][:, :], K.fresh_dram.rearrange("t h e -> (t h) e")
                             [bass.ds(marks, GT * H0), :]).then_inc(data_in[k], 16)

            slots(sp, slot)

        @block.gpsimd
        def _(pool):
            def slot(s, k, i):
                pool.wait_ge(data_in[k], (i + 1) * 32)
                seen(pool, msg_ready, s - UNROLL)
                pool.sem_inc(rows_wanted, 1)
                for t in range(GT):
                    pool.indirect_dma_start(
                        rows[k][:, t, :], None, K.table0[:, :],
                        bass.IndirectOffsetOnAxis(ap=step_data[k][:, 2 * GT + t:2 * GT + t + 1].bitcast(I32), axis=0)
                    ).then_inc(gathered[k], 16)

            slots(pool, slot)

        @block.tensor
        def _(pe):
            def turn_scores(s, k, i):
                pe.wait_ge(gathered[k], (i + 1) * (16 * GT))
                seen(pe, scanned, s - 1)
                pe.transpose(ps_scoreT[0:GT * H0, 0:P], heads(rows[k][:, :, :])[:, :, :, DH0], K.identity[:, :]) \
                  .then_inc(scoreT_ready, 1)

            def turn_maxima(s, k):
                seen(pe, scanned, s)
                seen(pe, run_top_ready, s - 1)
                pe.matmul(ps_run[:, 0:GT * H0], running[k % 2][:, :], K.identity_b[0:GT * H0, 0:GT * H0],
                          start=True, stop=False)
                pe.matmul(ps_run[:, 0:GT * H0], K.ones_b[0:1, :], low_line[:, :], start=False, stop=True) \
                  .then_inc(run_turned, 1)

            def node_maxima(s, k):
                seen(pe, sel_ready, s)
                seen(pe, run_top_ready, s)
                seen(pe, node_ready, s - 1)
                for t in range(GT):
                    mm = pe.matmul(ps_top[:, t * H0:(t + 1) * H0], sel[k][:, t, :], run_top[k % 2][:, t, :],
                                   start=True, stop=True)
                mm.then_inc(top_ready, 1)

            def turn_sel(s, k):
                seen(pe, selT_ready, s - 1)
                for t in range(GT):
                    tr = pe.transpose(ps_selT[:, t * P:(t + 1) * P], sel[k][:, t, :], K.identity_b[:, :])
                tr.then_inc(selT_turned, 1)

            def to_edges(s, k):
                seen(pe, node_ready, s)
                seen(pe, parts_ready, s)
                seen(pe, selT_ready, s)
                seen(pe, z_ready, s - 1)
                for t in range(GT):
                    pe.matmul(ps_edge[:, (GT + t) * H0:(GT + t + 1) * H0], selT[k % 2][:, t, :],
                              node[k % 2][:, 3 * H0:4 * H0], start=True, stop=True)
                    for j in range(3):
                        mm = pe.matmul(ps_edge[:, t * H0:(t + 1) * H0], selT[k % 2][:, t, :],
                                       node[k % 2][:, j * H0:(j + 1) * H0], start=(j == 0), stop=(j == 2))
                mm.then_inc(edge_ready, 1)

            def sums(s, k):
                seen(pe, msg_ready, s)
                seen(pe, sel_f_ready, s)
                seen(pe, acc_ready, s - 2)
                for t in range(GT):
                    mm = pe.matmul(ps_sum[k % 2][:, 0:W0], sel_f[k][:, t, :], msg[k % 2][:, t, :],
                                   start=(t == 0), stop=(t == GT - 1))
                mm.then_inc(sum_ready, 1)

            def slot(s, k, i):
                if exists(s):
                    turn_scores(s, k, i)
                    turn_maxima(s, k)
                if exists(s - 3):
                    sums(s - 3, (k - 3) % UNROLL)
                if exists(s - 1):
                    to_edges(s - 1, (k - 1) % UNROLL)
                if exists(s):
                    node_maxima(s, k)
                    turn_sel(s, k)

            pe.wait_ge(low_ready, 1)
            slots(pe, slot, lag=3)

        @block.scalar
        def _(act):
            fetched = act.alloc_register("block_ahead")
            act.load([fetched], K.step_list[0:1, 1, UNROLL:UNROLL + 1])

            def slot(s, k, i):
                if exists(s):
                    b = act.snap(fetched, min_val=0, max_val=DUMMY)
                    seen(act, edge_ready, s - 2)
                    act.activation(node[k % 2][:, 0:3 * H0], at_block(K.dst_parts, b), ACT.Copy) \
                       .then_inc(parts_ready, 1)
                    act.wait_ge(data_in[k], (i + 1) * 32)
                    seen(act, sel_ready, s - 2)
                    act.activation(dst_here[k % 2][:, :], step_data[k][:, 0:GT], ACT.Identity,
                                   bias=K.minus_first[:, bass.ds(b, 1)]).then_inc(dst_ready, 1)
                if exists(s - 2):
                    seen(act, z_ready, s - 2)
                    seen(act, sum_ready, s - 4)
                    act.activation(heads(msg[k % 2][:, :, :])[:, :, :, DH0], z_low[k % 2][:, :, :], ACT.Exp) \
                       .then_inc(p_ready, 1)
                if exists(s - 1):
                    seen(act, node_ready, s - 1)
                    seen(act, acc_ready, s - 5)
                    act.activation(scale[(k - 1) % UNROLL][:, :], drop[(k - 1) % 2][:, :], ACT.Exp) \
                       .then_inc(scale_ready, 1)
                if exists(s):
                    seen(act, sel_ready, s)
                    seen(act, sum_ready, s - UNROLL)
                    act.activation(sel_f[k][:, :, :], sel[k][:, :, :], ACT.Copy).then_inc(sel_f_ready, 1)
                    seen(act, selT_turned, s)
                    seen(act, edge_ready, s - 2)
                    act.activation(selT[k % 2][:, :, :].rearrange("p t e -> p (t e)"), ps_selT[:, 0:GT * P],
                                   ACT.Copy).then_inc(selT_ready, 1)
                    act.load([fetched], K.step_list[0:1, 1, bass.ds(s + (UNROLL + 1), 1)])

            slots(act, slot, lag=2)

        @block.vector
        def _(dve):
            own = Steps(dve, vec)
            blocks = Listed(K, dve, K.step_list[0:1, 1, UNROLL:], DUMMY)

            def slot(s, k, i):
                if k == 0:
                    if not isinstance(i, int):
                        own.loop(i - 1, PER_ROUND)
                    blocks.read()
                now, node_step, edge_step, sum_step = exists(s), exists(s - 1), exists(s - 2), exists(s - 4)
                kn, ke, ks = (k - 1) % UNROLL, (k - 2) % UNROLL, (k - 4) % UNROLL
                edge = ps_edge[:, 0:2 * GT * H0].rearrange("p (j t h) -> p j t h", j=2, h=H0)
                bn, bs = blocks.of(k, 1), blocks.of(k, 4)
                top, shift, new = at_block(K.top_src, bn), at_block(K.shift, bn), node[kn % 2][:, 3 * H0:4 * H0]
                acc = at_block(K.acc, bs)
                own.settle()
                if edge_step:
                    seen(dve, edge_ready, s - 2)
                    seen(dve, z_ready, s - 3)
                    za = own.done(dve.tensor_tensor(z[:, :, :], heads(rows[ke][:, :, :])[:, :, :, DH0],
                                                    edge[:, 0, :, :], ALU.add))
                if node_step:
                    seen(dve, top_ready, s - 1)
                    na = own.done(dve.tensor_reduce(node_top[:, :], ps_top[:, 0:GT * H0]
                                                    .rearrange("p (t h) -> p h t", h=H0), AX.X, ALU.max))
                if now:
                    seen(dve, scoreT_ready, s)
                    dve.wait_ge(data_in[k], (i + 1) * 32)
                    seen(dve, run_turned, s - 2)
                    dve.tensor_tensor_scan(running[k % 2][:, :], fresh[k][:, :], ps_scoreT[0:GT * H0, 0:P],
                                           -3 * BIG, ALU.add, ALU.max).then_inc(scanned, 1)
                if edge_step:
                    own.until(za)
                    za = own.done(dve.scalar_tensor_tensor(z[:, :, :], z[:, :, :], 0.2, z[:, :, :],
                                                           ALU.mult, ALU.max))
                if node_step:
                    own.until(na)
                    na = own.done(dve.tensor_tensor(top, top, node_top[:, :], ALU.max))
                if sum_step:
                    seen(dve, scale_ready, s - 4)
                    seen(dve, acc_ready, s - 5)
                    acc_h = acc.rearrange("p (h c) -> p h c", c=DH0 + 1)
                    sa = own.done(dve.tensor_tensor(
                        acc_h, acc_h, scale[ks][:, :].rearrange("p (h a) -> p h a", a=1)
                        .to_broadcast([P, H0, DH0 + 1]), ALU.mult))
                if now:
                    for used in (sel_f_ready, selT_turned, top_ready):
                        seen(dve, used, s - UNROLL)
                    seen(dve, dst_ready, s)
                    dve.tensor_tensor(
                        sel[k][:, :, :],
                        dst_here[k % 2][:, :].rearrange("p (t a) -> p t a", a=1).to_broadcast([P, GT, P]),
                        K.iota[:, 0:P].rearrange("p (a n) -> p a n", a=1).to_broadcast([P, GT, P]),
                        ALU.is_equal).then_inc(sel_ready, 1)
                if edge_step:
                    own.until(za)
                    za = own.done(dve.tensor_tensor(z[:, :, :], z[:, :, :], edge[:, 1, :, :], ALU.subtract))
                if node_step:
                    own.until(na)
                    na = own.done(dve.tensor_tensor(score[:, :], top, at_block(K.low_dst, bn), ALU.add))
                if now:
                    seen(dve, run_turned, s)
                    seen(dve, top_ready, s - 2)
                    last = step_data[k][:, GT:2 * GT].rearrange("p (t a) -> p t a", a=1).to_broadcast([P, GT, H0])
                    dve.tensor_tensor(run_top[k % 2][:, :, :],
                                      ps_run[:, 0:GT * H0].rearrange("p (t h) -> p t h", h=H0),
                                      last, ALU.mult).then_inc(run_top_ready, 1)
                if edge_step:
                    own.until(za)
                    seen(dve, p_ready, s - 4)
                    dve.tensor_scalar(z_low[ke % 2][:, :, :], z[:, :, :], SAFE, None, ALU.min).then_inc(z_ready, 1)
                if node_step:
                    own.until(na)
                    seen(dve, edge_ready, s - 3)
                    na = own.done(dve.scalar_tensor_tensor(new, score[:, :], 0.2, score[:, :], ALU.mult, ALU.max))
                if sum_step:
                    own.until(sa)
                    seen(dve, sum_ready, s - 4)
                    dve.tensor_tensor(acc, acc, ps_sum[ks % 2][:, 0:W0], ALU.add).then_inc(acc_ready, 1)
                if node_step:
                    own.until(na)
                    seen(dve, scale_ready, s - 3)
                    dve.tensor_tensor(drop[kn % 2][:, :], shift, new, ALU.subtract).then_inc(node_ready, 1)
                if node_step:
                    seen(dve, node_ready, s - 1)
                    own.done(dve.tensor_scalar(shift, new, 0.0, None, ALU.add))
                if edge_step:
                    seen(dve, p_ready, s - 2)
                    dve.tensor_tensor(heads(msg[ke % 2][:, :, :])[:, :, :, 0:DH0],
                                      heads(rows[ke][:, :, :])[:, :, :, 0:DH0],
                                      heads(msg[ke % 2][:, :, :])[:, :, :, DH0:DH0 + 1]
                                      .to_broadcast([P, GT, H0, DH0]), ALU.mult).then_inc(msg_ready, 1)
                if k == UNROLL - 1:
                    blocks.fetch(i)

            PER_ROUND = UNROLL * 9
            dve.tensor_copy(low_line[:, :], K.low_row[0:1, :, :].rearrange("p t h -> p (t h)")).then_inc(low_ready, 1)
            slots(dve, slot, lag=4, after_loop=lambda: own.left(STEPS // UNROLL - 1))


def batch_norm(nc, K, norm, bias, gamma, beta):
    CH = 5
    CHS = TILES // CH
    TAIL = N_NODES - (BLOCKS - 1) * P
    with ExitStack() as ctx:
        sb = lambda name, shape, dt=F32: ctx.enter_context(nc.sbuf_tensor(name, shape, dt))
        sem = ctx.enter_context(semaphores(nc))
        affine = sb("bn_affine", [P, 3, D])
        square = sb("bn_square", [P, 4, D])
        mean = sb("bn_mean", [P, D])
        factor = sb("bn_factor", [P, D])
        tail = sb("tail_ones", [P, P])
        zero = sb("zero_rows", [P, D])
        ps_mean = ctx.enter_context(nc.psum_tensor("ps_mean", [P, 512], F32))
        ps_var = ctx.enter_context(nc.psum_tensor("ps_var", [P, 512], F32))
        scaled, added = sem("bn_scaled"), sem("bn_added")
        affine_in, tail_ready, zero_ready, zeroed, beta_added = (sem(n) for n in (
            "affine_in", "tail_ready", "zero_ready", "zeroed", "beta_added"))
        vec, out_ready, mean_ready, centred, squared, square_used, var_ready, vareps, root = (sem(n) for n in (
            "bn_vec", "out_ready", "mean_ready", "centred", "squared", "square_used", "var_ready", "vareps", "root"))
        block = ctx.enter_context(nc.Block())
        ZT = 12
        heads = lambda ap: ap.rearrange("p t (h c) -> p t h c", c=DH0 + 1)
        of_heads = lambda ap: ap.rearrange("p (a h c) -> p a h c", a=1, c=DH0)

        @block.sync
        def _(sp):
            for j, v in enumerate((bias, gamma, beta)):
                sp.dma_start(affine[:, j, :], v.rearrange("(a n) -> a n", a=1).to_broadcast([P, D])) \
                  .then_inc(affine_in, 16)
            sp.wait_ge(zero_ready, 1)
            slots_v = K.slot_x.rearrange("(t p) d -> p t d", p=P)
            for t in range(0, SLOT_TILES, ZT):
                sp.dma_start(slots_v[:, t:t + ZT, :],
                             zero[:, :].rearrange("p (a d) -> p a d", a=1).to_broadcast([P, ZT, D])) \
                  .then_inc(zeroed, 16)
            sp.wait_ge(zeroed, 16 * (SLOT_TILES // ZT))

        @block.gpsimd
        def _(pool):
            pool.memset(zero[:, :], 0.0).then_inc(zero_ready, 1)
            pool.affine_select(out=tail[:, :], in_=K.ones[:, :], compare_op=ALU.is_ge, fill=0.0,
                               base=TAIL - 1, pattern=[[0, P]], channel_multiplier=-1).then_inc(tail_ready, 1)
            pool.wait_ge(affine_in, 48)
            for c in range(CHS):
                r = K.R[:, c * CH:(c + 1) * CH, :]
                pool.tensor_tensor(r, r, affine[:, 2:3, :].to_broadcast([P, CH, D]), ALU.add).then_inc(beta_added, 1)
            for c in range(CHS):
                pool.wait_ge(scaled, c + 1)
                pool.wait_ge(beta_added, c + 1)
                r = K.R[:, c * CH:(c + 1) * CH, :].rearrange("p t (h c) -> p t h c", c=DH0)
                pool.tensor_tensor(r, r, heads(K.acc[:, c * CH:(c + 1) * CH, :])[:, :, :, 0:DH0], ALU.add) \
                    .then_inc(added, 1)

        @block.vector
        def _(dve):
            own = Steps(dve, vec)
            weight = heads(K.acc[:, :, :])[:, :, :, DH0:DH0 + 1]
            own.chained(dve.reciprocal(weight, weight))
            dve.wait_ge(affine_in, 48)
            for c in range(CHS):
                part = heads(K.acc[:, c * CH:(c + 1) * CH, :])
                out = part[:, :, :, 0:DH0].rearrange("p t h c -> p (t h) c")
                own.chained(dve.tensor_tensor(out, out, part[:, :, :, DH0:DH0 + 1].rearrange("p t h c -> p (t h) c")
                                              .to_broadcast([P, CH * H0, DH0]), ALU.mult))
                out = part[:, :, :, 0:DH0]
                dve.tensor_tensor(out, out, of_heads(affine[:, 0, :]).to_broadcast([P, CH, H0, DH0]), ALU.add) \
                   .then_inc(out_ready, 1)
            dve.wait_ge(mean_ready, 1)
            own.chained(dve.tensor_scalar(mean[:, :], ps_mean[:, 0:D], 1.0 / N_NODES, None, ALU.mult))
            dve.wait_ge(out_ready, CHS)
            for c in range(CHS):
                out = heads(K.acc[:, c * CH:(c + 1) * CH, :])[:, :, :, 0:DH0]
                dve.tensor_tensor(out, out, of_heads(mean[:, :]).to_broadcast([P, CH, H0, DH0]), ALU.subtract) \
                   .then_inc(centred, 1)
            dve.wait_ge(var_ready, 1)
            dve.tensor_scalar(factor[:, :], ps_var[:, 0:D], 1.0 / N_NODES, LN_EPS, ALU.mult, ALU.add) \
               .then_inc(vareps, 1)
            dve.wait_ge(root, 1)
            own.chained(dve.reciprocal(factor[:, :], factor[:, :]))
            own.chained(dve.tensor_tensor(factor[:, :], factor[:, :], affine[:, 1, :], ALU.mult))
            dve.wait_ge(centred, CHS)
            dve.wait_ge(squared, BLOCKS)
            for c in range(CHS + 1):
                if c < CHS:
                    out = heads(K.acc[:, c * CH:(c + 1) * CH, :])[:, :, :, 0:DH0]
                    dve.tensor_tensor(out, out, of_heads(factor[:, :]).to_broadcast([P, CH, H0, DH0]), ALU.mult) \
                       .then_inc(scaled, 1)
                if c >= 1:
                    dve.wait_ge(added, c)
                    norm.statistics(dve, own, range((c - 1) * CH, c * CH))
            norm.inverse(dve, own)

        @block.scalar
        def _(act):
            for t in range(BLOCKS):
                act.wait_ge(centred, t // CH + 1)
                if t >= 4:
                    act.wait_ge(square_used, t - 3)
                act.activation(square[:, t % 4, :].rearrange("p (h c) -> p h c", c=DH0),
                               heads(K.acc[:, t:t + 1, :])[:, 0, :, 0:DH0], ACT.Square).then_inc(squared, 1)
            act.wait_ge(vareps, 1)
            act.activation(factor[:, :], factor[:, :], ACT.Sqrt).then_inc(root, 1)
            norm.roots(act)

        @block.tensor
        def _(pe):
            pe.wait_ge(tail_ready, 1)
            for t in range(BLOCKS):
                pe.wait_ge(out_ready, t // CH + 1)
                mm = pe.matmul(ps_mean[:, 0:D], (tail if t == BLOCKS - 1 else K.ones)[:, :],
                               heads(K.acc[:, t:t + 1, :])[:, 0, :, 0:DH0], start=(t == 0), stop=(t == BLOCKS - 1))
            mm.then_inc(mean_ready, 1)
            for t in range(BLOCKS):
                pe.wait_ge(squared, t + 1)
                mm = pe.matmul(ps_var[:, 0:D], (tail if t == BLOCKS - 1 else K.ones)[:, :], square[:, t % 4, :],
                               start=(t == 0), stop=(t == BLOCKS - 1)).then_inc(square_used, 1)
            pe.wait_ge(square_used, BLOCKS)
            pe.sem_inc(var_ready, 1)


class Normalised:

    def __init__(self, nc, ctx, name, x):
        self.x = x
        self.stats = ctx.enter_context(nc.sbuf_tensor(f"{name}_stats", [P, TILES, 6], F32))
        self.mv = ctx.enter_context(nc.sbuf_tensor(f"{name}_mean_var", [P, TILES, 2], F32))
        sem = ctx.enter_context(semaphores(nc))
        self.stats_ready, self.root_ready = sem(f"{name}_stats_ready"), sem(f"{name}_root_ready")

    def statistics(self, dve, own, tiles):
        for t in tiles:
            own.done(dve.bn_stats(self.stats[:, t, :], self.x[:, t, :]))
        own.settle()
        for t in tiles:
            own.done(dve.bn_aggr(self.mv[:, t, :], self.stats[:, t, :]))

    def inverse(self, dve, own):
        own.settle()
        dve.tensor_scalar(self.mv[:, :, 1], self.mv[:, :, 1], LN_EPS, None, ALU.add).then_inc(self.stats_ready, 1)
        dve.wait_ge(self.root_ready, 1)
        own.chained(dve.reciprocal(self.mv[:, :, 1], self.mv[:, :, 1]))

    def roots(self, act):
        act.wait_ge(self.stats_ready, 1)
        act.activation(self.mv[:, :, 1], self.mv[:, :, 1], ACT.Sqrt).then_inc(self.root_ready, 1)

    def tile(self, dve, y, t):
        return dve.tensor_scalar(y, at_block(self.x, t), self.mv[:, bass.ds(t, 1), 0], self.mv[:, bass.ds(t, 1), 1],
                                 ALU.subtract, ALU.mult)


def gate(nc, K, norm, wg, bg, bias, w1, b1, w2, b2):
    with ExitStack() as ctx:
        sb = lambda name, shape, dt=F32: ctx.enter_context(nc.sbuf_tensor(name, shape, dt))
        sem = ctx.enter_context(semaphores(nc))
        E = EXPERTS
        KF = DFF // P
        weights_in = sem("weights_in")
        y = sb("gate_y", [P, FLOW, D])
        yT = sb("gate_yT", [P, FLOW, 2, P])
        wg_sb = sb("wg_sb", [P, 2, E])
        offset = sb("gate_offset", [P, 2, E])
        logits = sb("logits", [P, TILES, E])
        best = sb("best", [P, TILES, E])
        best_i = sb("best_i", [P, TILES, E], mybir.dt.uint32)
        choice = sb("choice", [P, TILES, 2])
        gap = sb("gap", [P, TILES])
        one_hot = sb("one_hot", [P, 2, TILES, E])
        taken = sb("taken", [P, TILES, E])
        before = sb("before", [P, P])
        keep = sb("keep", [P, E, TILES])
        by_tile = sb("by_tile", [P, E, TILES])
        upto = sb("upto", [P, E, TILES])
        tiles_i = sb("expert_tiles_i", [P, E], I32)
        tiles_f = sb("expert_tiles", [P, E])
        zero8 = sb("zero8", [P, E])
        ends = sb("expert_ends", [P, E])
        place = sb("place", [P, TILES, E])
        owner = sb("owner_f", [1, OWNERS])
        slot_f = sb("slot_f", [P, 2, TILES])
        psT = [ctx.enter_context(nc.psum_tensor(f"gate_psT{k}", [P, 512], F32)) for k in range(3)]
        psL = [ctx.enter_context(nc.psum_tensor(f"gate_psL{k}", [P, 512], F32)) for k in range(3)]
        vec, w_in, y_ready, turned, yT_ready, logit_ready, logit_kept = (sem(n) for n in (
            "gate_vec", "wg_in", "gate_y_ready", "gate_turned", "gate_yT_ready", "logit_ready", "logit_kept"))
        before_ready, taken_ready, ranked, gap_ready, gap_exp = (sem(n) for n in (
            "before_ready", "taken_ready", "ranked", "gap_ready", "gap_exp"))
        NB = 3
        block = ctx.enter_context(nc.Block())

        @block.sync
        def _(sp):
            for k in range(2):
                sp.dma_start(wg_sb[:, k, :], wg[k * P:(k + 1) * P, :]).then_inc(w_in, 16)
            for j, v in enumerate((bg, bias)):
                sp.dma_start(offset[:, j, :], v.rearrange("(a n) -> a n", a=1).to_broadcast([P, E])).then_inc(w_in, 16)
            sp.dma_start(K.b1_rows[:, :], b1.rearrange("e (f p) -> (e f) p", p=P)).then_inc(weights_in, 16)
            sp.dma_start(K.b2[:, :, :], b2.rearrange("(a e) d -> a e d", a=1).to_broadcast([P, EXPERTS, D])) \
              .then_inc(weights_in, 16)
            for e in range(EXPERTS):
                sp.dma_start(K.w1[:, 2 * e:2 * e + 2, :], w1[e].rearrange("(j p) f -> p j f", p=P)) \
                  .then_inc(weights_in, 16)
                sp.dma_start(K.w2[:, KF * e:KF * (e + 1), :], w2[e].rearrange("(j p) f -> p j f", p=P)) \
                  .then_inc(weights_in, 16)
            sp.wait_ge(weights_in, 16 * (2 * EXPERTS + 2))

        @block.gpsimd
        def _(pool):
            pool.affine_select(out=before[:, :], in_=K.ones[:, :], compare_op=ALU.is_ge, fill=0.0,
                               base=-1, pattern=[[1, P]], channel_multiplier=-1).then_inc(before_ready, 1)

        @block.scalar
        def _(act):

            def turn(i):
                for k in range(FLOW):
                    act.wait_ge(turned, i * FLOW + (k + 1))
                    free(act, logit_ready, i, k)
                    act.activation(yT[:, k, :, :].rearrange("p j e -> p (j e)"), psT[k % NB][:, 0:D], ACT.Copy) \
                       .then_inc(yT_ready, 1)
                for k in range(FLOW):
                    act.wait_ge(logit_ready, i * FLOW + (k + 1))
                    act.activation(at_block(logits, i * FLOW + k), psL[k % NB][:, 0:E], ACT.Copy) \
                       .then_inc(logit_kept, 1)

            rounds(act, turn)
            act.wait_ge(gap_ready, 1)
            act.activation(gap[:, :], gap[:, :], ACT.Exp).then_inc(gap_exp, 1)

        @block.tensor
        def _(pe):
            pe.wait_ge(w_in, 64)

            def turn(i):
                for k in range(FLOW):
                    pe.wait_ge(y_ready, i * FLOW + (k + 1))
                    free(pe, yT_ready, i, k, NB)
                    for j in range(2):
                        tr = pe.transpose(psT[k % NB][:, j * P:(j + 1) * P], y[:, k, j * P:(j + 1) * P],
                                          K.identity[:, :])
                    tr.then_inc(turned, 1)
                for k in range(FLOW):
                    pe.wait_ge(yT_ready, i * FLOW + (k + 1))
                    free(pe, logit_kept, i, k, NB)
                    for j in range(2):
                        mm = pe.matmul(psL[k % NB][:, 0:E], yT[:, k, j, :], wg_sb[:, j, :],
                                       start=(j == 0), stop=(j == 1))
                    mm.then_inc(logit_ready, 1)

            rounds(pe, turn)
            pe.wait_ge(before_ready, 1)
            pe.wait_ge(taken_ready, 1)
            pe.wait_ge(logit_kept, TILES)
            flat = taken[:, :, :].rearrange("p t e -> p (t e)")
            pe.matmul(psL[0][:, 0:TILES * E], before[:, :], flat, start=True, stop=True).then_inc(ranked, 1)
            pe.matmul(psL[1][:, 0:TILES * E], K.ones[:, :], flat, start=True, stop=True).then_inc(ranked, 1)

        @block.vector
        def _(dve):
            own = Steps(dve, vec)

            def turn(i):
                for k in range(FLOW):
                    free(dve, turned, i, k)
                    norm.tile(dve, y[:, k, :], i * FLOW + k).then_inc(y_ready, 1)

            rounds(dve, turn)
            dve.wait_ge(logit_kept, TILES)
            dve.wait_ge(w_in, 64)
            for j in range(2):
                own.chained(dve.tensor_tensor(logits[:, :, :], logits[:, :, :],
                                              offset[:, j:j + 1, :].to_broadcast([P, TILES, E]), ALU.add))
            for t in range(TILES):
                own.done(dve.max(best[:, t, :], logits[:, t, :]))
            own.settle()
            for t in range(TILES):
                own.done(dve.max_index(best_i[:, t, :], best[:, t, :], logits[:, t, :]))
            own.done(dve.memset(keep[:, :, :], 1.0))
            own.done(dve.memset(zero8[:, :], 0.0))
            own.done(dve.memset(K.slot[:, TILES:TILES + FLOW, :], 0))
            own.settle()
            dve.tensor_tensor(gap[:, :], best[:, :, 1], best[:, :, 0], ALU.subtract).then_inc(gap_ready, 1)
            own.done(dve.memset(keep[:, :, 0:1], 0.0))
            own.chained(dve.tensor_copy(choice[:, :, :], best_i[:, :, 0:2]))
            for j in range(2):
                own.done(dve.tensor_tensor(
                    one_hot[:, j, :, :], choice[:, :, j:j + 1].to_broadcast([P, TILES, E]),
                    K.iota[:, 0:E].rearrange("p (a e) -> p a e", a=1).to_broadcast([P, TILES, E]), ALU.is_equal))
            own.settle()
            dve.tensor_tensor(taken[:, :, :], one_hot[:, 0, :, :], one_hot[:, 1, :, :], ALU.add) \
               .then_inc(taken_ready, 1)
            dve.wait_ge(gap_exp, 1)
            own.chained(dve.tensor_scalar(K.share[:, :, 0], gap[:, :], 1.0, None, ALU.add))
            own.chained(dve.reciprocal(K.share[:, :, 0], K.share[:, :, 0]))
            own.done(dve.tensor_tensor(K.share[:, :, 1], gap[:, :], K.share[:, :, 0], ALU.mult))
            dve.wait_ge(ranked, 2)
            own.chained(dve.tensor_copy(by_tile[:, :, :], psL[1][:, 0:TILES * E].rearrange("p (t e) -> p e t", e=E)))
            flat = lambda x: x[:, :, :].rearrange("p e t -> p (e t)")
            own.chained(dve.tensor_tensor_scan(flat(upto), flat(keep), flat(by_tile), 0.0, ALU.mult, ALU.add))
            own.chained(dve.tensor_scalar(tiles_f[:, :], upto[:, :, TILES - 1], float(P - 1), None, ALU.add))
            own.chained(dve.tensor_copy(tiles_i[:, :], tiles_f[:, :]))
            own.chained(dve.tensor_single_scalar(tiles_i[:, :], tiles_i[:, :], 7, ALU.arith_shift_right))
            own.chained(dve.tensor_copy(tiles_f[:, :], tiles_i[:, :]))
            own.chained(dve.tensor_tensor_scan(ends[:, :], zero8[:, :], tiles_f[:, :], 0.0, ALU.add, ALU.add))
            own.chained(dve.tensor_tensor(tiles_f[:, :], ends[:, :], tiles_f[:, :], ALU.subtract))
            own.chained(dve.tensor_scalar(tiles_f[:, :], tiles_f[:, :], float(P), None, ALU.mult))
            own.chained(dve.tensor_tensor(upto[:, :, :], upto[:, :, :], by_tile[:, :, :], ALU.subtract))
            own.chained(dve.tensor_tensor(place[:, :, :], psL[0][:, 0:TILES * E].rearrange("p (t e) -> p t e", e=E),
                                          upto[:, :, :].rearrange("p e t -> p t e"), ALU.add))
            own.chained(dve.tensor_tensor(place[:, :, :], place[:, :, :],
                                          tiles_f[:, :].rearrange("p (a e) -> p a e", a=1)
                                          .to_broadcast([P, TILES, E]), ALU.add))
            for j in range(2):
                own.chained(dve.tensor_tensor(one_hot[:, j, :, :], one_hot[:, j, :, :], place[:, :, :], ALU.mult))
                own.chained(dve.tensor_reduce(slot_f[:, j, :], one_hot[:, j, :, :], AX.X, ALU.add))
                own.done(dve.tensor_copy(K.slot[:, 0:TILES, j], slot_f[:, j, :]))
            own.chained(dve.memset(owner[:, :], 0.0))
            for e in range(E - 1):
                own.chained(dve.scalar_tensor_tensor(owner[:, :], K.iota[0:1, 0:OWNERS], ends[0:1, e:e + 1],
                                                     owner[:, :], ALU.is_ge, ALU.add))
            own.chained(dve.tensor_copy(K.owner[:, :], owner[:, :]))


def dispatch(nc, K, norm):
    with ExitStack() as ctx:
        sem = ctx.enter_context(semaphores(nc))
        y = ctx.enter_context(nc.sbuf_tensor("send_y", [P, FLOW, D], F32))
        where = ctx.enter_context(nc.sbuf_tensor("send_where", [P, FLOW, 2], I32))
        y_ready, where_ready, pool_turn = sem("send_y_ready"), sem("where_ready"), sem("send_turn")
        sent = [sem(f"sent{k}") for k in range(FLOW)]
        block = ctx.enter_context(nc.Block())

        @block.vector
        def _(dve):
            def turn(i):
                for k in range(FLOW):
                    if not isinstance(i, int):
                        dve.wait_ge(sent[k], i * 32)
                    norm.tile(dve, y[:, k, :], i * FLOW + k).then_inc(y_ready, 1)
                    dve.tensor_scalar(where[:, k, :], at_block(K.slot, i * FLOW + k), 0.0, None, ALU.add) \
                       .then_inc(where_ready, 1)

            rounds(dve, turn)

        @block.gpsimd
        def _(pool):
            def turn(i):
                for k in range(FLOW):
                    pool.wait_ge(y_ready, i * FLOW + (k + 1))
                    pool.wait_ge(where_ready, i * FLOW + (k + 1))
                    pool.sem_inc(pool_turn, 1)
                    for j in range(2):
                        pool.indirect_dma_start(K.slot_x[:, :],
                                                bass.IndirectOffsetOnAxis(ap=where[:, k, j:j + 1], axis=0),
                                                y[:, k, :], None).then_inc(sent[k], 16)

            rounds(pool, turn)
            for k in range(FLOW):
                pool.wait_ge(sent[k], 32 * (TILES // FLOW))




def experts(nc, K):
    KF = DFF // P
    with ExitStack() as ctx:
        sb = lambda name, shape, dt=F32: ctx.enter_context(nc.sbuf_tensor(name, shape, dt))
        sem = ctx.enter_context(semaphores(nc))
        ps = lambda name: ctx.enter_context(nc.psum_tensor(name, [P, 512], F32))
        b1_sb = sb("experts_b1", [P, EXPERTS * KF])
        x = [sb(f"slot_rows{k}", [P, D]) for k in range(UNROLL)]
        xT = [sb(f"slot_rowsT{k}", [P, 2 * P]) for k in range(2)]
        h = [sb(f"hidden{k}", [P, DFF]) for k in range(2)]
        hT = [sb(f"hiddenT{k}", [P, KF * P]) for k in range(2)]
        o = [sb(f"slot_out{k}", [P, D]) for k in range(UNROLL)]
        psX, psH, psHT, psO = ([ps(f"ps_{n}{k}") for k in range(2)] for n in ("rowsT", "hidden", "hiddenT", "out"))
        x_in = [sem(f"slot_in{k}") for k in range(UNROLL)]
        o_out = [sem(f"slot_out{k}") for k in range(UNROLL)]
        xT_turned, xT_ready, h_ready, h_kept, hT_turned, hT_ready, o_ready, o_kept = (sem(n) for n in (
            "xT_turned", "xT_ready", "h_ready", "h_kept", "hT_turned", "hT_ready", "o_ready", "o_kept"))
        turn, b1_turned, b1_ready = sem("expert_turn"), sem("b1_turned"), sem("b1_ready")
        block = ctx.enter_context(nc.Block())
        x_v = K.slot_x.rearrange("(t p) d -> p t d", p=P)
        y_v = K.slot_y.rearrange("(t p) d -> p t d", p=P)
        flat = lambda t: t.rearrange("p (a d) -> p a d", a=1)
        own_list = K.owner[0:1, :]
        STORE_LAG = 5

        @block.sync
        def _(sp):
            def slot(s, k, i):
                if exists(s, SLOT_TILES):
                    seen(sp, xT_turned, s - UNROLL)
                    sp.sem_inc(turn, 1)
                    sp.dma_start(flat(x[k][:, :]), x_v[:, bass.ds(s, 1), :]).then_inc(x_in[k], 16)
                if exists(s - STORE_LAG, SLOT_TILES):
                    seen(sp, o_kept, s - STORE_LAG)
                    sp.sem_inc(turn, 1)
                    ko = (k - STORE_LAG) % UNROLL
                    sp.dma_start(y_v[:, bass.ds(s - STORE_LAG, 1), :], flat(o[ko][:, :])).then_inc(o_out[ko], 16)

            slots(sp, slot, lag=STORE_LAG, steps=SLOT_TILES)
            for k in range(UNROLL):
                sp.wait_ge(o_out[k], 16 * (SLOT_TILES // UNROLL + (1 if k >= UNROLL - 3 else 0)))

        @block.tensor
        def _(pe):
            owners = Listed(K, pe, own_list, EXPERTS - 1)

            def slot(s, k, i):
                if k == 0:
                    owners.read()
                if exists(s, SLOT_TILES):
                    pe.wait_ge(x_in[k], (i + 1) * 16)
                    seen(pe, xT_ready, s - 2)
                    for j in range(2):
                        tr = pe.transpose(psX[k % 2][:, j * P:(j + 1) * P], x[k][:, j * P:(j + 1) * P],
                                          K.identity[:, :])
                    tr.then_inc(xT_turned, 1)
                if exists(s - 1, SLOT_TILES):
                    e = owners.of(k, 1)
                    q = (k - 1) % 2
                    seen(pe, xT_ready, s - 1)
                    seen(pe, h_kept, s - 3)
                    for j in range(2):
                        mm = pe.matmul(psH[q][:, :], xT[q][:, j * P:(j + 1) * P], at_block(K.w1, e * 2 + j),
                                       start=(j == 0), stop=(j == 1))
                    mm.then_inc(h_ready, 1)
                if exists(s - 2, SLOT_TILES):
                    q = (k - 2) % 2
                    seen(pe, h_kept, s - 2)
                    seen(pe, hT_ready, s - 4)
                    for j in range(KF):
                        tr = pe.transpose(psHT[q][:, j * P:(j + 1) * P], h[q][:, j * P:(j + 1) * P],
                                          K.identity[:, :])
                    tr.then_inc(hT_turned, 1)
                if exists(s - 3, SLOT_TILES):
                    e = owners.of(k, 3)
                    q = (k - 3) % 2
                    seen(pe, hT_ready, s - 3)
                    seen(pe, o_kept, s - 5)
                    for j in range(KF):
                        mm = pe.matmul(psO[q][:, 0:D], hT[q][:, j * P:(j + 1) * P], at_block(K.w2, e * KF + j),
                                       start=(j == 0), stop=(j == KF - 1))
                    mm.then_inc(o_ready, 1)
                if k == UNROLL - 1:
                    owners.fetch(i)

            pe.transpose(psX[0][:, 0:EXPERTS * KF], K.b1_rows[:, :], K.identity[0:EXPERTS * KF, 0:EXPERTS * KF]) \
              .then_inc(b1_turned, 1)
            pe.wait_ge(b1_ready, 1)
            slots(pe, slot, lag=3, steps=SLOT_TILES)

        @block.scalar
        def _(act):
            owners = Listed(K, act, own_list, EXPERTS - 1)

            def slot(s, k, i):
                if k == 0:
                    owners.read()
                if exists(s, SLOT_TILES):
                    seen(act, xT_turned, s)
                    seen(act, h_ready, s - 2)
                    act.activation(xT[k % 2][:, :], psX[k % 2][:, 0:2 * P], ACT.Copy).then_inc(xT_ready, 1)
                if exists(s - 2, SLOT_TILES):
                    e = owners.of(k, 2)
                    q = (k - 2) % 2
                    seen(act, hT_turned, s - 2)
                    seen(act, o_ready, s - 4)
                    for j in range(KF):
                        r = act.activation(hT[q][:, j * P:(j + 1) * P], psHT[q][:, j * P:(j + 1) * P], ACT.Relu,
                                           bias=b1_sb[:, bass.ds(e * KF + j, 1)])
                    r.then_inc(hT_ready, 1)
                if k == UNROLL - 1:
                    owners.fetch(i)

            act.wait_ge(b1_turned, 1)
            act.activation(b1_sb[:, :], psX[0][:, 0:EXPERTS * KF], ACT.Copy).then_inc(b1_ready, 1)
            act.wait_ge(b1_ready, 1)
            slots(act, slot, lag=2, steps=SLOT_TILES)

        @block.vector
        def _(dve):
            owners = Listed(K, dve, own_list, EXPERTS - 1)

            def slot(s, k, i):
                if k == 0:
                    owners.read()
                if exists(s - 1, SLOT_TILES):
                    seen(dve, h_ready, s - 1)
                    seen(dve, hT_turned, s - 3)
                    dve.tensor_copy(h[(k - 1) % 2][:, :], psH[(k - 1) % 2][:, :]).then_inc(h_kept, 1)
                if exists(s - 3, SLOT_TILES):
                    ko = (k - 3) % UNROLL
                    seen(dve, o_ready, s - 3)
                    if after(i, 0):
                        dve.wait_ge(o_out[ko], i * 16)
                    dve.tensor_tensor(o[ko][:, :], psO[(k - 3) % 2][:, 0:D], at_block(K.b2, owners.of(k, 3)),
                                      ALU.add).then_inc(o_kept, 1)
                if k == UNROLL - 1:
                    owners.fetch(i)

            for ko in range(UNROLL - 3, UNROLL):
                dve.sem_inc(o_out[ko], 16)
            slots(dve, slot, lag=3, steps=SLOT_TILES)


def second_tables(nc, K, w_forward, w_reverse, attn):
    FS = F1 + H1
    with ExitStack() as ctx:
        sb = lambda name, shape, dt=F32: ctx.enter_context(nc.sbuf_tensor(name, shape, dt))
        sem = ctx.enter_context(semaphores(nc))
        fetched_y = sb("fetched_rows", [P, FLOW, 2, D])
        where = sb("fetch_where", [P, FLOW, 2], I32)
        stats = sb("t1_stats", [P, FLOW, 6])
        mv = sb("t1_mean_var", [P, FLOW, 2])
        y = sb("t1_y", [P, FLOW, D])
        yT = sb("t1_yT", [P, FLOW, 2 * P])
        w_raw = sb("t1_w_raw", [F1, 2, D])
        attT = sb("t1_attT", [F1, H1])
        w = sb("t1_w", [P, 2, W1C])
        rows = sb("t1_rows", [P, FLOW, W1C])
        psT = [ctx.enter_context(nc.psum_tensor(f"t1_psT{k}", [P, 512], F32)) for k in range(BANKS)]
        psX = [ctx.enter_context(nc.psum_tensor(f"t1_psX{k}", [P, 512], F32)) for k in range(BANKS)]
        vec, w_in, w_turned, w_ready, y_ready, turned, yT_ready, row_ready, row_kept, row_turn = (sem(n) for n in (
            "t1_vec", "t1_w_in", "t1_w_turned", "t1_w_ready", "t1_y_ready", "t1_turned", "t1_yT_ready",
            "t1_row_ready", "t1_row_kept", "t1_row_turn"))
        where_ready, pool_turn, added, var_ready, root_ready = (sem("t1_" + n) for n in (
            "where_ready", "pool_turn", "added", "var_ready", "root_ready"))
        stats_turn = sem("t1_stats_turn")
        fetched = [sem(f"fetched{k}") for k in range(FLOW)]
        rows_out = [sem(f"t1_rows_out{k}") for k in range(FLOW)]
        block = ctx.enter_context(nc.Block())
        table_v = K.table1.rearrange("(t p) w -> p t w", p=P)

        @block.sync
        def _(sp):
            for j, v in enumerate((w_forward, w_reverse)):
                sp.dma_start(w_raw[:, j, :], v[:, :]).then_inc(w_in, 16)
            with nc.allow_non_contiguous_dma(reason="256 numbers, once"):
                sp.dma_start(attT[:, :], attn.rearrange("a h f -> f (a h)")).then_inc(w_in, 16)

            def turn(i):
                for k in range(FLOW):
                    sp.wait_ge(row_kept, i * FLOW + (k + 1))
                    sp.sem_inc(row_turn, 1)
                    sp.dma_start(table_v[:, bass.ds(i * FLOW + k, 1), :], rows[:, k:k + 1, :]).then_inc(rows_out[k], 16)

            rounds(sp, turn)
            for k in range(FLOW):
                sp.wait_ge(rows_out[k], 16 * (TILES // FLOW))

        @block.gpsimd
        def _(pool):
            def turn(i):
                for k in range(FLOW):
                    free(pool, added, i, k)
                    pool.wait_ge(where_ready, i * FLOW + (k + 1))
                    pool.sem_inc(pool_turn, 1)
                    for j in range(2):
                        pool.indirect_dma_start(fetched_y[:, k, j, :], None, K.slot_y[:, :],
                                                bass.IndirectOffsetOnAxis(ap=where[:, k, j:j + 1], axis=0)) \
                            .then_inc(fetched[k], 16)

            rounds(pool, turn)

        @block.vector
        def _(dve):
            own = Steps(dve, vec)

            def place(i, k):
                dve.tensor_scalar(where[:, k, :], at_block(K.slot, i * FLOW + k), 0.0, None, ALU.add) \
                   .then_inc(where_ready, 1)

            def turn(i):
                if not isinstance(i, int):
                    own.loop(i - 1, PER_ROUND)
                for k in range(FLOW):
                    t = i * FLOW + k
                    dve.wait_ge(fetched[k], (i + 1) * 32)
                    place(i + 1, k)
                    r = at_block(K.R, t)
                    own.chained(dve.scalar_tensor_tensor(r, fetched_y[:, k, 0, :], K.share[:, bass.ds(t, 1), 0], r,
                                                         ALU.mult, ALU.add))
                    dve.scalar_tensor_tensor(r, fetched_y[:, k, 1, :], K.share[:, bass.ds(t, 1), 1], r,
                                             ALU.mult, ALU.add).then_inc(added, 1)
                for k in range(FLOW):
                    dve.wait_ge(added, i * FLOW + (k + 1))
                    dve.sem_inc(stats_turn, 1)
                    own.done(dve.bn_stats(stats[:, k, :], at_block(K.R, i * FLOW + k)))
                own.settle()
                dve.sem_inc(stats_turn, 1)
                for k in range(FLOW):
                    own.done(dve.bn_aggr(mv[:, k, :], stats[:, k, :]))
                own.settle()
                dve.tensor_scalar(mv[:, :, 1], mv[:, :, 1], LN_EPS, None, ALU.add).then_inc(var_ready, 1)
                dve.wait_ge(root_ready, i + 1)
                own.chained(dve.reciprocal(mv[:, :, 1], mv[:, :, 1]))
                for k in range(FLOW):
                    free(dve, turned, i, k)
                    dve.tensor_scalar(y[:, k, :], at_block(K.R, i * FLOW + k), mv[:, k, 0:1], mv[:, k, 1:2],
                                      ALU.subtract, ALU.mult).then_inc(y_ready, 1)
                dve.wait_ge(y_ready, i * FLOW + FLOW)

            PER_ROUND = 3 * FLOW + 1
            for k in range(FLOW):
                place(0, k)
            rounds(dve, turn)

        @block.tensor
        def _(pe):
            pe.wait_ge(w_in, 48)
            for j in range(2):
                for k in range(2):
                    pe.transpose(psT[k][:, j * FS:j * FS + F1], w_raw[:, j, k * P:(k + 1) * P],
                                 K.identity[0:F1, 0:F1]).then_inc(w_turned, 1)
                    pe.matmul(psT[k][:, j * FS + F1:(j + 1) * FS], w_raw[:, j, k * P:(k + 1) * P], attT[:, :],
                              start=True, stop=True).then_inc(w_turned, 1)
            pe.wait_ge(w_ready, 2)

            def turn(i):
                for k in range(FLOW):
                    pe.wait_ge(y_ready, i * FLOW + (k + 1))
                    free(pe, yT_ready, i, k, BANKS)
                    for j in range(2):
                        tr = pe.transpose(psT[k % BANKS][:, j * P:(j + 1) * P], y[:, k, j * P:(j + 1) * P],
                                          K.identity[:, :])
                    tr.then_inc(turned, 1)
                for k in range(FLOW):
                    pe.wait_ge(yT_ready, i * FLOW + (k + 1))
                    free(pe, row_kept, i, k, BANKS)
                    for j in range(2):
                        mm = pe.matmul(psX[k % BANKS][:, 0:W1C], yT[:, k, j * P:(j + 1) * P], w[:, j, :],
                                       start=(j == 0), stop=(j == 1))
                    mm.then_inc(row_ready, 1)

            rounds(pe, turn)

        @block.scalar
        def _(act):
            act.wait_ge(w_turned, 8)
            for k in range(2):
                act.activation(w[:, k, :], psT[k][:, 0:W1C], ACT.Copy).then_inc(w_ready, 1)

            def turn(i):
                act.wait_ge(var_ready, i + 1)
                act.activation(mv[:, :, 1], mv[:, :, 1], ACT.Sqrt).then_inc(root_ready, 1)
                for k in range(FLOW):
                    act.wait_ge(turned, i * FLOW + (k + 1))
                    free(act, row_ready, i, k)
                    act.activation(yT[:, k, :], psT[k % BANKS][:, 0:2 * P], ACT.Copy).then_inc(yT_ready, 1)
                for k in range(FLOW):
                    act.wait_ge(row_ready, i * FLOW + (k + 1))
                    if not isinstance(i, int):
                        act.wait_ge(rows_out[k], i * 16)
                    act.activation(rows[:, k, :], psX[k % BANKS][:, 0:W1C], ACT.Copy).then_inc(row_kept, 1)

            rounds(act, turn)


def second_edges(nc, K):
    FS = F1 + H1
    with ExitStack() as ctx:
        sb = lambda name, shape, dt=F32: ctx.enter_context(nc.sbuf_tensor(name, shape, dt))
        sem = ctx.enter_context(semaphores(nc))
        pb = lambda name: ctx.enter_context(nc.psum_tensor(name, [P, 512], F32))
        step_data = [sb(f"e1_data{k}", [P, 5 * GT]) for k in range(UNROLL)]
        dst_here = [sb(f"e1_dst{k}", [P, GT]) for k in range(2)]
        rows = [sb(f"e1_rows{k}", [P, GT, W1C]) for k in range(UNROLL)]
        sel = [sb(f"e1_sel{k}", [P, GT, P]) for k in range(UNROLL)]
        both = [sb(f"e1_both{k}", [P, 2 * GT, FS]) for k in range(2)]
        plain = [sb(f"e1_plain{k}", [P, GT, FS]) for k in range(UNROLL)]
        sc = [sb(f"e1_sc{k}", [P, GT, H1]) for k in range(UNROLL)]
        lane_top = [sb(f"e1_lane_top{k}", [P, H1]) for k in range(2)]
        head_top = sb("e1_head_top", [H1, 1])
        diag = [sb(f"e1_diag{k}", [H1, H1]) for k in range(2)]
        z = [sb(f"e1_z{k}", [P, GT, H1]) for k in range(2)]
        drop = [sb(f"e1_drop{k}", [P, H1]) for k in range(2)]
        scale = [sb(f"e1_scale{k}", [P, H1]) for k in range(UNROLL)]
        msg = [sb(f"e1_msg{k}", [P, GT, A1]) for k in range(2)]
        rest = sb("e1_rest", [P, TILES, H1])
        FEATURES = H1 * F1
        ps_turned = [pb(f"e1_ps_turned{k}") for k in range(2)]
        ps_top = [pb(f"e1_ps_top{k}") for k in range(2)]
        ps_sum = [pb(f"e1_ps_sum{k}") for k in range(2)]
        data_in = [sem(f"e1_data_in{k}") for k in range(UNROLL)]
        gathered = [sem(f"e1_gathered{k}") for k in range(UNROLL)]
        vec, data_wanted, rows_wanted, start, rest_ready, rest_exp = (sem(n) for n in (
            "e1_vec", "e1_data_wanted", "e1_rows_wanted", "e1_start", "e1_rest_ready", "e1_rest_exp"))
        dst_ready, sel_ready, plain_ready, lane_ready, turned, diag_ready, top_ready = (sem("e1_" + n) for n in (
            "dst_ready", "sel_ready", "plain_ready", "lane_ready", "turned", "diag_ready", "top_ready"))
        z_ready, drop_ready, p_ready, scale_ready, msg_ready, sum_ready, acc_ready = (sem("e1_" + n) for n in (
            "z_ready", "drop_ready", "p_ready", "scale_ready", "msg_ready", "sum_ready", "acc_ready"))
        scaled = sem("e1_scaled")
        block = ctx.enter_context(nc.Block())

        @block.sync
        def _(sp):
            groups = []

            def slot(s, k, i):
                if k == 0:
                    groups[:] = load_list(nc, K, 0, UNROLL + i * UNROLL, UNROLL, GROUPS - 1, ENG.SP)
                edges = sp.snap(groups[k] * (5 * GT), min_val=0, max_val=(GROUPS - 1) * 5 * GT)
                if after(i, 0):
                    sp.wait_ge(gathered[k], i * (16 * GT))
                    sp.sem_inc(data_wanted, 1)
                    for used in (scaled, dst_ready):
                        seen(sp, used, s - UNROLL)
                sp.sem_inc(data_wanted, 1)
                sp.dma_start(step_data[k][:, :], K.edges[:, :, :].rearrange("p g c -> p (g c)")
                             [:, bass.ds(edges, 5 * GT)]).then_inc(data_in[k], 16)

            slots(sp, slot)

        @block.gpsimd
        def _(pool):
            def slot(s, k, i):
                pool.wait_ge(data_in[k], (i + 1) * 16)
                seen(pool, scaled, s - UNROLL)
                pool.sem_inc(rows_wanted, 1)
                for t in range(GT):
                    pool.indirect_dma_start(
                        rows[k][:, t, :], None, K.table1[:, :],
                        bass.IndirectOffsetOnAxis(ap=step_data[k][:, 2 * GT + t:2 * GT + t + 1].bitcast(I32), axis=0)
                    ).then_inc(gathered[k], 16)

            slots(pool, slot)

        @block.tensor
        def _(pe):
            def slot(s, k, i):
                if exists(s - 1):
                    q = (k - 1) % 2
                    seen(pe, lane_ready, s - 1)
                    seen(pe, diag_ready, s - 3)
                    pe.transpose(ps_turned[q][0:H1, 0:P], lane_top[q][:, :], K.identity[:, :]).then_inc(turned, 1)
                if exists(s - 2):
                    q = (k - 2) % 2
                    seen(pe, diag_ready, s - 2)
                    seen(pe, z_ready, s - 4)
                    pe.matmul(ps_top[q][:, 0:H1], K.ones[0:H1, :], diag[q][:, :], start=True, stop=True) \
                      .then_inc(top_ready, 1)
                if exists(s - 4):
                    q = (k - 4) % 2
                    seen(pe, msg_ready, s - 4)
                    seen(pe, sel_ready, s - 4)
                    seen(pe, acc_ready, s - 6)
                    for t in range(GT):
                        mm = pe.matmul(ps_sum[q][:, 0:A1], sel[(k - 4) % UNROLL][:, t, :], msg[q][:, t, :],
                                       start=(t == 0), stop=(t == GT - 1))
                    mm.then_inc(sum_ready, 1)

            slots(pe, slot, lag=4)

        @block.scalar
        def _(act):
            blocks = Listed(K, act, K.step_list[0:1, 1, UNROLL:], DUMMY)

            def slot(s, k, i):
                if k == 0:
                    blocks.read()
                if exists(s):
                    act.wait_ge(data_in[k], (i + 1) * 16)
                    seen(act, sel_ready, s - 2)
                    act.activation(dst_here[k % 2][:, :], step_data[k][:, 0:GT], ACT.Identity,
                                   bias=K.minus_first[:, bass.ds(blocks.of(k, 0), 1)]).then_inc(dst_ready, 1)
                if exists(s - 3):
                    q = (k - 3) % 2
                    seen(act, z_ready, s - 3)
                    seen(act, sum_ready, s - 5)
                    act.activation(msg[q][:, :, FEATURES:A1], z[q][:, :, :], ACT.Exp).then_inc(p_ready, 1)
                    seen(act, drop_ready, s - 3)
                    seen(act, acc_ready, s - UNROLL)
                    act.activation(scale[(k - 3) % UNROLL][:, :], drop[q][:, :], ACT.Exp).then_inc(scale_ready, 1)
                if exists(s):
                    act.wait_ge(gathered[k], (i + 1) * (16 * GT))
                    seen(act, plain_ready, s - 2)
                    for c in range(2 * GT):
                        r = act.activation(both[k % 2][:, c, :], rows[k][:, c // 2, (c % 2) * FS:(c % 2 + 1) * FS],
                                           ACT.Copy, scale=step_data[k][:, 3 * GT + c:3 * GT + c + 1])
                    r.then_inc(scaled, 1)
                if k == UNROLL - 1:
                    blocks.fetch(i)

            slots(act, slot, lag=3)
            act.wait_ge(rest_ready, 1)
            act.activation(rest[:, :, :], rest[:, :, :], ACT.Exp).then_inc(rest_exp, 1)

        @block.vector
        def _(dve):
            own = Steps(dve, vec)
            blocks = Listed(K, dve, K.step_list[0:1, 1, UNROLL:], DUMMY)
            own.done(dve.memset(K.acc1[:, :, :], 0.0))
            own.done(dve.memset(K.against[:, :, :], -BIG))
            own.done(dve.memset(K.all_top[:, :], -BIG))
            own.settle()

            def slot(s, k, i):
                if k == 0:
                    if not isinstance(i, int):
                        own.loop(i - 1, PER_ROUND)
                    blocks.read()
                kp, kt, kz, km, ks = ((k - n) % UNROLL for n in range(1, 6))
                sels, plains, tops, zs, ms, sums = (exists(s - n) for n in range(6))
                against = at_block(K.against, blocks.of(k, 3))
                acc = at_block(K.acc1, blocks.of(k, 5))
                acc_h = acc[:, 0:FEATURES].rearrange("p (h c) -> p h c", c=F1)
                own.settle()
                if tops:
                    seen(dve, turned, s - 2)
                    ta = own.done(dve.tensor_reduce(head_top[:, :], ps_turned[kt % 2][0:H1, 0:P], AX.X, ALU.max))
                if zs:
                    seen(dve, top_ready, s - 3)
                    za = own.done(dve.tensor_tensor(K.all_top[:, :], K.all_top[:, :], ps_top[kz % 2][:, 0:H1], ALU.max))
                if plains:
                    seen(dve, scaled, s - 1)
                    seen(dve, msg_ready, s - UNROLL)
                    halves = both[kp % 2][:, :, :].rearrange("p (t j) c -> p t j c", j=2)
                    dve.tensor_tensor(plain[kp][:, :, :], halves[:, :, 0, :], halves[:, :, 1, :], ALU.add) \
                       .then_inc(plain_ready, 1)
                if tops:
                    own.until(ta)
                    seen(dve, top_ready, s - 4)
                    dve.tensor_scalar(diag[kt % 2][:, :], K.identity[0:H1, 0:H1], head_top[:, 0:1], None, ALU.mult) \
                       .then_inc(diag_ready, 1)
                if zs:
                    own.until(za)
                    seen(dve, p_ready, s - 5)
                    dve.tensor_tensor(z[kz % 2][:, :, :], sc[kz][:, :, :],
                                      K.all_top[:, :].rearrange("p (a h) -> p a h", a=1).to_broadcast([P, GT, H1]),
                                      ALU.subtract).then_inc(z_ready, 1)
                if plains:
                    seen(dve, plain_ready, s - 1)
                    seen(dve, z_ready, s - UNROLL)
                    scores = plain[kp][:, :, F1:FS]
                    na = own.done(dve.scalar_tensor_tensor(sc[kp][:, :, :], scores, 0.2, scores, ALU.mult, ALU.max))
                if zs:
                    seen(dve, scale_ready, s - 5)
                    dve.tensor_tensor(drop[kz % 2][:, :], against, K.all_top[:, :], ALU.subtract) \
                       .then_inc(drop_ready, 1)
                if sums:
                    seen(dve, scale_ready, s - 5)
                    seen(dve, acc_ready, s - 6)
                    own.done(dve.tensor_tensor(
                        acc_h, acc_h, scale[ks][:, :].rearrange("p (h a) -> p h a", a=1)
                        .to_broadcast([P, H1, F1]), ALU.mult))
                    sa = own.done(dve.tensor_tensor(acc[:, FEATURES:A1], acc[:, FEATURES:A1], scale[ks][:, :], ALU.mult))
                if plains:
                    own.until(na)
                    seen(dve, turned, s - 3)
                    dve.tensor_reduce(lane_top[kp % 2][:, :], sc[kp][:, :, :].rearrange("p t h -> p h t"), AX.X, ALU.max) \
                       .then_inc(lane_ready, 1)
                if zs:
                    seen(dve, drop_ready, s - 3)
                    own.done(dve.tensor_scalar(against, K.all_top[:, :], 0.0, None, ALU.add))
                if sums:
                    own.until(sa)
                    seen(dve, sum_ready, s - 5)
                    dve.tensor_tensor(acc, acc, ps_sum[ks % 2][:, 0:A1], ALU.add).then_inc(acc_ready, 1)
                if ms:
                    seen(dve, p_ready, s - 4)
                    dve.tensor_tensor(
                        msg[km % 2][:, :, 0:FEATURES].rearrange("p t (h f) -> p t h f", f=F1),
                        plain[km][:, :, 0:F1].rearrange("p t (a f) -> p t a f", a=1).to_broadcast([P, GT, H1, F1]),
                        msg[km % 2][:, :, FEATURES:A1].rearrange("p t (h a) -> p t h a", a=1)
                        .to_broadcast([P, GT, H1, F1]), ALU.mult).then_inc(msg_ready, 1)
                if sels:
                    seen(dve, sum_ready, s - UNROLL)
                    seen(dve, dst_ready, s)
                    dve.tensor_tensor(
                        sel[k][:, :, :],
                        dst_here[k % 2][:, :].rearrange("p (t a) -> p t a", a=1).to_broadcast([P, GT, P]),
                        K.iota[:, 0:P].rearrange("p (a n) -> p a n", a=1).to_broadcast([P, GT, P]),
                        ALU.is_equal).then_inc(sel_ready, 1)
                if k == UNROLL - 1:
                    blocks.fetch(i)

            PER_ROUND = UNROLL * 6
            slots(dve, slot, lag=5, after_loop=lambda: own.left(STEPS // UNROLL - 1))
            own.settle()
            dve.wait_ge(acc_ready, STEPS)
            dve.wait_ge(drop_ready, STEPS)
            own.chained(dve.tensor_tensor(rest[:, :, :], K.all_top[:, :].rearrange("p (a h) -> p a h", a=1)
                                          .to_broadcast([P, TILES, H1]), K.against[:, :, :], ALU.subtract))
            dve.tensor_scalar(rest[:, :, :], rest[:, :, :], 2 * SAFE, None, ALU.min).then_inc(rest_ready, 1)
            dve.wait_ge(rest_exp, 1)
            weight = K.acc1[:, :, FEATURES:A1]
            own.chained(dve.scalar_tensor_tensor(weight, rest[:, :, :], 1e-10, weight, ALU.mult, ALU.add))
            own.chained(dve.reciprocal(weight, weight))


def route(nc, K, wr, br):
    E = EXPERTS
    CAPACITY = float(-(-N_NODES * 5 // (4 * EXPERTS)))
    with ExitStack() as ctx:
        sb = lambda name, shape, dt=F32: ctx.enter_context(nc.sbuf_tensor(name, shape, dt))
        sem = ctx.enter_context(semaphores(nc))
        stats = sb("r_stats", [P, TILES, 6])
        mv = sb("r_mean_var", [P, TILES, 2])
        minus = sb("r_minus", [P, TILES])
        parts = sb("r_parts", [P, 2, TILES // 10])
        wr_sb = sb("r_wr", [P, 2, E])
        br_sb = sb("r_br", [P, E])
        mean = sb("r_mean", [P, 2])
        spread = sb("r_spread", [P, 2, P])
        q = sb("r_q", [P, E])
        load = sb("r_load", [P, E])
        over = sb("r_over", [P, E])
        top = sb("r_top", [P, 1])
        total = sb("r_total", [P, 1])
        best = sb("r_best", [P, 8])
        best_i = sb("r_best_i", [P, 8], mybir.dt.uint32)
        ps_logit = ctx.enter_context(nc.psum_tensor("r_ps_logit", [P, 512], F32))
        psT = [ctx.enter_context(nc.psum_tensor(f"r_psT{k}", [P, 512], F32)) for k in range(BANKS)]
        turned, yT_ready, divided, added, var_ready, root_ready, norm_ready = (sem("r_" + n) for n in (
            "turned", "yT_ready", "divided", "added", "var_ready", "root_ready", "norm_ready"))
        w_in, vec, y_ready, spread_ready, logit_ready, exp_wanted, exp_ready = (sem(n) for n in (
            "r_w_in", "r_vec", "r_y_ready", "r_spread_ready", "r_logit_ready",
            "r_exp_wanted", "r_exp_ready"))
        block = ctx.enter_context(nc.Block())
        CH = 10
        CHS = TILES // CH

        @block.sync
        def _(sp):
            for k in range(2):
                sp.dma_start(wr_sb[:, k, :], wr[k * P:(k + 1) * P, :]).then_inc(w_in, 16)
            sp.dma_start(br_sb[:, :], br.rearrange("(a n) -> a n", a=1).to_broadcast([P, E])).then_inc(w_in, 16)

        @block.gpsimd
        def _(pool):
            for c in range(CHS):
                pool.wait_ge(divided, c + 1)
                r = K.R[:, c * CH:(c + 1) * CH, :]
                pool.tensor_tensor(r, r, K.Y[:, c * CH:(c + 1) * CH, :], ALU.add).then_inc(added, 1)

        @block.tensor
        def _(pe):
            for t in range(TILES):
                pe.wait_ge(y_ready, t + 1)
                if t >= BANKS:
                    pe.wait_ge(yT_ready, t + 1 - BANKS)
                for j in range(2):
                    tr = pe.transpose(psT[t % BANKS][:, j * P:(j + 1) * P], K.Y[:, t, j * P:(j + 1) * P],
                                      K.identity[:, :])
                tr.then_inc(turned, 1)
            pe.wait_ge(w_in, 48)
            pe.wait_ge(spread_ready, 2)
            for j in range(2):
                mm = pe.matmul(ps_logit[:, 0:E], spread[:, j, :], wr_sb[:, j, :], start=(j == 0), stop=(j == 1))
            mm.then_inc(logit_ready, 1)

        @block.scalar
        def _(act):
            for t in range(TILES + 2):
                c = t // CH
                if t < TILES:
                    if t % CH == 0:
                        var = mv[:, c * CH:(c + 1) * CH, 1]
                        act.wait_ge(var_ready, c + 1)
                        act.activation(var, var, ACT.Sqrt).then_inc(root_ready, 1)
                        act.wait_ge(norm_ready, c + 1)
                    act.activation(K.Y[:, t, :], K.R[:, t, :], ACT.Identity, bias=minus[:, t:t + 1],
                                   scale=mv[:, t, 1:2]).then_inc(y_ready, 1)
                t -= 2
                if t < 0:
                    continue
                act.wait_ge(turned, t + 1)
                act.activation(K.YT[:, :, t * P:(t + 1) * P],
                               psT[t % BANKS][:, 0:2 * P].rearrange("p (j e) -> p j e", j=2), ACT.Copy) \
                   .then_inc(yT_ready, 1)
            for n in range(2):
                act.wait_ge(exp_wanted, n + 1)
                act.activation(q[:, :], q[:, :], ACT.Exp).then_inc(exp_ready, 1)
            act.wait_ge(exp_wanted, 3)
            act.activation(K.pair[:, 1:2], K.pair[:, 1:2], ACT.Exp).then_inc(exp_ready, 1)

        @block.vector
        def _(dve):
            own = Steps(dve, vec)
            for c in range(CHS + 3):
                if c < CHS:
                    sums = K.acc1[:, c * CH:(c + 1) * CH, :]
                    dve.tensor_tensor(
                        sums[:, :, 0:D].rearrange("p t (h f) -> p t h f", f=F1),
                        sums[:, :, 0:D].rearrange("p t (h f) -> p t h f", f=F1),
                        sums[:, :, D:A1].rearrange("p t (h a) -> p t h a", a=1).to_broadcast([P, CH, H1, F1]),
                        ALU.mult).then_inc(divided, 1)
                if 1 <= c <= CHS:
                    dve.wait_ge(added, c)
                    for t in range((c - 1) * CH, c * CH):
                        own.done(dve.bn_stats(stats[:, t, :], K.R[:, t, :]))
                    own.settle()
                    for t in range((c - 1) * CH, c * CH):
                        own.done(dve.bn_aggr(mv[:, t, :], stats[:, t, :]))
                    own.settle()
                    var = mv[:, (c - 1) * CH:c * CH, 1]
                    dve.tensor_scalar(var, var, LN_EPS, None, ALU.add).then_inc(var_ready, 1)
                if 2 <= c < CHS + 2:
                    part = slice((c - 2) * CH, (c - 1) * CH)
                    dve.wait_ge(root_ready, c - 1)
                    own.chained(dve.reciprocal(mv[:, part, 1], mv[:, part, 1]))
                    dve.scalar_tensor_tensor(minus[:, part], mv[:, part, 0], -1.0, mv[:, part, 1],
                                             ALU.mult, ALU.mult).then_inc(norm_ready, 1)
                if c >= 3:
                    dve.wait_ge(yT_ready, (c - 2) * CH)
                    own.done(dve.tensor_reduce(
                        parts[:, :, c - 3], K.YT[:, :, (c - 3) * CH * P:min((c - 2) * CH * P, N_NODES)], AX.X, ALU.add))
            own.settle()
            own.chained(dve.tensor_reduce(mean[:, :], parts[:, :, :], AX.X, ALU.add))
            own.chained(dve.tensor_scalar(mean[:, :], mean[:, :], 1.0 / N_NODES, None, ALU.mult))
            for j in range(2):
                dve.tensor_scalar(spread[:, j, :], K.ones[:, :], mean[:, j:j + 1], None, ALU.mult) \
                   .then_inc(spread_ready, 1)
            dve.wait_ge(w_in, 48)
            dve.wait_ge(logit_ready, 1)
            own.chained(dve.tensor_tensor(q[:, :], ps_logit[:, 0:E], br_sb[:, :], ALU.add))
            for n in range(2):
                own.chained(dve.tensor_reduce(top[:, :], q[:, :], AX.X, ALU.max))
                dve.tensor_scalar(q[:, :], q[:, :], top[:, 0:1], None, ALU.subtract).then_inc(exp_wanted, 1)
                dve.wait_ge(exp_ready, n + 1)
                own.chained(dve.tensor_reduce(total[:, :], q[:, :], AX.X, ALU.add))
                own.chained(dve.reciprocal(total[:, :], total[:, :]))
                own.chained(dve.tensor_scalar(q[:, :], q[:, :], total[:, 0:1], None, ALU.mult))
                if n == 0:
                    own.chained(dve.tensor_scalar(load[:, :], q[:, :], float(N_NODES), None, ALU.mult))
                    own.done(dve.tensor_scalar(over[:, :], load[:, :], CAPACITY, None, ALU.is_gt))
                    own.chained(dve.tensor_scalar(load[:, :], load[:, :], CAPACITY, None, ALU.max))
                    own.chained(dve.reciprocal(load[:, :], load[:, :]))
                    own.chained(dve.tensor_scalar(load[:, :], load[:, :], CAPACITY, -1.0, ALU.mult, ALU.add))
                    own.chained(dve.tensor_tensor(load[:, :], load[:, :], over[:, :], ALU.mult))
                    own.chained(dve.tensor_scalar(load[:, :], load[:, :], 1.0, None, ALU.add))
                    own.chained(dve.tensor_tensor(q[:, :], q[:, :], load[:, :], ALU.mult))
            own.chained(dve.max(best[:, :], q[:, :]))
            own.chained(dve.max_index(best_i[:, :], best[:, :], q[:, :]))
            own.done(dve.tensor_copy(K.chosen[:, :], best_i[0:1, 0:2]))
            dve.tensor_tensor(K.pair[:, 1:2], best[:, 1:2], best[:, 0:1], ALU.subtract).then_inc(exp_wanted, 1)
            dve.wait_ge(exp_ready, 3)
            own.chained(dve.tensor_scalar(K.pair[:, 0:1], K.pair[:, 1:2], 1.0, None, ALU.add))
            own.chained(dve.reciprocal(K.pair[:, 0:1], K.pair[:, 0:1]))
            own.chained(dve.tensor_tensor(K.pair[:, 1:2], K.pair[:, 1:2], K.pair[:, 0:1], ALU.mult))


def last_experts(nc, K, w1, b1, w2, b2, gamma, beta, out_rows):
    KF = DFF // P
    PAIR = 2
    HT = 2 * KF
    HB = 4
    TURNS = TILES // PAIR
    assert TURNS % 2 == 1
    CH = 10
    with ExitStack() as ctx:
        sb = lambda name, shape, dt=F32: ctx.enter_context(nc.sbuf_tensor(name, shape, dt))
        sem = ctx.enter_context(semaphores(nc))
        ps = lambda name: ctx.enter_context(nc.psum_tensor(name, [P, 512], F32))
        w1_sb = sb("l_w1", [P, 2 * 2, DFF])
        w2_sb = sb("l_w2", [P, HT, D])
        b1_rows = sb("l_b1_rows", [HT, P])
        b1_sb = sb("l_b1", [P, HT])
        b2_sb = sb("l_b2", [P, 2, D])
        affine = sb("l_affine", [P, 2, D])
        stats = sb("l_stats", [P, PAIR, 6])
        mv = [sb(f"l_mean_var{n}", [P, PAIR, 2]) for n in range(2)]
        hT = [sb(f"l_hT{n}", [P, HT, PAIR * P]) for n in range(2)]
        psY = ps("l_psY")
        psH = [ps(f"l_psH{n}") for n in range(HB)]
        psO = [ps(f"l_psO{a}") for a in range(PAIR)]
        weights_in, rows_in, affine_in, vec, b1_turned, b1_ready, w2_ready, beta_added = (sem("l_" + n) for n in (
            "weights_in", "rows_in", "affine_in", "vec", "b1_turned", "b1_ready", "w2_ready", "beta_added"))
        stats_turn, var_ready, root_ready, done, out_turn, out_done = (sem("l_" + n) for n in (
            "stats_turn", "var_ready", "root_ready", "done", "out_turn", "out_done"))
        hidden, hT_ready, out_ready, z_ready = (sem("l_" + n) for n in (
            "hidden", "hT_ready", "out_ready", "z_ready"))
        block = ctx.enter_context(nc.Block())

        def turns(eng, turn):
            turn(0, 0)
            turn(1, 1)
            with eng.Fori(1, TURNS // 2) as r:
                turn(r * 2, 0)
                turn(r * 2 + 1, 1)
            turn(TURNS - 1, 0)

        @block.sync
        def _(sp):
            _, e = nc.values_load_multi_w_load_instructions(K.chosen[0:1, 0:2], engines=(ENG.SP,), min_val=0,
                                                            max_val=EXPERTS - 1)
            for n in range(2):
                sp.dma_start(b1_rows[n * KF:(n + 1) * KF, :],
                             b1.rearrange("e (f p) -> e f p", p=P)[bass.ds(e[n], 1), :, :]
                             .rearrange("e f p -> (e f) p")).then_inc(rows_in, 16)
                sp.dma_start(b2_sb[:, n, :], b2[bass.ds(e[n], 1), :].to_broadcast([P, D])).then_inc(rows_in, 16)
                sp.dma_start(w1_sb[:, 2 * n:2 * n + 2, :],
                             w1[bass.ds(e[n], 1), :, :].rearrange("e (j p) f -> p (e j) f", p=P)) \
                  .then_inc(weights_in, 16)
                sp.dma_start(w2_sb[:, KF * n:KF * (n + 1), :],
                             w2[bass.ds(e[n], 1), :, :].rearrange("e (j p) f -> p (e j) f", p=P)) \
                  .then_inc(weights_in, 16)
            for j, v in enumerate((gamma, beta)):
                sp.dma_start(affine[:, j, :], v.rearrange("(a n) -> a n", a=1).to_broadcast([P, D])) \
                  .then_inc(affine_in, 16)

            def turn(i, n):
                sp.wait_ge(done, i * PAIR + PAIR)
                sp.sem_inc(out_turn, 1)
                sp.dma_start(out_rows.rearrange("(t p) d -> p t d", p=P)[:, bass.ds(i * PAIR, PAIR), :],
                             K.Y[:, bass.ds(i * PAIR, PAIR), :]).then_inc(out_done, 16)

            turns(sp, turn)
            sp.wait_ge(out_done, 16 * TURNS)

        @block.gpsimd
        def _(pool):
            pool.wait_ge(affine_in, 32)
            for c in range(TILES // CH):
                r = K.R[:, c * CH:(c + 1) * CH, :]
                pool.tensor_tensor(r, r, affine[:, 1:2, :].to_broadcast([P, CH, D]), ALU.add).then_inc(beta_added, 1)
            pool.wait_ge(beta_added, TILES // CH)

        @block.tensor
        def _(pe):
            def give(i, n):
                pe.wait_ge(hT_ready, i * HT + HT)
                if after(i, 0):
                    pe.wait_ge(z_ready, i * PAIR)
                for a in range(PAIR):
                    for m in range(HT):
                        mm = pe.matmul(psO[a][:, 0:D], hT[n][:, m, a * P:(a + 1) * P], w2_sb[:, m, :],
                                       start=(m == 0), stop=(m == HT - 1))
                    mm.then_inc(out_ready, 1)

            def turn(i, n):
                for m in range(HT):
                    if m >= HB or after(i, 0):
                        pe.wait_ge(hT_ready, i * HT + (m + 1 - HB))
                    for j in range(2):
                        mm = pe.matmul(psH[m % HB][:, 0:PAIR * P],
                                       w1_sb[:, (m // KF) * 2 + j, (m % KF) * P:(m % KF + 1) * P],
                                       K.YT[:, j, bass.ds(i * (PAIR * P), PAIR * P)],
                                       start=(j == 0), stop=(j == 1))
                    mm.then_inc(hidden, 1)
                if after(i, 0):
                    give(i - 1, 1 - n)

            pe.wait_ge(rows_in, 64)
            pe.transpose(psY[:, 0:HT], b1_rows[:, :], K.identity[0:HT, 0:HT]).then_inc(b1_turned, 1)
            pe.wait_ge(weights_in, 64)
            pe.wait_ge(b1_ready, 1)
            pe.wait_ge(w2_ready, 1)
            turns(pe, turn)
            give(TURNS - 1, 0)

        @block.scalar
        def _(act):
            def turn(i, n):
                if after(i, 1):
                    act.wait_ge(out_ready, (i - 1) * PAIR)
                for m in range(HT):
                    act.wait_ge(hidden, i * HT + (m + 1))
                    act.activation(hT[n][:, m, :], psH[m % HB][:, 0:PAIR * P], ACT.Gelu, bias=b1_sb[:, m:m + 1]) \
                       .then_inc(hT_ready, 1)
                if after(i, 1):
                    root(i - 2, n)

            def root(i, n):
                act.wait_ge(var_ready, i + 1)
                act.activation(mv[n][:, :, 1], mv[n][:, :, 1], ACT.Sqrt).then_inc(root_ready, 1)

            act.wait_ge(b1_turned, 1)
            act.activation(b1_sb[:, :], psY[:, 0:HT], ACT.Copy).then_inc(b1_ready, 1)
            act.wait_ge(b1_ready, 1)
            turns(act, turn)
            root(TURNS - 2, 1)
            root(TURNS - 1, 0)

        @block.vector
        def _(dve):
            own = Steps(dve, vec)
            dve.wait_ge(weights_in, 64)
            dve.wait_ge(rows_in, 64)
            for n in range(2):
                w = w2_sb[:, n * KF:(n + 1) * KF, :]
                own.done(dve.tensor_scalar(w, w, K.pair[:, n:n + 1], None, ALU.mult))
            own.chained(dve.tensor_scalar(b2_sb[:, 1, :], b2_sb[:, 1, :], K.pair[:, 1:2], None, ALU.mult))
            own.chained(dve.scalar_tensor_tensor(b2_sb[:, 0, :], b2_sb[:, 0, :], K.pair[:, 0:1], b2_sb[:, 1, :],
                                                 ALU.mult, ALU.add))
            dve.sem_inc(w2_ready, 1)

            def sums(i, n):
                for a in range(PAIR):
                    y = at_block(K.Y, i * PAIR + a)
                    own.done(dve.tensor_tensor(y, y, b2_sb[:, 0, :], ALU.add))
                own.settle()
                for a in range(PAIR):
                    y = at_block(K.Y, i * PAIR + a)
                    dve.wait_ge(out_ready, i * PAIR + (a + 1))
                    dve.tensor_tensor(y, y, psO[a][:, 0:D], ALU.add).then_inc(z_ready, 1)
                for a in range(PAIR):
                    dve.wait_ge(z_ready, i * PAIR + (a + 1))
                    dve.sem_inc(stats_turn, 1)
                    own.done(dve.bn_stats(stats[:, a, :], at_block(K.Y, i * PAIR + a)))
                own.settle()
                dve.sem_inc(stats_turn, 1)
                for a in range(PAIR):
                    own.done(dve.bn_aggr(mv[n][:, a, :], stats[:, a, :]))
                own.settle()
                dve.tensor_scalar(mv[n][:, :, 1], mv[n][:, :, 1], LN_EPS, None, ALU.add).then_inc(var_ready, 1)

            def normalise(i, n):
                dve.wait_ge(root_ready, i + 1)
                own.chained(dve.reciprocal(mv[n][:, :, 1], mv[n][:, :, 1]))
                for a in range(PAIR):
                    y = at_block(K.Y, i * PAIR + a)
                    own.done(dve.scalar_tensor_tensor(y, y, mv[n][:, a, 0:1], affine[:, 0, :],
                                                      ALU.subtract, ALU.mult))
                own.settle()
                for a in range(PAIR):
                    y = at_block(K.Y, i * PAIR + a)
                    dve.scalar_tensor_tensor(y, y, mv[n][:, a, 1:2], at_block(K.R, i * PAIR + a),
                                             ALU.mult, ALU.add).then_inc(done, 1)
                dve.wait_ge(done, i * PAIR + PAIR)

            def turn(i, n):
                if after(i, 1):
                    normalise(i - 2, n)
                if after(i, 0):
                    sums(i - 1, 1 - n)

            PER_ROUND = 2 * (4 * PAIR + 1)
            dve.wait_ge(beta_added, TILES // CH)
            turn(0, 0)
            turn(1, 1)
            with dve.Fori(1, TURNS // 2) as r:
                own.loop(r - 1, PER_ROUND)
                turn(r * 2, 0)
                turn(r * 2 + 1, 1)
            own.left(TURNS // 2 - 1)
            turn(TURNS - 1, 0)
            turn(TURNS, 1)
            normalise(TURNS - 1, 0)


class Kept:
    pass


def program(nc, a, out):
    K = Kept()
    K.registers = {}
    with ExitStack() as ctx:
        sb = lambda name, shape, dt=F32: ctx.enter_context(nc.sbuf_tensor(name, shape, dt))
        dram = lambda name, shape, dt=F32: nc.dram_tensor(name, shape, dt, kind="Internal").ap()
        take = ctx.enter_context(semaphores(nc))
        K.x_in = [take(f"x_in{c}") for c in range(5)]
        x_tiles = a["x"].rearrange("(t p) d -> p t d", p=P)
        K.table0 = dram("table0", [N_PAD, W0])
        K.table1 = dram("table1", [N_PAD, W1C])
        K.fresh_dram = dram("fresh_marks", [EDGE_TILES, H0, P])
        K.list_dram = dram("step_list_dram", [2, HALVES * P], I32)
        K.slot_x = dram("slot_x", [SLOT_TILES * P, D])
        K.slot_y = dram("slot_y", [SLOT_TILES * P, D])
        K.R = sb("R", [P, TILES, D])
        K.identity = sb("identity", [P, P])
        K.ones = sb("ones", [P, P])
        K.identity_b = sb("identity_b", [P, P], BF16)
        K.ones_b = sb("ones_b", [P, P], BF16)
        K.iota = sb("iota", [P, 2 * P])
        with ExitStack() as edges:
            sb = lambda name, shape, dt=F32: edges.enter_context(nc.sbuf_tensor(name, shape, dt))
            K.minus_first = sb("minus_first", [P, TILES])
            norm = Normalised(nc, edges, "ffn0", K.R)
            K.edges = sb("edges", [P, GROUPS, 5 * GT])
            K.step_list = sb("step_list", [1, 2, 2 * UNROLL + HALVES * P], I32)
            with ExitStack() as early:
                K.iota_i = early.enter_context(nc.sbuf_tensor("iota_i", [P, 2 * P], I32))
                K.step_seed = early.enter_context(nc.sbuf_tensor("step_seed", [P, HALVES], I32))
                edge_lists(nc, K, x_tiles, a["dst"], a["src"], a["edge_attr_2"])
            with ExitStack() as first:
                sb = lambda name, shape, dt=F32: first.enter_context(nc.sbuf_tensor(name, shape, dt))
                K.acc = sb("acc", [P, TILES, W0])
                with ExitStack() as scores:
                    sb = lambda name, shape, dt=F32: scores.enter_context(nc.sbuf_tensor(name, shape, dt))
                    K.top_src = sb("top_src", [P, TILES, H0])
                    K.sc_dst = sb("sc_dst", [P, TILES, H0])
                    K.low_dst = sb("low_dst", [P, TILES, H0])
                    K.dst_parts = sb("dst_parts", [P, TILES, 3 * H0], BF16)
                    K.shift = sb("shift", [P, TILES, H0], BF16)
                    K.low_row = sb("low_row", [P, GT, H0])
                    first_tables(nc, K, x_tiles, a["L0_gnn_W"], a["L0_gnn_att_src"], a["L0_gnn_att_dst"])
                    first_edges(nc, K)
                batch_norm(nc, K, norm, a["L0_gnn_bias"], a["L0_gnn_gamma"], a["L0_gnn_beta"])
            with ExitStack() as ffn:
                sb = lambda name, shape, dt=F32: ffn.enter_context(nc.sbuf_tensor(name, shape, dt))
                K.share = sb("share", [P, TILES, 2])
                K.slot = sb("slot", [P, TILES + FLOW, 2], I32)
                K.owner = sb("owner", [1, OWNERS], I32)
                K.w1 = sb("experts_w1", [P, EXPERTS * 2, DFF])
                K.w2 = sb("experts_w2", [P, EXPERTS * DFF // P, D])
                K.b2 = sb("experts_b2", [P, EXPERTS, D])
                K.b1_rows = sb("experts_b1_rows", [EXPERTS * DFF // P, P])
                gate(nc, K, norm, a["L0_ffn_Wg"], a["L0_ffn_bg"], a["L0_ffn_bias"],
                     a["L0_ffn_W1"], a["L0_ffn_b1"], a["L0_ffn_W2"], a["L0_ffn_b2"])
                dispatch(nc, K, norm)
                experts(nc, K)
                second_tables(nc, K, a["L1_gnn_W_forward"], a["L1_gnn_W_reverse"], a["L1_gnn_attn_forward"])
            K.acc1 = ctx.enter_context(nc.sbuf_tensor("acc1", [P, TILES, A1], F32, side="right"))
            with ExitStack() as second:
                sb = lambda name, shape, dt=F32: second.enter_context(nc.sbuf_tensor(name, shape, dt))
                K.against = sb("against", [P, TILES, H1])
                K.all_top = sb("all_top", [P, H1])
                second_edges(nc, K)
        K.Y = K.acc1[:, :, 0:D]
        K.YT = ctx.enter_context(nc.sbuf_tensor("YT", [P, 2, N_PAD], F32))
        K.pair = ctx.enter_context(nc.sbuf_tensor("pair", [P, 2], F32))
        K.chosen = ctx.enter_context(nc.sbuf_tensor("chosen", [1, 2], I32))
        route(nc, K, a["L1_ffn_Wr"], a["L1_ffn_br"])
        last_experts(nc, K, a["L1_ffn_W1"], a["L1_ffn_b1"], a["L1_ffn_W2"], a["L1_ffn_b2"],
                     a["L1_ffn_gamma"], a["L1_ffn_beta"], out)


_INS = ['x', 'src', 'dst', 'edge_attr_2', 'L0_gnn_W', 'L0_gnn_att_src', 'L0_gnn_att_dst', 'L0_gnn_bias',
        'L0_gnn_gamma', 'L0_gnn_beta', 'L0_ffn_Wg', 'L0_ffn_bg', 'L0_ffn_bias', 'L0_ffn_W1', 'L0_ffn_b1',
        'L0_ffn_W2', 'L0_ffn_b2', 'L1_gnn_W_forward', 'L1_gnn_W_reverse', 'L1_gnn_attn_forward', 'L1_ffn_Wr',
        'L1_ffn_br', 'L1_ffn_W1', 'L1_ffn_b1', 'L1_ffn_W2', 'L1_ffn_b2', 'L1_ffn_gamma', 'L1_ffn_beta']


def kernel(**inputs):
    import numpy as _np
    import concourse.bacc as _bacc
    from concourse import mybir as _mybir
    from concourse.bass_utils import run_bass_kernel_spmd as _run

    def padded(a, rows, **how):
        return _np.pad(a, [(0, rows - a.shape[0])] + [(0, 0)] * (a.ndim - 1), **how)

    laid = {k: _np.asarray(v) for k, v in inputs.items()}
    laid['x'] = padded(laid['x'], N_PAD)
    laid['src'] = padded(laid['src'], E_PAD, mode='edge').reshape(EDGE_ROWS, ROW_EDGES)
    laid['dst'] = padded(laid['dst'], E_PAD, constant_values=PAD_DST).reshape(EDGE_ROWS, ROW_EDGES)
    laid['edge_attr_2'] = padded(laid['edge_attr_2'], E_PAD, mode='edge').reshape(EDGE_ROWS, ROW_EDGES, 2)

    nc = _bacc.Bacc("TRN2", target_bir_lowering=False, num_devices=1)
    arrays, args = {}, {}
    for name in _INS:
        a = _np.ascontiguousarray(laid[name])
        arrays[f"in_{name}_dram"] = a
        args[name] = nc.dram_tensor(f"in_{name}_dram", a.shape, _mybir.dt.from_np(a.dtype), kind="ExternalInput").ap()
    out = nc.dram_tensor("out_0_dram", (N_PAD, D), _mybir.dt.float32, kind="ExternalOutput").ap()
    program(nc, args, out)
    r = _run(nc, [arrays], core_ids=[0])
    return r.results[0]["out_0_dram"][:N_NODES]
```
